# Optimizing a Trainium2 kernel written in Bass

```python
import numpy as np
import jax
import jax.numpy as jnp

def _softmax(x, axis=-1):
    return jax.nn.softmax(x, axis=axis)

def _gelu(x):
    return jax.nn.gelu(x, approximate=True)

def _silu(x):
    return jax.nn.silu(x)

def _sigmoid(x):
    return jax.nn.sigmoid(x)

def _layernorm(x, axis=-1, eps=1e-05):
    m = jnp.mean(x, axis=axis, keepdims=True)
    v = jnp.var(x, axis=axis, keepdims=True)
    return (x - m) / jnp.sqrt(v + eps)

def _scatter_add(tgt, idx, src, axis=0):
    return tgt.at[idx].add(src)

def _segment_sum(src, seg, n):
    return jax.ops.segment_sum(src, seg, n)
kernel_name = 'mk_gnn_resnorm_d2_gnn_r64_8e378f'

def setup_inputs(seed: int=0):
    np.random.seed(seed)
    _w = jnp.asarray

    def _rec_inputs():
        import jax
        import jax.numpy as jnp
        _gk = jax.random.key(seed)
        x = -6.985e-05 + 0.9998 * jax.random.normal(jax.random.fold_in(_gk, 1), (10000, 512), jnp.float32)
        _s = jax.random.randint(jax.random.fold_in(_gk, 2), (1250,), 0, 10000, jnp.int32)
        _d = jax.random.randint(jax.random.fold_in(_gk, 3), (1250,), 0, 10000, jnp.int32)
        _loop = jnp.arange(10000, dtype=jnp.int32)
        src = jnp.concatenate([_s, _d, _loop])
        dst = jnp.concatenate([_d, _s, _loop])
        _o = jnp.argsort(dst, stable=True)
        src = src[_o]
        dst = dst[_o]
        return (x, src, dst)
    x, src, dst = _rec_inputs()

    def _L0_gnn_setup():
        import jax, jax.numpy as jnp
        import numpy as np
        B = 32
        MAXN = 32
        HEADS = 8
        DH = 64
        M = 256
        D = 512
        EPS = 1e-05
        KEPS = 1e-06

        def _batchnorm(x, g, b):
            mu = jnp.mean(x, axis=0)
            var = jnp.mean((x - mu) ** 2, axis=0)
            return (x - mu) * jax.lax.rsqrt(var + EPS) * g + b

        def _forward(x, batch, edge_index, norm1_g, norm1_b, norm2_g, norm2_b, W_conv, b_conv, Wq, Wk, Wv, Wo, proj):
            N = x.shape[0]
            E = edge_index.shape[1]
            h = x
            xn = _batchnorm(x, norm1_g, norm1_b)
            msg = xn[edge_index[0]]
            agg = jax.ops.segment_sum(msg, edge_index[1], num_segments=N)
            deg = jax.ops.segment_sum(jnp.ones((E,), x.dtype), edge_index[1], num_segments=N)
            agg = agg / jnp.maximum(deg, 1.0)[:, None]
            conv_out = jax.nn.relu(agg @ W_conv + b_conv)
            counts = jax.ops.segment_sum(jnp.ones((N,), jnp.int32), batch, num_segments=B)
            offsets = jnp.concatenate([jnp.zeros((1,), jnp.int32), jnp.cumsum(counts)[:-1]])
            pos = jnp.arange(N, dtype=jnp.int32) - offsets[batch]
            h_dense = jnp.zeros((B, MAXN, D), x.dtype).at[batch, pos].set(h)
            mask = jnp.zeros((B, MAXN), bool).at[batch, pos].set(True)

            def heads(t, W):
                return (t @ W).reshape(B, MAXN, HEADS, DH).transpose(0, 2, 1, 3)
            q, k, v = (heads(h_dense, Wq), heads(h_dense, Wk), heads(h_dense, Wv))
            scale = DH ** (-0.25)

            def phi(t, is_query):
                t = t * scale
                u = jnp.einsum('bhnd,md->bhnm', t, proj)
                diag = 0.5 * jnp.sum(t * t, axis=-1, keepdims=True)
                if is_query:
                    m_ = jnp.max(u, axis=-1, keepdims=True)
                else:
                    m_ = jnp.max(u, axis=(-2, -1), keepdims=True)
                return jnp.exp(u - diag - jax.lax.stop_gradient(m_)) / np.sqrt(M) + KEPS
            qf = phi(q, True)
            kf = phi(k, False) * mask[:, None, :, None]
            vm = v * mask[:, None, :, None]
            kv = jnp.einsum('bhnm,bhnd->bhmd', kf, vm)
            z = 1.0 / (jnp.einsum('bhnm,bhm->bhn', qf, kf.sum(axis=2)) + KEPS)
            attn = jnp.einsum('bhnm,bhmd->bhnd', qf, kv) * z[..., None]
            attn = attn.transpose(0, 2, 1, 3).reshape(B, MAXN, D) @ Wo
            h_attn = attn[batch, pos]
            return _batchnorm(conv_out + h_attn + h, norm2_g, norm2_b)
        key = jax.random.key(seed)
        ks = jax.random.split(key, 10)
        sizes = 1024 + np.arange(B) * 131 % 1025
        N = int(sizes.sum())
        E = N * 8
        batch = jnp.asarray(np.repeat(np.arange(B), sizes), dtype=jnp.int32)
        edge_index = jax.random.randint(ks[0], (2, E), 0, N, dtype=jnp.int32)
        s = 1.0 / np.sqrt(D)
        return {'x': jax.random.normal(ks[1], (N, D), jnp.float32), 'batch': batch, 'edge_index': edge_index, 'norm1_g': jnp.ones((D,), jnp.float32), 'norm1_b': jnp.zeros((D,), jnp.float32), 'norm2_g': jnp.ones((D,), jnp.float32), 'norm2_b': jnp.zeros((D,), jnp.float32), 'W_conv': jax.random.normal(ks[2], (D, D), jnp.float32) * s, 'b_conv': jnp.zeros((D,), jnp.float32), 'Wq': jax.random.normal(ks[3], (D, D), jnp.float32) * s, 'Wk': jax.random.normal(ks[4], (D, D), jnp.float32) * s, 'Wv': jax.random.normal(ks[5], (D, D), jnp.float32) * s, 'Wo': jax.random.normal(ks[6], (D, D), jnp.float32) * s, 'proj': jax.random.normal(ks[7], (M, DH), jnp.float32)}
    _L0_gnn_all = _L0_gnn_setup()
    _L0_gnn_in = {k: v for k, v in _L0_gnn_all.items() if k in ('norm1_g', 'norm1_b', 'norm2_g', 'norm2_b', 'W_conv', 'b_conv', 'Wq', 'Wk', 'Wv', 'Wo', 'proj')}
    del _L0_gnn_all

    def _L1_gnn_setup():
        import jax, jax.numpy as jnp
        import numpy as np
        NHEAD = 8
        M_NODES = 20000
        D_MODEL = 512
        N_EDGES = 10000
        key = jax.random.key(seed)
        ks = jax.random.split(key, 8)
        sc = 1.0 / np.sqrt(D_MODEL)
        return {'s': jax.random.normal(ks[0], (M_NODES, D_MODEL), dtype=jnp.float32), 'edge_index': jax.random.randint(ks[1], (2, N_EDGES), 0, M_NODES, dtype=jnp.int64), 'Wq': jax.random.normal(ks[2], (D_MODEL, D_MODEL), dtype=jnp.float32) * sc, 'bq': jax.random.normal(ks[3], (D_MODEL,), dtype=jnp.float32) * sc, 'Wkv': jax.random.normal(ks[4], (2 * D_MODEL, D_MODEL), dtype=jnp.float32) * sc, 'bkv': jax.random.normal(ks[5], (2 * D_MODEL,), dtype=jnp.float32) * sc, 'Wo': jax.random.normal(ks[6], (D_MODEL, D_MODEL), dtype=jnp.float32) * sc, 'bo': jax.random.normal(ks[7], (D_MODEL,), dtype=jnp.float32) * sc}
    _L1_gnn_all = _L1_gnn_setup()
    _L1_gnn_in = {k: v for k, v in _L1_gnn_all.items() if k in ('Wq', 'bq', 'Wkv', 'bkv', 'Wo', 'bo')}
    del _L1_gnn_all
    return {'x': x, 'src': src, 'dst': dst, 'L0_gnn_norm1_g': _L0_gnn_in['norm1_g'], 'L0_gnn_norm1_b': _L0_gnn_in['norm1_b'], 'L0_gnn_norm2_g': _L0_gnn_in['norm2_g'], 'L0_gnn_norm2_b': _L0_gnn_in['norm2_b'], 'L0_gnn_W_conv': _L0_gnn_in['W_conv'], 'L0_gnn_b_conv': _L0_gnn_in['b_conv'], 'L0_gnn_Wq': _L0_gnn_in['Wq'], 'L0_gnn_Wk': _L0_gnn_in['Wk'], 'L0_gnn_Wv': _L0_gnn_in['Wv'], 'L0_gnn_Wo': _L0_gnn_in['Wo'], 'L0_gnn_proj': _L0_gnn_in['proj'], 'L1_gnn_Wq': _L1_gnn_in['Wq'], 'L1_gnn_bq': _L1_gnn_in['bq'], 'L1_gnn_Wkv': _L1_gnn_in['Wkv'], 'L1_gnn_bkv': _L1_gnn_in['bkv'], 'L1_gnn_Wo': _L1_gnn_in['Wo'], 'L1_gnn_bo': _L1_gnn_in['bo']}

def reference(x, src, dst, L0_gnn_norm1_g, L0_gnn_norm1_b, L0_gnn_norm2_g, L0_gnn_norm2_b, L0_gnn_W_conv, L0_gnn_b_conv, L0_gnn_Wq, L0_gnn_Wk, L0_gnn_Wv, L0_gnn_Wo, L0_gnn_proj, L1_gnn_Wq, L1_gnn_bq, L1_gnn_Wkv, L1_gnn_bkv, L1_gnn_Wo, L1_gnn_bo):
    import jax
    import jax.numpy as jnp

    def _L0_gnn_ref(x, batch, edge_index, norm1_g, norm1_b, norm2_g, norm2_b, W_conv, b_conv, Wq, Wk, Wv, Wo, proj):
        import jax, jax.numpy as jnp
        import numpy as np
        B = 32
        MAXN = 32
        HEADS = 8
        DH = 64
        M = 256
        D = 512
        EPS = 1e-05
        KEPS = 1e-06

        def _batchnorm(x, g, b):
            mu = jnp.mean(x, axis=0)
            var = jnp.mean((x - mu) ** 2, axis=0)
            return (x - mu) * jax.lax.rsqrt(var + EPS) * g + b

        def _forward(x, batch, edge_index, norm1_g, norm1_b, norm2_g, norm2_b, W_conv, b_conv, Wq, Wk, Wv, Wo, proj):
            N = x.shape[0]
            E = edge_index.shape[1]
            h = x
            xn = _batchnorm(x, norm1_g, norm1_b)
            msg = xn[edge_index[0]]
            agg = jax.ops.segment_sum(msg, edge_index[1], num_segments=N)
            deg = jax.ops.segment_sum(jnp.ones((E,), x.dtype), edge_index[1], num_segments=N)
            agg = agg / jnp.maximum(deg, 1.0)[:, None]
            conv_out = jax.nn.relu(agg @ W_conv + b_conv)
            counts = jax.ops.segment_sum(jnp.ones((N,), jnp.int32), batch, num_segments=B)
            offsets = jnp.concatenate([jnp.zeros((1,), jnp.int32), jnp.cumsum(counts)[:-1]])
            pos = jnp.arange(N, dtype=jnp.int32) - offsets[batch]
            h_dense = jnp.zeros((B, MAXN, D), x.dtype).at[batch, pos].set(h)
            mask = jnp.zeros((B, MAXN), bool).at[batch, pos].set(True)

            def heads(t, W):
                return (t @ W).reshape(B, MAXN, HEADS, DH).transpose(0, 2, 1, 3)
            q, k, v = (heads(h_dense, Wq), heads(h_dense, Wk), heads(h_dense, Wv))
            scale = DH ** (-0.25)

            def phi(t, is_query):
                t = t * scale
                u = jnp.einsum('bhnd,md->bhnm', t, proj)
                diag = 0.5 * jnp.sum(t * t, axis=-1, keepdims=True)
                if is_query:
                    m_ = jnp.max(u, axis=-1, keepdims=True)
                else:
                    m_ = jnp.max(u, axis=(-2, -1), keepdims=True)
                return jnp.exp(u - diag - jax.lax.stop_gradient(m_)) / np.sqrt(M) + KEPS
            qf = phi(q, True)
            kf = phi(k, False) * mask[:, None, :, None]
            vm = v * mask[:, None, :, None]
            kv = jnp.einsum('bhnm,bhnd->bhmd', kf, vm)
            z = 1.0 / (jnp.einsum('bhnm,bhm->bhn', qf, kf.sum(axis=2)) + KEPS)
            attn = jnp.einsum('bhnm,bhmd->bhnd', qf, kv) * z[..., None]
            attn = attn.transpose(0, 2, 1, 3).reshape(B, MAXN, D) @ Wo
            h_attn = attn[batch, pos]
            return _batchnorm(conv_out + h_attn + h, norm2_g, norm2_b)
        return _forward(x, batch, edge_index, norm1_g, norm1_b, norm2_g, norm2_b, W_conv, b_conv, Wq, Wk, Wv, Wo, proj)

    def _L1_gnn_ref(s, edge_index, Wq, bq, Wkv, bkv, Wo, bo):
        import jax, jax.numpy as jnp
        import numpy as np
        NHEAD = 8
        M_NODES = 20000
        D_MODEL = 512
        N_EDGES = 10000
        M, C = s.shape
        H = NHEAD
        Dh = C // H
        scale = 1.0 / np.sqrt(Dh).astype(np.float32)
        q = (s @ Wq.T + bq).reshape(M, H, Dh)
        kv = (s @ Wkv.T + bkv).reshape(M, H, 2 * Dh)
        k, v = (kv[..., :Dh], kv[..., Dh:])
        src, tgt = (edge_index[0], edge_index[1])
        a = jnp.einsum('ehc,ehc->eh', q[tgt], k[src]) * scale
        a_max = jax.ops.segment_max(a, tgt, num_segments=M)
        ex = jnp.exp(a - a_max[tgt])
        denom = jax.ops.segment_sum(ex, tgt, num_segments=M)
        attn = ex / denom[tgt]
        o_msg = attn[..., None] * v[src]
        o = jax.ops.segment_sum(o_msg, tgt, num_segments=M)
        o = o.reshape(M, C)
        return o @ Wo.T + bo
    edge_index = jnp.stack([src, dst])
    batch0 = jnp.zeros((10000,), jnp.int32)
    x = _layernorm(x + _L0_gnn_ref(x, batch0, edge_index, L0_gnn_norm1_g, L0_gnn_norm1_b, L0_gnn_norm2_g, L0_gnn_norm2_b, L0_gnn_W_conv, L0_gnn_b_conv, L0_gnn_Wq, L0_gnn_Wk, L0_gnn_Wv, L0_gnn_Wo, L0_gnn_proj), axis=-1)
    x = _layernorm(x + _L1_gnn_ref(x, edge_index, L1_gnn_Wq, L1_gnn_bq, L1_gnn_Wkv, L1_gnn_bkv, L1_gnn_Wo, L1_gnn_bo), axis=-1)
    return x

_drawn_inputs = setup_inputs


def setup_inputs(seed=0):
    import zlib

    import numpy as np

    out = dict(_drawn_inputs(seed))
    spreads = {'L0_gnn_norm1_g': (1.0, 0.2),
     'L0_gnn_norm1_b': (0.0, 0.368),
     'L0_gnn_norm2_g': (1.0, 0.2),
     'L0_gnn_norm2_b': (0.0, 0.1),
     'L0_gnn_b_conv': (0.0, 0.39)}
    factors = {'L0_gnn_Wq': 8.0,
     'L0_gnn_Wk': 8.0,
     'L0_gnn_Wv': 8.0,
     'L0_gnn_Wo': 8.0,
     'L0_gnn_proj': 8.0,
     'L1_gnn_bq': 8.0}
    for name, (base, spread) in spreads.items():
        noise = np.random.default_rng([zlib.crc32(name.encode()), seed]).standard_normal(out[name].shape)
        drawn = base * np.exp(spread * noise) if base else spread * noise
        out[name] = jnp.asarray(drawn.astype(out[name].dtype))
    for name, factor in factors.items():
        out[name] = (out[name] * factor).astype(out[name].dtype)
    return out
```

```python
from contextlib import ExitStack

import numpy as np
import concourse.bass as bass
from concourse import mybir

F32 = mybir.dt.float32
F32R = mybir.dt.float32r
I32 = mybir.dt.int32
ACT = mybir.ActivationFunctionType
ALU = mybir.AluOpType
AX = mybir.AxisListType
RMAX = bass.bass_isa.ReduceOp.max

P = 128
D = 512
KC = D // P
HEADS = 8
DH = D // HEADS
NF = 256
EPS = 1e-5
KEPS = 1e-6
BIG = 20000.0
FAR = 1e30


class Step:

    def __init__(self, ring, j, slot):
        self.ring, self.j, self.slot = ring, j, slot
        self.n = j * ring + slot

    def ahead(self, k):
        return Step(self.ring, self.j + (self.slot + k) // self.ring, (self.slot + k) % self.ring)

    def reaches(self, k):
        return not isinstance(self.n, int) or self.n >= k


def steps(engine, total, ring, body, peel_last=1):
    rings = (total - peel_last) // ring
    for n in range(ring):
        body(Step(ring, 0, n))
    with engine.Fori(1, rings) as j:
        for slot in range(ring):
            body(Step(ring, j, slot))
    for n in range(rings * ring, total):
        body(Step(ring, n // ring, n % ring))


def wait_alone(engine, semaphore, value, passed):
    engine.wait_ge(semaphore, value)
    engine.sem_inc(passed, 1)


def landed(step):
    return 16 * (step.j + 1)


def gnn_program(nc, x, src, dst, g1, b1, g2, b2, w_conv, b_conv, fq, fk, fv, fo, projT,
                wqT, bq, wkvT, bkv, woT, bo, out):
    N = x.shape[0]
    E = src.shape[0]
    TILES = -(-N // P)
    LAST_ROWS = N - (TILES - 1) * P
    EPC = P - 1
    CHUNKS = -(-E // EPC)
    PADDED = CHUNKS * EPC + 2
    NODES = TILES * P

    def rows(step):
        return LAST_ROWS if isinstance(step.n, int) and step.n == TILES - 1 else P

    aggregated = nc.dram_tensor("aggregated", [NODES, D], F32, kind="Internal").ap()
    attended = nc.dram_tensor("attended", [NODES, D], F32, kind="Internal").ap()
    y_dram = nc.dram_tensor("y_dram", [NODES, D], F32, kind="Internal").ap()
    x1_dram = nc.dram_tensor("x1_dram", [NODES, D], F32, kind="Internal").ap()
    q_dram = nc.dram_tensor("q_dram", [NODES, D], F32, kind="Internal").ap()
    kv_dram = nc.dram_tensor("kv_dram", [NODES, 2 * D], F32, kind="Internal").ap()
    dst_f = nc.dram_tensor("dst_f", [1, PADDED], F32, kind="Internal").ap()
    src_f = nc.dram_tensor("src_f", [1, PADDED], F32, kind="Internal").ap()

    def node_rows(t, step):
        return t[bass.ds(step.n * P, rows(step)), :]

    def windows(t, shift):
        return bass.AP(tensor=t.tensor, offset=shift, ap=[[EPC, CHUNKS], [1, P]])

    def window_on_all(t, step):
        return t[0:1, bass.ds(step.n * EPC, P)].to_broadcast([P, P])

    def row_on_all(t):
        return t.rearrange("(a n) -> a n", a=1).to_broadcast([P, t.shape[0]])

    top = ExitStack()
    with top:
        def tensors(ctx, stage):
            def sb(name, shape, dt=F32):
                return ctx.enter_context(nc.sbuf_tensor(f"{stage}_{name}", shape, dt))
            return sb

        stage_sems = []

        def sem(name):
            stage_sems.append(nc.alloc_semaphore(name))
            return stage_sems[-1]

        def sems(name, n):
            return [sem(f"{name}{i}") for i in range(n)]

        sb = tensors(top, "kept")
        bank = [top.enter_context(nc.psum_tensor(f"bank{i}", [P, D], F32)) for i in range(8)]

        identity = sb("identity", [P, P])
        ones = sb("ones", [P, P])
        split = {}
        for name in ("conv", "q", "k", "v", "o"):
            split[name] = (sb(f"w_{name}_hi", [P, KC, D], F32R), sb(f"w_{name}_lo", [P, KC, D], F32R))
        norm1_mul = sb("norm1_mul", [P, D])
        norm1_add = sb("norm1_add", [P, D])
        y_sum = sb("y_sum", [P, D])
        y_sq_sum = sb("y_sq_sum", [P, D])
        favor_out = sb("favor_out", [32, D])
        dst_col = sb("dst_col", [P, CHUNKS])
        edge_index = sb("edge_index", [P, CHUNKS, 4], I32)

        with ExitStack() as ctx:
            sb = tensors(ctx, "setup")
            stage = [sb(f"stage{i}", [P, KC, D]) for i in range(2)]
            zeros = sb("zeros", [P, D])
            e_int = [sb(f"e_int{i}", [100, E // 100], I32) for i in range(2)]
            e_flt = [sb(f"e_flt{i}", [100, E // 100]) for i in range(2)]
            pads = sb("pads", [1, P])
            win = [sb(f"win{i}", [CHUNKS, P]) for i in range(3)]
            cols = [sb(f"cols{i}", [P, CHUNKS]) for i in range(3)]
            not_last = sb("not_last", [P, CHUNKS])
            below = sb("below", [P, CHUNKS])
            index_f = sb("index_f", [P, CHUNKS, 4])
            weights = [("conv", w_conv), ("q", wqT), ("k", wkvT[:, 0:D]), ("v", wkvT[:, D:2 * D]), ("o", woT)]
            weight_loaded, zeroed = sems("weight_loaded", 2), sem("zeroed")
            edges_loaded, padded, windowed = sem("edges_loaded"), sem("padded"), sem("windowed")
            ident_ready, zero_ready, pad_ready = sem("ident_ready"), sem("zero_ready"), sem("pad_ready")
            edges_float, hi_ready, lo_ready = sem("edges_float"), sem("hi_ready"), sem("lo_ready")
            win_turned, cols_ready, table_step = sem("win_turned"), sem("cols_ready"), sem("table_step")

            with nc.Block() as block:
                @block.sync
                def _(sp):
                    for i, t in enumerate((dst, src)):
                        sp.dma_start(e_int[i][:, :], t.rearrange("(a n) -> a n", a=100)).then_inc(edges_loaded, 16)
                    for n, (name, w) in enumerate(weights):
                        if n >= 2:
                            sp.wait_ge(lo_ready, n - 1)
                        sp.dma_start(stage[n % 2][:, :, :], w.rearrange("(k p) n -> p k n", p=P)).then_inc(weight_loaded[n % 2], 16)
                        if n == 1:
                            sp.wait_ge(edges_float, 2)
                            sp.wait_ge(pad_ready, 3)
                            for i, t in enumerate((dst_f, src_f)):
                                sp.dma_start(t[0:1, 1:E + 1].rearrange("a (p n) -> (a p) n", p=100), e_flt[i][:, :]).then_inc(padded, 16)
                                sp.dma_start(t[0:1, 0:1], pads[0:1, 0:1]).then_inc(padded, 16)
                                sp.dma_start(t[0:1, E + 1:PADDED], pads[0:1, 1:PADDED - E]).then_inc(padded, 16)
                            sp.wait_ge(padded, 96)
                            for i, (t, shift) in enumerate(((dst_f, 0), (dst_f, 1), (src_f, 0))):
                                sp.dma_start(win[i][:, :], windows(t, shift)).then_inc(windowed, 16)
                    sp.wait_ge(zero_ready, 1)
                    for t in (aggregated, attended):
                        sp.dma_start(t.rearrange("(i p) n -> p i n", p=P), zeros[:, :].rearrange("p (i n) -> p i n", i=1).to_broadcast([P, TILES, D])).then_inc(zeroed, 16)
                    sp.wait_ge(zeroed, 32)

                @block.gpsimd
                def _(pool):
                    pool.memset(zeros[:, :], 0.0).then_inc(zero_ready, 1)
                    pool.memset(ones[:, :], 1.0).then_inc(pad_ready, 1)
                    pool.memset(pads[:, :], -2.0).then_inc(pad_ready, 1)
                    pool.wait_ge(pad_ready, 2)
                    pool.memset(pads[0:1, 0:1], -1.0).then_inc(pad_ready, 1)
                    pool.memset(identity[:, :], 0.0).then_inc(ident_ready, 1)
                    pool.wait_ge(ident_ready, 1)
                    pool.affine_select(out=identity[:, :], in_=identity[:, :], compare_op=ALU.not_equal, fill=1.0,
                                       base=0, pattern=[[-1, P]], channel_multiplier=1).then_inc(ident_ready, 1)

                @block.scalar
                def _(act):
                    for n, (name, _) in enumerate(weights):
                        act.wait_ge(weight_loaded[n % 2], 16 * (n // 2 + 1))
                        act.activation(split[name][0][:, :, :], stage[n % 2][:, :, :], ACT.Copy).then_inc(hi_ready, 1)

                @block.vector
                def _(dve):
                    dve.wait_ge(edges_loaded, 32)
                    for i in range(2):
                        dve.tensor_copy(e_flt[i][:, :], e_int[i][:, :]).then_inc(edges_float, 1)
                    for n, (name, _) in enumerate(weights):
                        hi, lo = split[name]
                        dve.wait_ge(hi_ready, n + 1)
                        dve.tensor_tensor(lo[:, :, :], stage[n % 2][:, :, :], hi[:, :, :].bitcast(F32), ALU.subtract).then_inc(lo_ready, 1)
                    dve.wait_ge(win_turned, 1)
                    for i in range(3):
                        dve.tensor_copy(cols[i][:, :], bank[i][:, 0:CHUNKS]).then_inc(cols_ready, 1)
                    dve.wait_ge(cols_ready, 3)
                    dcol, dnext, scol = cols
                    dve.tensor_copy(dst_col[:, :], dcol[:, :]).then_inc(table_step, 1)
                    dve.tensor_tensor(not_last[:, :], dcol[:, :], dnext[:, :], ALU.is_equal).then_inc(table_step, 1)
                    dve.tensor_scalar(below[:, :], dcol[:, :], 0.0, BIG, ALU.is_lt, ALU.mult).then_inc(table_step, 1)
                    dve.wait_ge(table_step, 3)
                    dve.tensor_tensor(index_f[:, :, 1], dcol[:, :], below[:, :], ALU.add).then_inc(table_step, 1)
                    dve.memset(index_f[:, :, 3], 0.0).then_inc(table_step, 1)
                    dve.wait_ge(table_step, 5)
                    dve.scalar_tensor_tensor(index_f[:, :, 2], not_last[:, :], BIG, index_f[:, :, 1], ALU.mult, ALU.add).then_inc(table_step, 1)
                    dve.tensor_scalar(below[:, :], scol[:, :], 0.0, BIG, ALU.is_lt, ALU.mult).then_inc(table_step, 1)
                    dve.wait_ge(table_step, 7)
                    dve.tensor_tensor(index_f[:, :, 0], scol[:, :], below[:, :], ALU.add).then_inc(table_step, 1)
                    dve.wait_ge(table_step, 8)
                    dve.memset(index_f[0:1, :, 0:3], BIG).then_inc(table_step, 1)
                    dve.wait_ge(table_step, 9)
                    dve.tensor_copy(edge_index[:, :, :], index_f[:, :, :]).then_inc(table_step, 1)

                @block.tensor
                def _(pe):
                    pe.wait_ge(ident_ready, 2)
                    pe.wait_ge(windowed, 48)
                    for i in range(3):
                        m = pe.transpose(bank[i][:, 0:CHUNKS], win[i][:, :], identity[0:CHUNKS, 0:CHUNKS])
                    m.then_inc(win_turned, 1)

        with ExitStack() as ctx:
            sb = tensors(ctx, "stats")
            RING = 3
            xs = [sb(f"xs{i}", [P, D]) for i in range(RING)]
            xsq = [sb(f"xsq{i}", [P, D]) for i in range(RING)]
            x_sum = sb("x_sum", [P, D])
            mean, var, tmp = sb("mean", [P, D]), sb("var", [P, D]), sb("tmp", [P, D])
            gain, shift = sb("gain", [P, D]), sb("shift", [P, D])
            loaded, consts = sems("s_x_loaded", RING), sem("s_consts")
            summed, squared, sq_summed = sem("s_summed"), sem("s_squared"), sem("s_sq_summed")
            sum_cleared, totals, affine = sem("s_sum_cleared"), sem("s_totals"), sem("s_affine")
            root = sem("s_root")
            with nc.Block() as block:
                @block.sync
                def _(sp):
                    sp.dma_start(gain[:, :], row_on_all(g1)).then_inc(consts, 16)
                    sp.dma_start(shift[:, :], row_on_all(b1)).then_inc(consts, 16)

                    def load(s):
                        if s.reaches(RING):
                            sp.wait_ge(summed, s.n - RING + 1)
                            sp.wait_ge(squared, s.n - RING + 1)
                        sp.dma_start(xs[s.slot][0:rows(s), :], node_rows(x, s)).then_inc(loaded[s.slot], 16)
                    steps(sp, TILES, RING, load)

                @block.vector
                def _(dve):
                    dve.memset(x_sum[:, :], 0.0).then_inc(sum_cleared, 1)
                    dve.wait_ge(sum_cleared, 1)

                    def add(s):
                        r = rows(s)
                        dve.wait_ge(loaded[s.slot], landed(s))
                        if s.reaches(1):
                            dve.wait_ge(summed, s.n)
                        dve.tensor_tensor(x_sum[0:r, :], x_sum[0:r, :], xs[s.slot][0:r, :], ALU.add).then_inc(summed, 1)
                    steps(dve, TILES, RING, add)
                    dve.wait_ge(totals, 1)
                    dve.tensor_scalar(mean[:, :], bank[0][:, :], 1.0 / N, None, ALU.mult).then_inc(affine, 1)
                    dve.tensor_scalar(var[:, :], bank[1][:, :], 1.0 / N, EPS, ALU.mult, ALU.add).then_inc(affine, 1)
                    dve.wait_ge(affine, 2)
                    dve.tensor_tensor(tmp[:, :], mean[:, :], mean[:, :], ALU.mult).then_inc(affine, 1)
                    dve.wait_ge(affine, 3)
                    dve.tensor_tensor(var[:, :], var[:, :], tmp[:, :], ALU.subtract).then_inc(affine, 1)
                    dve.wait_ge(root, 1)
                    dve.reciprocal(tmp[:, :], var[:, :]).then_inc(affine, 1)
                    dve.wait_ge(affine, 5)
                    dve.wait_ge(consts, 32)
                    dve.tensor_tensor(norm1_mul[:, :], tmp[:, :], gain[:, :], ALU.mult).then_inc(affine, 1)
                    dve.wait_ge(affine, 6)
                    dve.tensor_tensor(tmp[:, :], mean[:, :], norm1_mul[:, :], ALU.mult).then_inc(affine, 1)
                    dve.wait_ge(affine, 7)
                    dve.tensor_tensor(norm1_add[:, :], shift[:, :], tmp[:, :], ALU.subtract).then_inc(affine, 1)

                @block.scalar
                def _(act):
                    def square(s):
                        r = rows(s)
                        act.wait_ge(loaded[s.slot], landed(s))
                        if s.reaches(RING):
                            act.wait_ge(sq_summed, s.n - RING + 1)
                        act.activation(xsq[s.slot][0:r, :], xs[s.slot][0:r, :], ACT.Square).then_inc(squared, 1)
                    steps(act, TILES, RING, square)
                    act.wait_ge(affine, 4)
                    act.activation(var[:, :], var[:, :], ACT.Sqrt).then_inc(root, 1)

                @block.tensor
                def _(pe):
                    def total_squares(s):
                        r = rows(s)
                        pe.wait_ge(squared, s.n + 1)
                        first = isinstance(s.n, int) and s.n == 0
                        last = isinstance(s.n, int) and s.n == TILES - 1
                        pe.matmul(bank[1][:, :], ones[0:r, :], xsq[s.slot][0:r, :], start=first, stop=last).then_inc(sq_summed, 1)
                    steps(pe, TILES, RING, total_squares)
                    pe.wait_ge(summed, TILES)
                    pe.matmul(bank[0][:, :], ones[:, :], x_sum[:, :], start=True, stop=True).then_inc(totals, 1)

        with ExitStack() as ctx:
            sb = tensors(ctx, "favor")
            R = 32
            h = sb("h", [R, D])
            hT = sb("hT", [P, KC, R])
            fw = {n: sb(f"fw_{n}", [P, KC, D]) for n in "qkvo"}
            pT = sb("pT", [P, NF])
            rowform = {n: sb(f"row_{n}", [R, D]) for n in "qk"}
            colform = {n: sb(f"col_{n}", [P, KC, R]) for n in "qk"}
            v_one = sb("v_one", [R, HEADS, DH + 1])
            sq = {n: sb(f"sq_{n}", [R, D]) for n in "qk"}
            diag = {n: sb(f"diag_{n}", [R, HEADS]) for n in "qk"}
            peak = {n: sb(f"peak_{n}", [R, HEADS]) for n in "qk"}
            peak_all = sb("peak_all", [R, HEADS])
            bias = {n: sb(f"bias_{n}", [R, HEADS]) for n in "qk"}
            feat = {n: sb(f"feat_{n}", [R, HEADS, NF]) for n in "qk"}
            featT = sb("featT", [P, 2 * HEADS, R])
            kv = sb("kv", [P, 2 * HEADS, DH + 1])
            den = sb("den", [R, HEADS])
            inv = sb("inv", [R, HEADS])
            av = sb("av", [R, D])
            avT = sb("avT", [P, KC, R])
            avD = sb("avD", [P, KC, R])
            f_loaded, f_turned, f_hT, f_proj, f_colp = (sem(n) for n in ("f_loaded", "f_turned", "f_hT", "f_proj", "f_colp"))
            f_vec, f_u, f_peak, f_exp, f_featT = (sem(n) for n in ("f_vec", "f_u", "f_peak", "f_exp", "f_featT"))
            f_kv, f_kvs, f_attn, f_avT, f_out = (sem(n) for n in ("f_kv", "f_kvs", "f_attn", "f_avT", "f_out"))
            f_copied, f_one = sem("f_copied"), sem("f_one")
            TEMPER = float(DH) ** -0.25

            def features(b, hd):
                return bank[4 * b + 2 * (hd % 2) + hd // 4][0:R, (hd // 2 % 2) * NF:(hd // 2 % 2 + 1) * NF]

            with nc.Block() as block:
                @block.sync
                def _(sp):
                    sp.dma_start(h[:, :], x[0:R, :]).then_inc(f_loaded, 16)
                    for n, w in zip("qkvo", (fq, fk, fv, fo)):
                        sp.dma_start(fw[n][:, :, :], w.rearrange("(k p) n -> p k n", p=P)).then_inc(f_loaded, 16)
                    for half in range(2):
                        sp.dma_start(pT[half * DH:(half + 1) * DH, :], projT).then_inc(f_loaded, 16)

                @block.tensor
                def _(pe):
                    pe.wait_ge(f_loaded, 7 * 16)
                    for k in range(KC):
                        m = pe.transpose(bank[0][:, k * R:(k + 1) * R], h[:, k * P:(k + 1) * P], identity[0:R, 0:R])
                    m.then_inc(f_turned, 1)
                    pe.wait_ge(f_hT, 1)
                    for b, n in enumerate("qkv"):
                        for k in range(KC):
                            m = pe.matmul(bank[1 + b][0:R, :], hT[:, k, :], fw[n][:, k, :], start=k == 0, stop=k == KC - 1)
                    m.then_inc(f_proj, 1)
                    for b, n in enumerate("qk"):
                        for c in range(KC):
                            for k in range(KC):
                                m = pe.matmul(bank[4 + b][:, c * R:(c + 1) * R], fw[n][:, k, c * P:(c + 1) * P], hT[:, k, :], start=k == 0, stop=k == KC - 1)
                    m.then_inc(f_colp, 1)
                    pe.wait_ge(f_copied, 5)
                    for b, n in enumerate("qk"):
                        for hd in range(HEADS):
                            o = (hd % 2) * DH
                            m = pe.matmul(features(b, hd), 
                                          colform[n][o:o + DH, hd // 2, :], pT[o:o + DH, :], start=True, stop=True)
                        m.then_inc(f_u, 1)
                    pe.wait_ge(f_exp, 6)
                    for hd in range(HEADS):
                        for half in range(2):
                            i = 2 * hd + half
                            m = pe.transpose(bank[0][:, i * R:(i + 1) * R], feat["q"][:, hd, half * P:(half + 1) * P], identity[0:R, 0:R])
                    m.then_inc(f_featT, 1)
                    for hd in range(HEADS):
                        for half in range(2):
                            i = 2 * hd + half
                            m = pe.matmul(bank[1 + i // 4][:, (i % 4) * (DH + 1):(i % 4 + 1) * (DH + 1)],
                                          feat["k"][:, hd, half * P:(half + 1) * P], v_one[:, hd, :], start=True, stop=True)
                    m.then_inc(f_kv, 1)
                    pe.wait_ge(f_kvs, 5)
                    for hd in range(HEADS):
                        for half in range(2):
                            i = 2 * hd + half
                            m = pe.matmul(bank[5 + hd // 4][0:R, (hd % 4) * (DH + 1):(hd % 4 + 1) * (DH + 1)],
                                          featT[:, i, :], kv[:, i, :], start=half == 0, stop=half == 1)
                    m.then_inc(f_attn, 1)
                    pe.wait_ge(f_vec, 8)
                    for k in range(KC):
                        m = pe.transpose(bank[7][:, k * R:(k + 1) * R], av[:, k * P:(k + 1) * P], identity[0:R, 0:R])
                    m.then_inc(f_avT, 1)
                    pe.wait_ge(f_vec, 13)
                    for k in range(KC):
                        m = pe.matmul(bank[0][0:R, :], avD[:, k, :], fw["o"][:, k, :], start=k == 0, stop=k == KC - 1)
                    m.then_inc(f_out, 1)

                @block.scalar
                def _(act):
                    for i, n in enumerate("qk"):
                        act.wait_ge(f_peak, i + 1)
                        for hd in range(HEADS):
                            m = act.activation(feat[n][:, hd, :], features(i, hd), ACT.Exp, bias=bias[n][:, hd:hd + 1])
                        m.then_inc(f_exp, 1)

                @block.gpsimd
                def _(pool):
                    pool.memset(v_one[:, :, DH:DH + 1], 1.0).then_inc(f_one, 1)
                    pool.wait_ge(f_vec, 5)
                    pool.partition_all_reduce(peak_all[:, :], peak["k"][:, :], R, RMAX).then_inc(f_one, 1)

                @block.vector
                def _(dve):
                    dve.wait_ge(f_turned, 1)
                    dve.tensor_copy(hT[:, :, :], bank[0][:, 0:KC * R].rearrange("p (k r) -> p k r", k=KC)).then_inc(f_hT, 1)
                    dve.wait_ge(f_proj, 1)
                    for b, n in enumerate("qk"):
                        dve.tensor_scalar(rowform[n][:, :], bank[1 + b][0:R, :], TEMPER, None, ALU.mult).then_inc(f_copied, 1)
                    dve.tensor_copy(v_one[:, :, 0:DH], bank[3][0:R, :].rearrange("p (h d) -> p h d", h=HEADS)).then_inc(f_copied, 1)
                    dve.wait_ge(f_colp, 1)
                    for b, n in enumerate("qk"):
                        dve.tensor_scalar(colform[n][:, :, :], bank[4 + b][:, 0:KC * R].rearrange("p (k r) -> p k r", k=KC), TEMPER, None, ALU.mult).then_inc(f_copied, 1)
                    dve.wait_ge(f_copied, 2)
                    for n in "qk":
                        dve.tensor_tensor(sq[n][:, :], rowform[n][:, :], rowform[n][:, :], ALU.mult).then_inc(f_vec, 1)
                    dve.wait_ge(f_vec, 2)
                    for n in "qk":
                        dve.tensor_reduce(diag[n][:, :], sq[n][:, :].rearrange("p (h d) -> p h d", h=HEADS), AX.X, ALU.add).then_inc(f_vec, 1)
                    dve.wait_ge(f_u, 2)
                    for i, n in ((1, "k"), (0, "q")):
                        for b in range(4):
                            first = 4 * (b % 2) + b // 2
                            m = dve.tensor_reduce(peak[n][:, first:first + 3:2], bank[4 * i + b][0:R, :].rearrange("p (h m) -> p h m", h=2), AX.X, ALU.max)
                        m.then_inc(f_vec, 1)
                    dve.wait_ge(f_vec, 6)
                    dve.scalar_tensor_tensor(bias["q"][:, :], diag["q"][:, :], -0.5, peak["q"][:, :], ALU.mult, ALU.subtract).then_inc(f_peak, 1)
                    dve.wait_ge(f_one, 2)
                    dve.scalar_tensor_tensor(bias["k"][:, :], diag["k"][:, :], -0.5, peak_all[:, :], ALU.mult, ALU.subtract).then_inc(f_peak, 1)
                    dve.wait_ge(f_exp, 2)
                    for n in "qk":
                        f = feat[n][:, :, :]
                        for half in range(2):
                            fh = feat[n][:, half * 4:half * 4 + 4, :]
                            dve.tensor_scalar(fh, fh, float(1.0 / np.sqrt(NF)), KEPS, ALU.mult, ALU.add).then_inc(f_exp, 1)
                    dve.wait_ge(f_featT, 1)
                    dve.tensor_copy(featT[:, :, :], bank[0][:, :].rearrange("p (i r) -> p i r", r=R)).then_inc(f_kvs, 1)
                    dve.wait_ge(f_kv, 1)
                    for b in range(4):
                        dve.tensor_copy(kv[:, 4 * b:4 * b + 4, :], bank[1 + b][:, 0:4 * (DH + 1)].rearrange("p (i d) -> p i d", i=4)).then_inc(f_kvs, 1)
                    dve.wait_ge(f_attn, 1)
                    for b in range(2):
                        m = dve.tensor_scalar(den[:, 4 * b:4 * b + 4], bank[5 + b][0:R, 0:4 * (DH + 1)].rearrange("p (i d) -> p i d", i=4)[:, :, DH], KEPS, None, ALU.add)
                    m.then_inc(f_vec, 1)
                    dve.wait_ge(f_vec, 7)
                    dve.reciprocal(inv[:, :], den[:, :]).then_inc(f_one, 1)
                    dve.wait_ge(f_one, 3)
                    for b in range(2):
                        m = dve.tensor_tensor(av[:, b * 4 * DH:(b + 1) * 4 * DH].rearrange("p (i d) -> p i d", i=4),
                                              bank[5 + b][0:R, 0:4 * (DH + 1)].rearrange("p (i d) -> p i d", i=4)[:, :, 0:DH],
                                              inv[:, 4 * b:4 * b + 4].rearrange("p (i d) -> p i d", d=1).to_broadcast([R, 4, DH]), ALU.mult)
                    m.then_inc(f_vec, 1)
                    dve.wait_ge(f_avT, 1)
                    dve.tensor_copy(avT[:, :, :], bank[7][:, 0:KC * R].rearrange("p (k r) -> p k r", k=KC)).then_inc(f_vec, 1)
                    dve.wait_ge(f_vec, 9)
                    for k in range(KC):
                        dve.tensor_scalar(avD[:, k, :], avT[:, k, :], avT[:, k, R - 1:R], None, ALU.subtract).then_inc(f_vec, 1)
                    dve.wait_ge(f_out, 1)
                    dve.tensor_copy(favor_out[:, :], bank[0][0:R, :]).then_inc(f_vec, 1)

        nc.clear_and_free_semaphores(stage_sems)
        nc.all_engine_barrier()
        stage_sems.clear()

        passed = sem("passed")

        with ExitStack() as ctx:
            sb = tensors(ctx, "gather")
            RING = 3
            window = [sb(f"a_window{i}", [P, P]) for i in range(RING)]
            same = [sb(f"a_same{i}", [P, P]) for i in range(RING)]
            idx = [sb(f"a_idx{i}", [P, 4], I32) for i in range(RING)]
            xg = [sb(f"xg{i}", [P, D]) for i in range(RING)]
            count = [sb(f"count{i}", [P, 1]) for i in range(RING)]
            inv_count = [sb(f"inv_count{i}", [P, 1]) for i in range(RING)]
            mean_mul = [sb(f"mean_mul{i}", [P, D]) for i in range(RING)]
            mean_row = [sb(f"mean_row{i}", [P, D]) for i in range(RING)]
            window_loaded, gathered, scattered = sems("a_window_loaded", RING), sems("a_gathered", RING), sems("a_scattered", RING)
            cleared, indexed, same_ready = sem("a_cleared"), sem("a_indexed"), sem("a_same_ready")
            carried, summed = sem("a_carried"), sem("a_summed")
            inverted, scaled, mean_ready = sem("a_inverted"), sem("a_scaled"), sem("a_mean_ready")
            sums = [bank[i] for i in range(RING)]
            counts = [bank[RING + i][:, 0:1] for i in range(RING)]
            with nc.Block() as block:
                @block.sync
                def _(sp):
                    def load(s):
                        if s.reaches(RING):
                            sp.wait_ge(same_ready, s.n - RING + 1)
                        sp.dma_start(window[s.slot][:, :], window_on_all(dst_f, s)).then_inc(window_loaded[s.slot], 16)
                    steps(sp, CHUNKS, RING, load)

                @block.gpsimd
                def _(pool):
                    limit = pool.to_reg(N - 1)
                    def gather(s):
                        if s.reaches(RING):
                            pool.wait_ge(scattered[s.slot], landed(s) - 16)
                        pool.tensor_copy(idx[s.slot][:, :], edge_index[:, bass.ds(s.n, 1), :].rearrange("p a b -> p (a b)")).then_inc(indexed, 1)
                        if s.reaches(RING):
                            pool.wait_ge(summed, s.n - RING + 1)
                        wait_alone(pool, indexed, s.n + 1, passed)
                        pool.indirect_dma_start(out=xg[s.slot][:, :], out_offset=None, in_=x,
                                                in_offset=bass.IndirectOffsetOnAxis(ap=idx[s.slot][:, 0:1], axis=0),
                                                bounds_check=limit, oob_is_err=False).then_inc(gathered[s.slot], 16)

                    def scatter(s):
                        wait_alone(pool, mean_ready, s.n + 1, passed)
                        pool.indirect_dma_start(out=aggregated, out_offset=bass.IndirectOffsetOnAxis(ap=idx[s.slot][:, 2:3], axis=0),
                                                in_=mean_row[s.slot][:, :], in_offset=None,
                                                bounds_check=limit, oob_is_err=False).then_inc(scattered[s.slot], 16)

                    for i in range(RING):
                        pool.memset(xg[i][:, :], 0.0).then_inc(cleared, 1)
                        pool.memset(count[i][:, :], 1.0).then_inc(cleared, 1)
                    pool.wait_ge(cleared, 2 * RING)
                    pool.memset(count[0][0:1, :], 0.0).then_inc(cleared, 1)
                    for n in range(RING - 1):
                        gather(Step(RING, 0, n))

                    def turn(s):
                        if isinstance(s.n, int):
                            if s.n + RING - 1 < CHUNKS:
                                gather(s.ahead(RING - 1))
                        else:
                            gather(s.ahead(RING - 1))
                        scatter(s)
                    steps(pool, CHUNKS, RING, turn, peel_last=RING)
                    for s in (Step(RING, n // RING, n % RING) for n in range(CHUNKS - RING, CHUNKS)):
                        pool.wait_ge(scattered[s.slot], landed(s))

                @block.vector
                def _(dve):
                    def compare(s):
                        u = s.slot
                        dve.wait_ge(window_loaded[u], landed(s))
                        if s.reaches(RING):
                            dve.wait_ge(summed, s.n - RING + 1)
                        own = dst_col[:, bass.ds(s.n, 1)]
                        dve.tensor_scalar(same[u][:, 1:P], window[u][:, 1:P], own, None, ALU.is_equal)
                        dve.tensor_scalar(same[u][:, 0:1], window[u][:, P - 1:P], own, None, ALU.is_equal).then_inc(same_ready, 1)

                    def normalize(s):
                        u = s.slot
                        if isinstance(s.n, int) and s.n == CHUNKS - 1:
                            dve.wait_ge(summed, s.n + 1)
                        else:
                            dve.wait_ge(carried, s.n + 1)
                        dve.reciprocal(inv_count[u][:, :], counts[u]).then_inc(inverted, 1)
                        dve.wait_ge(inverted, s.n + 1)
                        dve.scalar_tensor_tensor(mean_mul[u][:, :], sums[u][:, :], inv_count[u][:, 0:1], norm1_mul[:, :], ALU.mult, ALU.mult).then_inc(scaled, 1)
                        dve.wait_ge(scaled, s.n + 1)
                        if s.reaches(RING):
                            dve.wait_ge(scattered[u], landed(s) - 16)
                        dve.tensor_tensor(mean_row[u][:, :], mean_mul[u][:, :], norm1_add[:, :], ALU.add).then_inc(mean_ready, 1)

                    compare(Step(RING, 0, 0))

                    def turn(s):
                        if not isinstance(s.n, int) or s.n + 1 < CHUNKS:
                            compare(s.ahead(1))
                        normalize(s)
                    steps(dve, CHUNKS, RING, turn)

                @block.tensor
                def _(pe):
                    def total(s):
                        u = s.slot
                        pe.wait_ge(same_ready, s.n + 1)
                        pe.wait_ge(gathered[u], landed(s))
                        if s.reaches(1):
                            pe.wait_ge(carried, s.n)
                        else:
                            pe.wait_ge(cleared, 2 * RING + 1)
                        if s.reaches(RING):
                            pe.wait_ge(scaled, s.n - RING + 1)
                        pe.matmul(counts[u], same[u][:, :], count[u][:, :], start=True, stop=True)
                        pe.matmul(sums[u][:, :], same[u][:, :], xg[u][:, :], start=True, stop=True).then_inc(summed, 1)
                    steps(pe, CHUNKS, RING, total)

                @block.scalar
                def _(act):
                    act.wait_ge(cleared, 2 * RING + 1)

                    def carry(s):
                        to = s.ahead(1)
                        act.wait_ge(summed, s.n + 1)
                        act.activation(count[to.slot][0:1, :], counts[s.slot][0:1, :], ACT.Copy)
                        act.wait_ge(gathered[to.slot], landed(to))
                        act.activation(xg[to.slot][0:1, :], sums[s.slot][0:1, :], ACT.Copy).then_inc(carried, 1)
                    steps(act, CHUNKS - 1, RING, carry)

        def turn_tile(pe, psum, tile, r):
            for k in range(KC):
                m = pe.transpose(psum[:, k * P:k * P + r], tile[0:r, k * P:(k + 1) * P], identity[0:r, 0:r])
            return m

        def product(pe, psum, hi, lo, name, r):
            wh, wl = split[name]
            passes = [(hi, wh), (hi, wl), (lo, wh)]
            for i, (a, w) in enumerate(passes):
                for k in range(KC):
                    m = pe.matmul(psum[0:r, :], a[:, k * P:k * P + r], w[:, k, :],
                                  start=i == 0 and k == 0, stop=i == 2 and k == KC - 1)
            return m

        def blocks_of(t, r):
            return t[:, :].rearrange("p (k n) -> p k n", k=KC)[:, :, 0:r]

        with ExitStack() as ctx:
            sb = tensors(ctx, "conv")
            RING = 2
            ag = [sb(f"ag{i}", [P, D]) for i in range(RING)]
            xb = [sb(f"xb{i}", [P, D]) for i in range(RING)]
            hi = [sb(f"b_hi{i}", [P, D], F32R) for i in range(RING)]
            lo = [sb(f"b_lo{i}", [P, D], F32R) for i in range(RING)]
            pre = [sb(f"pre{i}", [P, D]) for i in range(RING)]
            y = [sb(f"y{i}", [P, D]) for i in range(RING)]
            ysq = [sb(f"ysq{i}", [P, D]) for i in range(RING)]
            bias_c = sb("bias_c", [P, D])
            ag_loaded, x_loaded, y_stored, consts = sems("b_ag_loaded", RING), sems("b_x_loaded", RING), sems("b_y_stored", RING), sem("b_consts")
            turned, hi_ready, lo_ready, made = sem("b_turned"), sem("b_hi_ready"), sem("b_lo_ready"), sem("b_made")
            biased, y_ready, squared, summed, sq_summed = sem("b_biased"), sem("b_y_ready"), sem("b_squared"), sem("b_summed"), sem("b_sq_summed")
            cleared, sq_cleared, favored = sem("b_cleared"), sem("b_sq_cleared"), sem("b_favored")
            tpose, acc = [bank[0], bank[1]], [bank[2], bank[3]]
            with nc.Block() as block:
                @block.sync
                def _(sp):
                    sp.dma_start(bias_c[:, :], row_on_all(b_conv)).then_inc(consts, 16)

                    def load(s):
                        u, r = s.slot, rows(s)
                        if s.reaches(RING):
                            sp.wait_ge(turned, s.n - RING + 1)
                        sp.dma_start(ag[u][0:r, :], node_rows(aggregated, s)).then_inc(ag_loaded[u], 16)
                        if s.reaches(RING):
                            sp.wait_ge(y_ready, s.n - RING + 1)
                        sp.dma_start(xb[u][0:r, :], node_rows(x, s)).then_inc(x_loaded[u], 16)
                    steps(sp, TILES, RING, load)

                @block.tensor
                def _(pe):
                    def turn(s):
                        pe.wait_ge(ag_loaded[s.slot], landed(s))
                        if s.reaches(RING):
                            pe.wait_ge(lo_ready, s.n - RING + 1)
                        turn_tile(pe, tpose[s.slot], ag[s.slot], rows(s)).then_inc(turned, 1)

                    def multiply(s):
                        pe.wait_ge(lo_ready, s.n + 1)
                        if s.reaches(RING):
                            pe.wait_ge(biased, s.n - RING + 1)
                        product(pe, acc[s.slot], hi[s.slot], lo[s.slot], "conv", rows(s)).then_inc(made, 1)

                    turn(Step(RING, 0, 0))

                    def both(s):
                        if not isinstance(s.n, int) or s.n + 1 < TILES:
                            turn(s.ahead(1))
                        multiply(s)
                    steps(pe, TILES, RING, both, peel_last=2)

                @block.scalar
                def _(act):
                    def copy_hi(s):
                        u, r = s.slot, rows(s)
                        act.wait_ge(turned, s.n + 1)
                        if s.reaches(RING):
                            act.wait_ge(made, s.n - RING + 1)
                        act.activation(blocks_of(hi[u], r), blocks_of(tpose[u], r), ACT.Copy).then_inc(hi_ready, 1)

                    def finish(s):
                        u, r = s.slot, rows(s)
                        act.wait_ge(y_ready, s.n + 1)
                        act.dma_start(node_rows(y_dram, s), y[u][0:r, :]).then_inc(y_stored[u], 16)
                        if s.reaches(RING):
                            act.wait_ge(sq_summed, s.n - RING + 1)
                        act.activation(ysq[u][0:r, :], y[u][0:r, :], ACT.Square).then_inc(squared, 1)

                    copy_hi(Step(RING, 0, 0))

                    def both(s):
                        if not isinstance(s.n, int) or s.n + 1 < TILES:
                            copy_hi(s.ahead(1))
                        finish(s)
                    steps(act, TILES, RING, both, peel_last=2)
                    for s in (Step(RING, n // RING, n % RING) for n in range(TILES - RING, TILES)):
                        act.wait_ge(y_stored[s.slot], landed(s))

                @block.vector
                def _(dve):
                    dve.memset(y_sum[:, :], 0.0).then_inc(cleared, 1)
                    dve.wait_ge(cleared, 1)
                    dve.wait_ge(consts, 16)

                    def take_lo(s):
                        u, r = s.slot, rows(s)
                        dve.wait_ge(hi_ready, s.n + 1)
                        dve.tensor_tensor(blocks_of(lo[u], r), blocks_of(tpose[u], r), blocks_of(hi[u], r).bitcast(F32), ALU.subtract).then_inc(lo_ready, 1)

                    def finish(s):
                        u, r = s.slot, rows(s)
                        dve.wait_ge(made, s.n + 1)
                        dve.tensor_tensor(pre[u][0:r, :], acc[u][0:r, :], bias_c[0:r, :], ALU.add).then_inc(biased, 1)
                        dve.wait_ge(biased, s.n + 1)
                        dve.wait_ge(x_loaded[u], landed(s))
                        if s.reaches(RING):
                            dve.wait_ge(y_stored[u], landed(s) - 16)
                            dve.wait_ge(squared, s.n - RING + 1)
                        if isinstance(s.n, int) and s.n == 0:
                            dve.scalar_tensor_tensor(y[u][0:r, :], pre[u][0:r, :], 0.0, xb[u][0:r, :], ALU.max, ALU.add).then_inc(favored, 1)
                            dve.wait_ge(favored, 1)
                            dve.tensor_tensor(y[u][0:32, :], y[u][0:32, :], favor_out[:, :], ALU.add).then_inc(y_ready, 1)
                        else:
                            dve.scalar_tensor_tensor(y[u][0:r, :], pre[u][0:r, :], 0.0, xb[u][0:r, :], ALU.max, ALU.add).then_inc(y_ready, 1)
                        dve.wait_ge(y_ready, s.n + 1)
                        dve.tensor_tensor(y_sum[0:r, :], y_sum[0:r, :], y[u][0:r, :], ALU.add).then_inc(summed, 1)

                    take_lo(Step(RING, 0, 0))

                    def both(s):
                        if not isinstance(s.n, int) or s.n + 1 < TILES:
                            take_lo(s.ahead(1))
                        finish(s)
                    steps(dve, TILES, RING, both, peel_last=2)

                @block.gpsimd
                def _(pool):
                    pool.memset(y_sq_sum[:, :], 0.0).then_inc(sq_cleared, 1)
                    pool.wait_ge(sq_cleared, 1)

                    def add(s):
                        u, r = s.slot, rows(s)
                        pool.wait_ge(squared, s.n + 1)
                        if s.reaches(1):
                            pool.wait_ge(sq_summed, s.n)
                        pool.tensor_tensor(y_sq_sum[0:r, :], y_sq_sum[0:r, :], ysq[u][0:r, :], ALU.add).then_inc(sq_summed, 1)
                    steps(pool, TILES, RING, add)

        with ExitStack() as ctx:
            sb = tensors(ctx, "qkv")
            RING = 2
            yb = [sb(f"yb{i}", [P, D]) for i in range(RING)]
            xc = [sb(f"xc{i}", [P, D]) for i in range(RING)]
            ym = [sb(f"ym{i}", [P, D]) for i in range(RING)]
            z = [sb(f"z{i}", [P, D]) for i in range(RING)]
            x1 = [sb(f"x1_{i}", [P, D]) for i in range(RING)]
            stat = [sb(f"c_stat{i}", [P, 6]) for i in range(RING)]
            mv = [sb(f"c_mv{i}", [P, 2]) for i in range(RING)]
            rstd = [sb(f"c_rstd{i}", [P, 1]) for i in range(RING)]
            veps = [sb(f"c_veps{i}", [P, 1]) for i in range(RING)]
            nmr = [sb(f"c_nmr{i}", [P, 1]) for i in range(RING)]
            minus_half = sb("c_minus_half", [P, 1])
            hi = [sb(f"c_hi{i}", [P, D], F32R) for i in range(RING)]
            lo = [sb(f"c_lo{i}", [P, D], F32R) for i in range(RING)]
            qo = [sb(f"qo{i}", [P, D]) for i in range(RING)]
            kvo = [sb(f"kvo{i}", [P, 2 * D]) for i in range(RING)]
            bias_q, bias_kv = sb("bias_q", [P, D]), sb("bias_kv", [P, 2 * D])
            mean, var, tmp = sb("c_mean", [P, D]), sb("c_var", [P, D]), sb("c_tmp", [P, D])
            gain, shift = sb("c_gain", [P, D]), sb("c_shift", [P, D])
            norm2_mul, norm2_add = sb("norm2_mul", [P, D]), sb("norm2_add", [P, D])
            y_loaded, x_loaded, stored, consts = sems("c_y_loaded", RING), sems("c_x_loaded", RING), sems("c_stored", RING), sem("c_consts")
            kv_stored, x1_stored = sems("c_kv_stored", RING), sems("c_x1_stored", RING)
            totals, affine, root, x_shifted, y_scaled, z_ready = (sem("c_" + n) for n in ("totals", "affine", "root", "x_shifted", "y_scaled", "z_ready"))
            stat_ready, mv_ready, veps_ready, rstd_ready, nmr_ready, x1_ready = (sem("c_" + n) for n in ("stat_ready", "mv_ready", "veps_ready", "rstd_ready", "nmr_ready", "x1_ready"))
            turned, hi_ready, lo_ready, made, q_ready, kv_ready, half_ready = (sem("c_" + n) for n in ("turned", "hi_ready", "lo_ready", "made", "q_ready", "kv_ready", "half_ready"))
            tpose = [bank[0], bank[1]]
            pq, pk, pv = [bank[2], bank[3]], [bank[4], bank[5]], [bank[6], bank[7]]
            with nc.Block() as block:
                @block.sync
                def _(sp):
                    for t, v in ((gain, g2), (shift, b2), (bias_q, bq), (bias_kv, bkv)):
                        sp.dma_start(t[:, :], row_on_all(v)).then_inc(consts, 16)

                    def load(s):
                        u, r = s.slot, rows(s)
                        if s.reaches(RING):
                            sp.wait_ge(y_scaled, s.n - RING + 1)
                        sp.dma_start(yb[u][0:r, :], node_rows(y_dram, s)).then_inc(y_loaded[u], 16)
                        if s.reaches(RING):
                            sp.wait_ge(z_ready, s.n - RING + 1)
                        sp.dma_start(xc[u][0:r, :], node_rows(x, s)).then_inc(x_loaded[u], 16)

                    def store(s):
                        u, r = s.slot, rows(s)
                        sp.wait_ge(x1_ready, s.n + 1)
                        sp.dma_start(node_rows(x1_dram, s), x1[u][0:r, :]).then_inc(x1_stored[u], 16)

                    load(Step(RING, 0, 0))
                    load(Step(RING, 0, 1))

                    def both(s):
                        store(s)
                        if not isinstance(s.n, int) or s.n + 2 < TILES:
                            load(s.ahead(2))
                    steps(sp, TILES, RING, both, peel_last=3)
                    for s in (Step(RING, n // RING, n % RING) for n in range(TILES - RING, TILES)):
                        sp.wait_ge(x1_stored[s.slot], landed(s))

                @block.gpsimd
                def _(pool):
                    pool.memset(minus_half[:, :], -0.5).then_inc(half_ready, 1)
                    pool.wait_ge(half_ready, 1)
                    pool.wait_ge(affine, 8)

                    def shift_x(s):
                        u, r = s.slot, rows(s)
                        pool.wait_ge(x_loaded[u], landed(s))
                        pool.tensor_tensor(xc[u][0:r, :], xc[u][0:r, :], norm2_add[0:r, :], ALU.add).then_inc(x_shifted, 1)

                    def inverse_root(s):
                        u, r = s.slot, rows(s)
                        pool.wait_ge(veps_ready, s.n + 1)
                        pool.tensor_tensor(rstd[u][0:r, :], veps[u][0:r, :], minus_half[0:r, :], ALU.pow).then_inc(rstd_ready, 1)

                    shift_x(Step(RING, 0, 0))

                    def both(s):
                        if not isinstance(s.n, int) or s.n + 1 < TILES:
                            shift_x(s.ahead(1))
                        inverse_root(s)
                    steps(pool, TILES, RING, both, peel_last=2)

                @block.tensor
                def _(pe):
                    pe.matmul(bank[2][:, :], ones[:, :], y_sum[:, :], start=True, stop=True)
                    pe.matmul(bank[3][:, :], ones[:, :], y_sq_sum[:, :], start=True, stop=True).then_inc(totals, 1)

                    def turn(s):
                        pe.wait_ge(x1_ready, s.n + 1)
                        if s.reaches(RING):
                            pe.wait_ge(lo_ready, s.n - RING + 1)
                        turn_tile(pe, tpose[s.slot], x1[s.slot], rows(s)).then_inc(turned, 1)

                    def multiply(s):
                        u, r = s.slot, rows(s)
                        pe.wait_ge(lo_ready, s.n + 1)
                        if s.reaches(RING):
                            pe.wait_ge(kv_ready, s.n - RING + 1)
                        product(pe, pq[u], hi[u], lo[u], "q", r).then_inc(made, 1)
                        product(pe, pk[u], hi[u], lo[u], "k", r).then_inc(made, 1)
                        product(pe, pv[u], hi[u], lo[u], "v", r).then_inc(made, 1)

                    turn(Step(RING, 0, 0))

                    def both(s):
                        if not isinstance(s.n, int) or s.n + 1 < TILES:
                            turn(s.ahead(1))
                        multiply(s)
                    steps(pe, TILES, RING, both, peel_last=2)

                @block.scalar
                def _(act):
                    act.wait_ge(affine, 4)
                    act.activation(var[:, :], var[:, :], ACT.Sqrt).then_inc(root, 1)

                    def normalize(s):
                        u, r = s.slot, rows(s)
                        act.wait_ge(nmr_ready, s.n + 1)
                        act.wait_ge(rstd_ready, s.n + 1)
                        if s.reaches(RING):
                            act.wait_ge(x1_stored[u], landed(s) - 16)
                            act.wait_ge(turned, s.n - RING + 1)
                        act.activation(x1[u][0:r, :], z[u][0:r, :], ACT.Identity, bias=nmr[u][0:r, 0:1], scale=rstd[u][0:r, 0:1]).then_inc(x1_ready, 1)

                    def copy_hi(s):
                        u, r = s.slot, rows(s)
                        act.wait_ge(turned, s.n + 1)
                        if s.reaches(RING):
                            act.wait_ge(made, 3 * (s.n - RING + 1))
                        act.activation(blocks_of(hi[u], r), blocks_of(tpose[u], r), ACT.Copy).then_inc(hi_ready, 1)

                    def store(s):
                        u, r = s.slot, rows(s)
                        act.wait_ge(q_ready, s.n + 1)
                        act.dma_start(node_rows(q_dram, s), qo[u][0:r, :]).then_inc(stored[u], 16)
                        act.wait_ge(kv_ready, s.n + 1)
                        act.dma_start(node_rows(kv_dram, s), kvo[u][0:r, :]).then_inc(kv_stored[u], 16)

                    normalize(Step(RING, 0, 0))
                    copy_hi(Step(RING, 0, 0))

                    def all3(s):
                        if not isinstance(s.n, int) or s.n + 1 < TILES:
                            normalize(s.ahead(1))
                            copy_hi(s.ahead(1))
                        store(s)
                    steps(act, TILES, RING, all3, peel_last=2)
                    for s in (Step(RING, n // RING, n % RING) for n in range(TILES - RING, TILES)):
                        act.wait_ge(stored[s.slot], landed(s))
                        act.wait_ge(kv_stored[s.slot], landed(s))

                @block.vector
                def _(dve):
                    dve.wait_ge(totals, 1)
                    dve.tensor_scalar(mean[:, :], bank[2][:, :], 1.0 / N, None, ALU.mult).then_inc(affine, 1)
                    dve.tensor_scalar(var[:, :], bank[3][:, :], 1.0 / N, EPS, ALU.mult, ALU.add).then_inc(affine, 1)
                    dve.wait_ge(affine, 2)
                    dve.tensor_tensor(tmp[:, :], mean[:, :], mean[:, :], ALU.mult).then_inc(affine, 1)
                    dve.wait_ge(affine, 3)
                    dve.tensor_tensor(var[:, :], var[:, :], tmp[:, :], ALU.subtract).then_inc(affine, 1)
                    dve.wait_ge(root, 1)
                    dve.reciprocal(tmp[:, :], var[:, :]).then_inc(affine, 1)
                    dve.wait_ge(affine, 5)
                    dve.wait_ge(consts, 64)
                    dve.tensor_tensor(norm2_mul[:, :], tmp[:, :], gain[:, :], ALU.mult).then_inc(affine, 1)
                    dve.wait_ge(affine, 6)
                    dve.tensor_tensor(tmp[:, :], mean[:, :], norm2_mul[:, :], ALU.mult).then_inc(affine, 1)
                    dve.wait_ge(affine, 7)
                    dve.tensor_tensor(norm2_add[:, :], shift[:, :], tmp[:, :], ALU.subtract).then_inc(affine, 1)

                    def front(s):
                        u, r = s.slot, rows(s)
                        dve.wait_ge(y_loaded[u], landed(s))
                        dve.tensor_tensor(ym[u][0:r, :], yb[u][0:r, :], norm2_mul[0:r, :], ALU.mult).then_inc(y_scaled, 1)
                        dve.wait_ge(y_scaled, s.n + 1)
                        dve.wait_ge(x_shifted, s.n + 1)
                        if s.reaches(RING):
                            dve.wait_ge(x1_ready, s.n - RING + 1)
                        dve.tensor_tensor(z[u][0:r, :], ym[u][0:r, :], xc[u][0:r, :], ALU.add).then_inc(z_ready, 1)
                        dve.wait_ge(z_ready, s.n + 1)
                        dve.bn_stats(stat[u][0:r, :], z[u][0:r, :]).then_inc(stat_ready, 1)
                        wait_alone(dve, stat_ready, s.n + 1, passed)
                        dve.bn_aggr(mv[u][0:r, :], stat[u][0:r, :]).then_inc(mv_ready, 1)
                        dve.wait_ge(mv_ready, s.n + 1)
                        dve.tensor_scalar(veps[u][0:r, :], mv[u][0:r, 1:2], EPS, None, ALU.add).then_inc(veps_ready, 1)
                        dve.wait_ge(rstd_ready, s.n + 1)
                        dve.scalar_tensor_tensor(nmr[u][0:r, :], mv[u][0:r, 0:1], -1.0, rstd[u][0:r, :], ALU.mult, ALU.mult).then_inc(nmr_ready, 1)

                    def take_lo(s):
                        u, r = s.slot, rows(s)
                        dve.wait_ge(hi_ready, s.n + 1)
                        dve.tensor_tensor(blocks_of(lo[u], r), blocks_of(tpose[u], r), blocks_of(hi[u], r).bitcast(F32), ALU.subtract).then_inc(lo_ready, 1)

                    def add_bias(s):
                        u, r = s.slot, rows(s)
                        dve.wait_ge(made, 3 * s.n + 1)
                        if s.reaches(RING):
                            dve.wait_ge(stored[u], landed(s) - 16)
                            dve.wait_ge(kv_stored[u], landed(s) - 16)
                        dve.tensor_tensor(qo[u][0:r, :], pq[u][0:r, :], bias_q[0:r, :], ALU.add).then_inc(q_ready, 1)
                        dve.wait_ge(made, 3 * s.n + 2)
                        dve.tensor_tensor(kvo[u][0:r, 0:D], pk[u][0:r, :], bias_kv[0:r, 0:D], ALU.add)
                        dve.wait_ge(made, 3 * s.n + 3)
                        dve.tensor_tensor(kvo[u][0:r, D:2 * D], pv[u][0:r, :], bias_kv[0:r, D:2 * D], ALU.add).then_inc(kv_ready, 1)

                    front(Step(RING, 0, 0))
                    take_lo(Step(RING, 0, 0))

                    def all3(s):
                        if not isinstance(s.n, int) or s.n + 1 < TILES:
                            front(s.ahead(1))
                            take_lo(s.ahead(1))
                        add_bias(s)
                    steps(dve, TILES, RING, all3, peel_last=2)

        with ExitStack() as ctx:
            sb = tensors(ctx, "attend")
            RING = 3
            window = [sb(f"d_window{i}", [P, P + 1]) for i in range(RING)]
            same = [sb(f"d_same{i}", [P, P]) for i in range(RING)]
            apart = [sb(f"apart{i}", [HEADS, P + 1]) for i in range(RING)]
            idx = [sb(f"d_idx{i}", [P, 4], I32) for i in range(RING)]
            qe = [sb(f"qe{i}", [P, D]) for i in range(RING)]
            kve = [sb(f"kve{i}", [P, 2 * D]) for i in range(RING)]
            qk = [sb(f"qk{i}", [P, D]) for i in range(2)]
            score = [sb(f"score{i}", [P, HEADS]) for i in range(RING)]
            scoreT = [sb(f"scoreT{i}", [HEADS, P]) for i in range(RING)]
            upto = [sb(f"upto{i}", [HEADS, P]) for i in range(RING)]
            peakT = [sb(f"peakT{i}", [HEADS, P]) for i in range(RING)]
            below = [sb(f"d_below{i}", [HEADS, P]) for i in range(RING)]
            probT = [sb(f"probT{i}", [HEADS, P]) for i in range(RING)]
            weight = [sb(f"weight{i}", [P, HEADS]) for i in range(RING)]
            prob = [sb(f"prob{i}", [P, HEADS]) for i in range(RING)]
            pv_e = [sb(f"pv_e{i}", [P, D]) for i in range(RING)]
            inv = [sb(f"d_inv{i}", [P, HEADS]) for i in range(RING)]
            orow = [sb(f"orow{i}", [P, D]) for i in range(RING)]
            window_loaded, q_got, kv_got, scattered = sems("d_window_loaded", RING), sems("d_q_got", RING), sems("d_kv_got", RING), sems("d_scattered", RING)
            names = ("cleared", "indexed", "same_ready", "apart_ready", "qk_ready", "score_ready", "score_turned", "scoreT_ready", "upto_ready",
                     "peak_ready", "below_ready", "probT_ready", "prob_turned", "prob_ready", "pv_ready", "summed", "inverted", "o_ready", "carried", "score_carried", "weight_carried")
            d = {n: sem("d_" + n) for n in names}
            sums = [bank[0], bank[1], bank[2]]
            small = [bank[3], bank[4], bank[5]]
            dens = [b[:, 0:HEADS] for b in small]
            scoreT_ps = bank[6][0:HEADS, 0:P]
            prob_ps = bank[7][:, 0:HEADS]
            SCALE = float(1.0 / np.sqrt(np.float32(DH)))

            def heads(t):
                return t.rearrange("p (h c) -> p h c", h=HEADS)

            def per_head(t):
                return t.rearrange("p (h c) -> p h c", c=1).to_broadcast([P, HEADS, DH])

            with nc.Block() as block:
                @block.sync
                def _(sp):
                    def load(s):
                        if s.reaches(RING):
                            sp.wait_ge(d["apart_ready"], s.n - RING + 1)
                        sp.dma_start(window[s.slot][:, :], dst_f[0:1, bass.ds(s.n * EPC, P + 1)].to_broadcast([P, P + 1])).then_inc(window_loaded[s.slot], 16)
                    steps(sp, CHUNKS, RING, load)

                @block.gpsimd
                def _(pool):
                    limit = pool.to_reg(N - 1)

                    def gather(s):
                        u = s.slot
                        if s.reaches(RING):
                            pool.wait_ge(scattered[u], landed(s) - 16)
                        pool.tensor_copy(idx[u][:, :], edge_index[:, bass.ds(s.n, 1), :].rearrange("p a b -> p (a b)")).then_inc(d["indexed"], 1)
                        if s.reaches(RING):
                            pool.wait_ge(d["summed"], s.n - RING + 1)
                        wait_alone(pool, d["indexed"], s.n + 1, passed)
                        pool.indirect_dma_start(out=qe[u][:, :], out_offset=None, in_=q_dram[0:N, :],
                                                in_offset=bass.IndirectOffsetOnAxis(ap=idx[u][:, 1:2], axis=0),
                                                bounds_check=limit, oob_is_err=False).then_inc(q_got[u], 16)
                        pool.indirect_dma_start(out=kve[u][:, :], out_offset=None, in_=kv_dram[0:N, :],
                                                in_offset=bass.IndirectOffsetOnAxis(ap=idx[u][:, 0:1], axis=0),
                                                bounds_check=limit, oob_is_err=False).then_inc(kv_got[u], 16)

                    def scatter(s):
                        u = s.slot
                        wait_alone(pool, d["o_ready"], s.n + 1, passed)
                        pool.indirect_dma_start(out=attended, out_offset=bass.IndirectOffsetOnAxis(ap=idx[u][:, 2:3], axis=0),
                                                in_=orow[u][:, :], in_offset=None,
                                                bounds_check=limit, oob_is_err=False).then_inc(scattered[u], 16)

                    for i in range(RING):
                        pool.memset(qe[i][:, :], 0.0).then_inc(d["cleared"], 1)
                        pool.memset(kve[i][:, :], 0.0).then_inc(d["cleared"], 1)
                        pool.memset(weight[i][:, :], 1.0).then_inc(d["cleared"], 1)
                    pool.wait_ge(d["cleared"], 3 * RING)
                    pool.memset(weight[0][0:1, :], 0.0).then_inc(d["cleared"], 1)
                    for n in range(RING - 1):
                        gather(Step(RING, 0, n))

                    def turn(s):
                        if not isinstance(s.n, int) or s.n + RING - 1 < CHUNKS:
                            gather(s.ahead(RING - 1))
                        scatter(s)
                    steps(pool, CHUNKS, RING, turn, peel_last=RING)
                    for s in (Step(RING, n // RING, n % RING) for n in range(CHUNKS - RING, CHUNKS)):
                        pool.wait_ge(scattered[s.slot], landed(s))

                @block.vector
                def _(dve):
                    dve.memset(scoreT[0][:, 0:1], -FAR).then_inc(d["score_carried"], 1)

                    def scores(s):
                        u = s.slot
                        dve.wait_ge(window_loaded[u], landed(s))
                        if s.reaches(RING):
                            dve.wait_ge(d["summed"], s.n - RING + 1)
                        own = dst_col[:, bass.ds(s.n, 1)]
                        dve.tensor_scalar(same[u][:, 1:P], window[u][:, 1:P], own, None, ALU.is_equal)
                        dve.tensor_scalar(same[u][:, 0:1], window[u][:, P - 1:P], own, None, ALU.is_equal).then_inc(d["same_ready"], 1)
                        dve.tensor_tensor(apart[u][:, 1:P + 1], window[u][0:HEADS, 1:P + 1], window[u][0:HEADS, 0:P], ALU.not_equal)
                        dve.memset(apart[u][:, 0:1], 0.0).then_inc(d["apart_ready"], 1)
                        dve.wait_ge(q_got[u], landed(s))
                        dve.wait_ge(kv_got[u], landed(s))
                        w = s.slot % 2
                        dve.tensor_tensor(qk[w][:, :], qe[u][:, :], kve[u][:, 0:D], ALU.mult).then_inc(d["qk_ready"], 1)
                        dve.wait_ge(d["apart_ready"], s.n + 1)
                        dve.tensor_scalar(apart[u][:, :], apart[u][:, :], -FAR, None, ALU.mult)
                        dve.wait_ge(d["qk_ready"], s.n + 1)
                        if s.reaches(RING):
                            dve.wait_ge(d["score_turned"], s.n - RING + 1)
                        dve.tensor_reduce(score[u][:, :], heads(qk[w][:, :]), AX.X, ALU.add).then_inc(d["score_ready"], 1)

                    def peaks(s):
                        u, to = s.slot, s.ahead(1)
                        dve.wait_ge(d["score_turned"], s.n + 1)
                        dve.tensor_copy(scoreT[u][:, 1:P], scoreT_ps[:, 1:P]).then_inc(d["scoreT_ready"], 1)
                        dve.wait_ge(d["scoreT_ready"], s.n + 1)
                        dve.wait_ge(d["score_carried"], s.n + 1)
                        dve.tensor_tensor_scan(upto[u][:, :], apart[u][:, 0:P], scoreT[u][:, :], -FAR, ALU.add, ALU.max).then_inc(d["upto_ready"], 1)
                        dve.wait_ge(d["upto_ready"], s.n + 1)
                        if s.reaches(RING):
                            dve.wait_ge(d["probT_ready"], s.n - RING + 1)
                        dve.tensor_tensor_scan(peakT[u][:, ::-1], apart[u][:, 1:P + 1][:, ::-1], upto[u][:, ::-1], -FAR, ALU.add, ALU.max).then_inc(d["peak_ready"], 1)
                        dve.wait_ge(d["peak_ready"], s.n + 1)
                        dve.tensor_copy(scoreT[to.slot][:, 0:1], peakT[u][:, P - 1:P]).then_inc(d["score_carried"], 1)
                        dve.tensor_tensor(below[u][:, :], scoreT[u][:, :], peakT[u][:, :], ALU.subtract).then_inc(d["below_ready"], 1)

                    def values(s):
                        u = s.slot
                        dve.wait_ge(d["prob_turned"], s.n + 1)
                        if s.reaches(1):
                            dve.wait_ge(d["carried"], s.n)
                        dve.tensor_tensor(prob[u][:, :], prob_ps, weight[u][:, :], ALU.mult)
                        dve.tensor_tensor(heads(pv_e[u][:, :]), heads(kve[u][:, D:2 * D]), per_head(prob_ps), ALU.mult).then_inc(d["pv_ready"], 1)

                    def normalize(s):
                        u = s.slot
                        if isinstance(s.n, int) and s.n == CHUNKS - 1:
                            dve.wait_ge(d["summed"], s.n + 1)
                        else:
                            dve.wait_ge(d["carried"], s.n + 1)
                        dve.reciprocal(inv[u][:, :], dens[u]).then_inc(d["inverted"], 1)
                        dve.wait_ge(d["inverted"], s.n + 1)
                        if s.reaches(RING):
                            dve.wait_ge(scattered[u], landed(s) - 16)
                        dve.tensor_tensor(heads(orow[u][:, :]), heads(sums[u][:, :]), per_head(inv[u][:, :]), ALU.mult).then_inc(d["o_ready"], 1)

                    dve.wait_ge(d["cleared"], 3 * RING + 1)
                    scores(Step(RING, 0, 0))

                    def turn(s):
                        peaks(s)
                        if not isinstance(s.n, int) or s.n + 1 < CHUNKS:
                            scores(s.ahead(1))
                        values(s)
                        normalize(s)
                    steps(dve, CHUNKS, RING, turn, peel_last=2)

                @block.tensor
                def _(pe):
                    def turn_scores(s):
                        pe.wait_ge(d["score_ready"], s.n + 1)
                        if s.reaches(1):
                            pe.wait_ge(d["scoreT_ready"], s.n)
                        pe.transpose(scoreT_ps, score[s.slot][:, :], identity[:, :]).then_inc(d["score_turned"], 1)

                    def total(s):
                        u = s.slot
                        wait_alone(pe, d["probT_ready"], s.n + 1, passed)
                        if s.reaches(1):
                            wait_alone(pe, d["pv_ready"], s.n, passed)
                        pe.transpose(prob_ps, probT[u][:, :], identity[0:HEADS, 0:HEADS]).then_inc(d["prob_turned"], 1)
                        pe.wait_ge(d["pv_ready"], s.n + 1)
                        if s.reaches(RING):
                            pe.wait_ge(d["o_ready"], s.n - RING + 1)
                        if s.reaches(RING):
                            pe.wait_ge(d["carried"], s.n - RING + 1)
                        pe.matmul(dens[u], same[u][:, :], prob[u][:, :], start=True, stop=True)
                        pe.matmul(sums[u][:, :], same[u][:, :], pv_e[u][:, :], start=True, stop=True).then_inc(d["summed"], 1)

                    turn_scores(Step(RING, 0, 0))

                    def both(s):
                        total(s)
                        if not isinstance(s.n, int) or s.n + 1 < CHUNKS:
                            turn_scores(s.ahead(1))
                    steps(pe, CHUNKS, RING, both, peel_last=2)

                @block.scalar
                def _(act):
                    act.wait_ge(d["cleared"], 3 * RING + 1)

                    def exponent(s):
                        u = s.slot
                        act.wait_ge(d["below_ready"], s.n + 1)
                        if s.reaches(RING):
                            act.wait_ge(d["prob_turned"], s.n - RING + 1)
                        act.activation(probT[u][:, :], below[u][:, :], ACT.Exp, scale=SCALE).then_inc(d["probT_ready"], 1)

                    def carry(s):
                        u, to = s.slot, s.ahead(1)
                        act.wait_ge(d["summed"], s.n + 1)
                        act.activation(weight[to.slot][0:1, :], dens[u][0:1, :], ACT.Copy)
                        act.wait_ge(kv_got[to.slot], landed(to))
                        act.activation(kve[to.slot][0:1, D:2 * D], sums[u][0:1, :], ACT.Copy).then_inc(d["carried"], 1)

                    def both(s):
                        exponent(s)
                        if not isinstance(s.n, int) or s.n + 1 < CHUNKS:
                            carry(s)
                    steps(act, CHUNKS, RING, both, peel_last=2)

        with ExitStack() as ctx:
            sb = tensors(ctx, "out")
            RING = 2
            ob = [sb(f"ob{i}", [P, D]) for i in range(RING)]
            xr = [sb(f"xr{i}", [P, D]) for i in range(RING)]
            z = [sb(f"e_z{i}", [P, D]) for i in range(RING)]
            res = [sb(f"res{i}", [P, D]) for i in range(RING)]
            stat = [sb(f"e_stat{i}", [P, 6]) for i in range(RING)]
            mv = [sb(f"e_mv{i}", [P, 2]) for i in range(RING)]
            rstd = [sb(f"e_rstd{i}", [P, 1]) for i in range(RING)]
            veps = [sb(f"e_veps{i}", [P, 1]) for i in range(RING)]
            nmr = [sb(f"e_nmr{i}", [P, 1]) for i in range(RING)]
            minus_half = sb("e_minus_half", [P, 1])
            hi = [sb(f"e_hi{i}", [P, D], F32R) for i in range(RING)]
            lo = [sb(f"e_lo{i}", [P, D], F32R) for i in range(RING)]
            bias_o = sb("bias_o", [P, D])
            o_loaded, x_loaded, stored, consts = sems("e_o_loaded", RING), sems("e_x_loaded", RING), sems("e_stored", RING), sem("e_consts")
            names = ("half_ready", "x_biased", "turned", "hi_ready", "lo_ready", "made", "z_ready", "stat_ready", "mv_ready", "veps_ready", "rstd_ready", "nmr_ready", "res_ready")
            e = {n: sem("e_" + n) for n in names}
            tpose, acc = [bank[0], bank[1]], [bank[2], bank[3]]
            with nc.Block() as block:
                @block.sync
                def _(sp):
                    sp.dma_start(bias_o[:, :], row_on_all(bo)).then_inc(consts, 16)

                    def load(s):
                        u, r = s.slot, rows(s)
                        if s.reaches(RING):
                            sp.wait_ge(e["turned"], s.n - RING + 1)
                        sp.dma_start(ob[u][0:r, :], node_rows(attended, s)).then_inc(o_loaded[u], 16)
                        if s.reaches(RING):
                            sp.wait_ge(e["z_ready"], s.n - RING + 1)
                        sp.dma_start(xr[u][0:r, :], node_rows(x1_dram, s)).then_inc(x_loaded[u], 16)
                    steps(sp, TILES, RING, load)

                @block.gpsimd
                def _(pool):
                    pool.memset(minus_half[:, :], -0.5).then_inc(e["half_ready"], 1)
                    pool.wait_ge(e["half_ready"], 1)
                    pool.wait_ge(consts, 16)

                    def add_bias(s):
                        u, r = s.slot, rows(s)
                        pool.wait_ge(x_loaded[u], landed(s))
                        pool.tensor_tensor(xr[u][0:r, :], xr[u][0:r, :], bias_o[0:r, :], ALU.add).then_inc(e["x_biased"], 1)

                    def inverse_root(s):
                        u, r = s.slot, rows(s)
                        pool.wait_ge(e["veps_ready"], s.n + 1)
                        pool.tensor_tensor(rstd[u][0:r, :], veps[u][0:r, :], minus_half[0:r, :], ALU.pow).then_inc(e["rstd_ready"], 1)

                    add_bias(Step(RING, 0, 0))

                    def both(s):
                        if not isinstance(s.n, int) or s.n + 1 < TILES:
                            add_bias(s.ahead(1))
                        inverse_root(s)
                    steps(pool, TILES, RING, both, peel_last=2)

                @block.tensor
                def _(pe):
                    def turn(s):
                        pe.wait_ge(o_loaded[s.slot], landed(s))
                        if s.reaches(RING):
                            pe.wait_ge(e["lo_ready"], s.n - RING + 1)
                        turn_tile(pe, tpose[s.slot], ob[s.slot], rows(s)).then_inc(e["turned"], 1)

                    def multiply(s):
                        pe.wait_ge(e["lo_ready"], s.n + 1)
                        if s.reaches(RING):
                            pe.wait_ge(e["z_ready"], s.n - RING + 1)
                        product(pe, acc[s.slot], hi[s.slot], lo[s.slot], "o", rows(s)).then_inc(e["made"], 1)

                    turn(Step(RING, 0, 0))

                    def both(s):
                        if not isinstance(s.n, int) or s.n + 1 < TILES:
                            turn(s.ahead(1))
                        multiply(s)
                    steps(pe, TILES, RING, both, peel_last=2)

                @block.scalar
                def _(act):
                    def copy_hi(s):
                        u, r = s.slot, rows(s)
                        act.wait_ge(e["turned"], s.n + 1)
                        if s.reaches(RING):
                            act.wait_ge(e["made"], s.n - RING + 1)
                        act.activation(blocks_of(hi[u], r), blocks_of(tpose[u], r), ACT.Copy).then_inc(e["hi_ready"], 1)

                    def finish(s):
                        u, r = s.slot, rows(s)
                        act.wait_ge(e["nmr_ready"], s.n + 1)
                        act.wait_ge(e["rstd_ready"], s.n + 1)
                        if s.reaches(RING):
                            act.wait_ge(stored[u], landed(s) - 16)
                        act.activation(res[u][0:r, :], z[u][0:r, :], ACT.Identity, bias=nmr[u][0:r, 0:1], scale=rstd[u][0:r, 0:1]).then_inc(e["res_ready"], 1)
                        act.wait_ge(e["res_ready"], s.n + 1)
                        act.dma_start(node_rows(out, s), res[u][0:r, :]).then_inc(stored[u], 16)

                    copy_hi(Step(RING, 0, 0))

                    def both(s):
                        if not isinstance(s.n, int) or s.n + 1 < TILES:
                            copy_hi(s.ahead(1))
                        finish(s)
                    steps(act, TILES, RING, both, peel_last=2)
                    for s in (Step(RING, n // RING, n % RING) for n in range(TILES - RING, TILES)):
                        act.wait_ge(stored[s.slot], landed(s))

                @block.vector
                def _(dve):
                    def take_lo(s):
                        u, r = s.slot, rows(s)
                        dve.wait_ge(e["hi_ready"], s.n + 1)
                        dve.tensor_tensor(blocks_of(lo[u], r), blocks_of(tpose[u], r), blocks_of(hi[u], r).bitcast(F32), ALU.subtract).then_inc(e["lo_ready"], 1)

                    def finish(s):
                        u, r = s.slot, rows(s)
                        dve.wait_ge(e["made"], s.n + 1)
                        dve.wait_ge(e["x_biased"], s.n + 1)
                        if s.reaches(RING):
                            dve.wait_ge(e["res_ready"], s.n - RING + 1)
                        dve.tensor_tensor(z[u][0:r, :], acc[u][0:r, :], xr[u][0:r, :], ALU.add).then_inc(e["z_ready"], 1)
                        dve.wait_ge(e["z_ready"], s.n + 1)
                        dve.bn_stats(stat[u][0:r, :], z[u][0:r, :]).then_inc(e["stat_ready"], 1)
                        wait_alone(dve, e["stat_ready"], s.n + 1, passed)
                        dve.bn_aggr(mv[u][0:r, :], stat[u][0:r, :]).then_inc(e["mv_ready"], 1)
                        dve.wait_ge(e["mv_ready"], s.n + 1)
                        dve.tensor_scalar(veps[u][0:r, :], mv[u][0:r, 1:2], EPS, None, ALU.add).then_inc(e["veps_ready"], 1)
                        dve.wait_ge(e["rstd_ready"], s.n + 1)
                        dve.scalar_tensor_tensor(nmr[u][0:r, :], mv[u][0:r, 0:1], -1.0, rstd[u][0:r, :], ALU.mult, ALU.mult).then_inc(e["nmr_ready"], 1)

                    take_lo(Step(RING, 0, 0))

                    def both(s):
                        if not isinstance(s.n, int) or s.n + 1 < TILES:
                            take_lo(s.ahead(1))
                        finish(s)
                    steps(dve, TILES, RING, both, peel_last=2)


def kernel(**inputs):
    import concourse.bacc as bacc
    from concourse.bass_utils import run_bass_kernel_spmd

    a = {k: np.asarray(v) for k, v in inputs.items()}
    wkv, bkv = a["L1_gnn_Wkv"], a["L1_gnn_bkv"]
    wkv = wkv.reshape(HEADS, 2, DH, D).transpose(1, 0, 2, 3).reshape(2 * D, D)
    bkv = bkv.reshape(HEADS, 2, DH).transpose(1, 0, 2).reshape(2 * D)
    arrays = {
        "x": a["x"], "src": a["src"], "dst": a["dst"],
        "g1": a["L0_gnn_norm1_g"], "b1": a["L0_gnn_norm1_b"], "g2": a["L0_gnn_norm2_g"], "b2": a["L0_gnn_norm2_b"],
        "w_conv": a["L0_gnn_W_conv"], "b_conv": a["L0_gnn_b_conv"],
        "fq": a["L0_gnn_Wq"], "fk": a["L0_gnn_Wk"], "fv": a["L0_gnn_Wv"], "fo": a["L0_gnn_Wo"],
        "projT": a["L0_gnn_proj"].T,
        "wqT": a["L1_gnn_Wq"].T, "bq": a["L1_gnn_bq"], "wkvT": wkv.T, "bkv": bkv,
        "woT": a["L1_gnn_Wo"].T, "bo": a["L1_gnn_bo"],
    }
    arrays = {f"in_{k}": np.ascontiguousarray(v) for k, v in arrays.items()}
    nc = bacc.Bacc("TRN2", target_bir_lowering=False, num_devices=1)
    args = [nc.dram_tensor(k, v.shape, mybir.dt.from_np(v.dtype), kind="ExternalInput").ap() for k, v in arrays.items()]
    out = nc.dram_tensor("out_dram", list(a["x"].shape), F32, kind="ExternalOutput").ap()
    gnn_program(nc, *args, out)
    r = run_bass_kernel_spmd(nc, [arrays], core_ids=[0])
    return r.results[0]["out_dram"]
```

```python
from contextlib import ExitStack

import numpy as np
import concourse.bass as bass
from concourse import mybir

F32 = mybir.dt.float32
F32R = mybir.dt.float32r
I32 = mybir.dt.int32
ACT = mybir.ActivationFunctionType
ALU = mybir.AluOpType
AX = mybir.AxisListType
RMAX = bass.bass_isa.ReduceOp.max

P = 128
D = 512
KC = D // P
HEADS = 8
DH = D // HEADS
NF = 256
EPS = 1e-5
KEPS = 1e-6
BIG = 20000.0
FAR = 1e30


class Step:

    def __init__(self, ring, j, slot):
        self.ring, self.j, self.slot = ring, j, slot
        self.n = j * ring + slot

    def ahead(self, k):
        return Step(self.ring, self.j + (self.slot + k) // self.ring, (self.slot + k) % self.ring)

    def reaches(self, k):
        return not isinstance(self.n, int) or self.n >= k

    def before(self):
        return Step(self.ring, self.j, self.slot - 1) if self.slot else Step(self.ring, self.j - 1, self.ring - 1)

    def within(self, total):
        return not isinstance(self.n, int) or self.n < total


def steps(engine, total, ring, body, peel_last=1):
    rings = (total - peel_last) // ring
    for n in range(ring):
        body(Step(ring, 0, n))
    with engine.Fori(1, rings) as j:
        for slot in range(ring):
            body(Step(ring, j, slot))
    for n in range(rings * ring, total):
        body(Step(ring, n // ring, n % ring))


def wait_alone(engine, semaphore, value, passed):
    engine.wait_ge(semaphore, value)
    engine.sem_inc(passed, 1)


def landed(step, semaphores):
    n = len(semaphores)
    return 16 * (step.j * (step.ring // n) + step.slot // n + 1)


def at(buffers, step):
    return buffers[step.slot % len(buffers)]


def wait_landed(engine, semaphores, step):
    engine.wait_ge(at(semaphores, step), landed(step, semaphores))


def wait_landed_before(engine, semaphores, step):
    if step.reaches(len(semaphores)):
        engine.wait_ge(at(semaphores, step), landed(step, semaphores) - 16)


def wait_all(engine, semaphores, total, ring):
    for n in range(total - len(semaphores), total):
        wait_landed(engine, semaphores, Step(ring, n // ring, n % ring))


def wait_before(engine, semaphore, step, distance):
    if step.reaches(distance):
        engine.wait_ge(semaphore, step.n - distance + 1)


def gnn_program(nc, x, src, dst, g1, b1, g2, b2, w_conv, b_conv, fq, fk, fv, fo, projT,
                wqT, bq, wkvT, bkv, woT, bo, out):
    N = x.shape[0]
    E = src.shape[0]
    TILES = -(-N // P)
    LAST_ROWS = N - (TILES - 1) * P
    EPC = P - 1
    CHUNKS = -(-E // EPC)
    PADDED = CHUNKS * EPC + 2
    NODES = TILES * P

    def rows(step):
        return LAST_ROWS if isinstance(step.n, int) and step.n == TILES - 1 else P

    aggregated = nc.dram_tensor("aggregated", [NODES, D], F32, kind="Internal").ap()
    attended = nc.dram_tensor("attended", [NODES, D], F32, kind="Internal").ap()
    y_dram = nc.dram_tensor("y_dram", [NODES, D], F32, kind="Internal").ap()
    x1_dram = nc.dram_tensor("x1_dram", [NODES, D], F32, kind="Internal").ap()
    q_dram = nc.dram_tensor("q_dram", [NODES, D], F32, kind="Internal").ap()
    apart_dram = nc.dram_tensor("apart_dram", [CHUNKS, P + 1], F32, kind="Internal").ap()
    kv_dram = nc.dram_tensor("kv_dram", [NODES, 2 * D], F32, kind="Internal").ap()
    dst_f = nc.dram_tensor("dst_f", [1, PADDED], F32, kind="Internal").ap()
    src_f = nc.dram_tensor("src_f", [1, PADDED], F32, kind="Internal").ap()

    def node_rows(t, step):
        return t[bass.ds(step.n * P, rows(step)), :]

    def windows(t, shift):
        return bass.AP(tensor=t.tensor, offset=shift, ap=[[EPC, CHUNKS], [1, P]])

    def window_on_all(t, step):
        return t[0:1, bass.ds(step.n * EPC, P)].to_broadcast([P, P])

    def row_on_all(t):
        return t.rearrange("(a n) -> a n", a=1).to_broadcast([P, t.shape[0]])

    top = ExitStack()
    with top:
        def tensors(ctx, stage):
            def sb(name, shape, dt=F32):
                return ctx.enter_context(nc.sbuf_tensor(f"{stage}_{name}", shape, dt))
            return sb

        stage_sems = []

        def sem(name):
            stage_sems.append(nc.alloc_semaphore(f"{name}_{nc.next_id()}"))
            return stage_sems[-1]

        def sems(name, n):
            return [sem(f"{name}{i}") for i in range(n)]

        sb = tensors(top, "kept")
        bank = [top.enter_context(nc.psum_tensor(f"bank{i}", [P, D], F32)) for i in range(8)]

        identity = sb("identity", [P, P])
        ones = sb("ones", [P, P])
        split = {}
        for name in ("conv", "q", "k", "v", "o"):
            split[name] = (sb(f"w_{name}_hi", [P, KC, D], F32R), sb(f"w_{name}_lo", [P, KC, D], F32R))
        norm1_mul = sb("norm1_mul", [P, D])
        norm1_add = sb("norm1_add", [P, D])
        zeros = sb("zeros", [P, D])
        y_sum = sb("y_sum", [P, D])
        y_sq_sum = sb("y_sq_sum", [P, D])
        all_zero = zeros[:, :].rearrange("p (i n) -> p i n", i=1).to_broadcast([P, TILES, D])
        favor_out = sb("favor_out", [32, D])
        dst_col = sb("dst_col", [P, CHUNKS])
        edge_index = sb("edge_index", [P, CHUNKS, 4], I32)

        def next_stage():
            nc.clear_and_free_semaphores(stage_sems)
            nc.all_engine_barrier()
            stage_sems.clear()

        with ExitStack() as ctx:
            sb = tensors(ctx, "setup")
            stage = [sb(f"stage{i}", [P, KC, D]) for i in range(2)]
            e_int = [sb(f"e_int{i}", [100, E // 100], I32) for i in range(2)]
            e_flt = [sb(f"e_flt{i}", [100, E // 100]) for i in range(2)]
            pads = sb("pads", [1, P])
            win = [sb(f"win{i}", [CHUNKS, P]) for i in range(3)]
            win_back = [sb(f"win_back{i}", [CHUNKS, P]) for i in range(2)]
            apart = sb("apart", [CHUNKS, P + 1])
            cols = [sb(f"cols{i}", [P, CHUNKS]) for i in range(4)]
            not_last = sb("not_last", [P, CHUNKS])
            below = sb("below", [P, CHUNKS])
            back_f = sb("back_f", [P, CHUNKS])
            index_f = sb("index_f", [P, CHUNKS, 4])
            weights = [("conv", w_conv), ("q", wqT), ("k", wkvT[:, 0:D]), ("v", wkvT[:, D:2 * D]), ("o", woT)]
            weight_loaded, apart_ready, apart_stored = sems("weight_loaded", 2), sem("apart_ready"), sem("apart_stored")
            edges_loaded, padded, windowed = sem("edges_loaded"), sem("padded"), sem("windowed")
            ident_ready, pad_ready, reversed_ready = sem("ident_ready"), sem("pad_ready"), sem("reversed_ready")
            edges_float, hi_ready, lo_ready = sem("edges_float"), sem("hi_ready"), sem("lo_ready")
            win_turned, cols_ready, table_step = sem("win_turned"), sem("cols_ready"), sem("table_step")

            with nc.Block() as block:
                @block.sync
                def _(sp):
                    for i, t in enumerate((dst, src)):
                        sp.dma_start(e_int[i][:, :], t.rearrange("(a n) -> a n", a=100)).then_inc(edges_loaded, 16)
                    for n, (name, w) in enumerate(weights):
                        if n >= 2:
                            sp.wait_ge(lo_ready, n - 1)
                        sp.dma_start(stage[n % 2][:, :, :], w.rearrange("(k p) n -> p k n", p=P)).then_inc(weight_loaded[n % 2], 16)
                        if n == 1:
                            sp.wait_ge(edges_float, 2)
                            sp.wait_ge(pad_ready, 3)
                            for i, t in enumerate((dst_f, src_f)):
                                sp.dma_start(t[0:1, 1:E + 1].rearrange("a (p n) -> (a p) n", p=100), e_flt[i][:, :]).then_inc(padded, 16)
                                sp.dma_start(t[0:1, 0:1], pads[0:1, 0:1]).then_inc(padded, 16)
                                sp.dma_start(t[0:1, E + 1:PADDED], pads[0:1, 1:PADDED - E]).then_inc(padded, 16)
                            sp.wait_ge(padded, 96)
                            for i, (t, shift) in enumerate(((dst_f, 0), (dst_f, 1), (src_f, 0))):
                                sp.dma_start(win[i][:, :], windows(t, shift)).then_inc(windowed, 16)
                    sp.wait_ge(apart_ready, 3)
                    sp.dma_start(apart_dram, apart[:, :]).then_inc(apart_stored, 16)
                    sp.wait_ge(apart_stored, 16)

                @block.gpsimd
                def _(pool):
                    pool.memset(zeros[:, :], 0.0).then_inc(ident_ready, 1)
                    pool.memset(ones[:, :], 1.0).then_inc(pad_ready, 1)
                    pool.memset(pads[:, :], -2.0).then_inc(pad_ready, 1)
                    pool.wait_ge(pad_ready, 2)
                    pool.memset(pads[0:1, 0:1], -1.0).then_inc(pad_ready, 1)
                    pool.memset(identity[:, :], 0.0).then_inc(ident_ready, 1)
                    pool.wait_ge(ident_ready, 2)
                    pool.affine_select(out=identity[:, :], in_=identity[:, :], compare_op=ALU.not_equal, fill=1.0,
                                       base=0, pattern=[[-1, P]], channel_multiplier=1).then_inc(ident_ready, 1)

                @block.scalar
                def _(act):
                    for n, (name, _) in enumerate(weights):
                        act.wait_ge(weight_loaded[n % 2], 16 * (n // 2 + 1))
                        act.activation(split[name][0][:, :, :], stage[n % 2][:, :, :], ACT.Copy).then_inc(hi_ready, 1)

                @block.vector
                def _(dve):
                    dve.wait_ge(edges_loaded, 32)
                    for i in range(2):
                        dve.tensor_copy(e_flt[i][:, :], e_int[i][:, :]).then_inc(edges_float, 1)
                    for n, (name, _) in enumerate(weights):
                        hi, lo = split[name]
                        dve.wait_ge(hi_ready, n + 1)
                        dve.tensor_tensor(lo[:, :, :], stage[n % 2][:, :, :], hi[:, :, :].bitcast(F32), ALU.subtract).then_inc(lo_ready, 1)
                    dve.wait_ge(windowed, 48)
                    for i in range(2):
                        dve.tensor_copy(win_back[i][:, :], win[i][:, ::-1]).then_inc(reversed_ready, 1)
                    dve.memset(apart[:, 0:1], 0.0).then_inc(apart_ready, 1)
                    dve.tensor_tensor(apart[:, 1:P + 1], win[0][:, :], win[1][:, :], ALU.not_equal).then_inc(apart_ready, 1)
                    dve.wait_ge(apart_ready, 2)
                    dve.tensor_scalar(apart[:, 1:P + 1], apart[:, 1:P + 1], -FAR, None, ALU.mult).then_inc(apart_ready, 1)
                    dve.wait_ge(win_turned, 1)
                    for i in range(4):
                        dve.tensor_copy(cols[i][:, :], bank[i][:, 0:CHUNKS]).then_inc(cols_ready, 1)
                    dve.wait_ge(cols_ready, 4)
                    dcol, dback, dnext, scol = cols
                    dve.tensor_copy(dst_col[:, :], dcol[:, :]).then_inc(table_step, 1)
                    dve.tensor_tensor(not_last[:, :], dback[:, :], dnext[:, :], ALU.is_equal).then_inc(table_step, 1)
                    dve.tensor_scalar(below[:, :], dcol[:, :], 0.0, BIG, ALU.is_lt, ALU.mult).then_inc(table_step, 1)
                    dve.wait_ge(table_step, 3)
                    dve.tensor_tensor(index_f[:, :, 1], dcol[:, :], below[:, :], ALU.add).then_inc(table_step, 1)
                    dve.memset(index_f[:, :, 3], 0.0).then_inc(table_step, 1)
                    dve.wait_ge(table_step, 5)
                    dve.tensor_scalar(below[:, :], scol[:, :], 0.0, BIG, ALU.is_lt, ALU.mult).then_inc(table_step, 1)
                    dve.wait_ge(table_step, 6)
                    dve.tensor_tensor(index_f[:, :, 0], scol[:, :], below[:, :], ALU.add).then_inc(table_step, 1)
                    dve.wait_ge(table_step, 7)
                    dve.tensor_scalar(below[:, :], dback[:, :], 0.0, BIG, ALU.is_lt, ALU.mult).then_inc(table_step, 1)
                    dve.scalar_tensor_tensor(back_f[:, :], not_last[:, :], BIG, dback[:, :], ALU.mult, ALU.add).then_inc(table_step, 1)
                    dve.wait_ge(table_step, 9)
                    dve.tensor_tensor(index_f[:, :, 2], back_f[:, :], below[:, :], ALU.add).then_inc(table_step, 1)
                    dve.memset(index_f[0:1, :, 0:2], BIG).then_inc(table_step, 1)
                    dve.wait_ge(table_step, 11)
                    dve.tensor_copy(edge_index[:, :, :], index_f[:, :, :]).then_inc(table_step, 1)

                @block.tensor
                def _(pe):
                    pe.wait_ge(ident_ready, 3)
                    pe.wait_ge(windowed, 48)
                    pe.wait_ge(reversed_ready, 2)
                    turned = (win[0][:, :], win_back[0][:, :], win_back[1][:, :], win[2][:, :])
                    for i in range(4):
                        m = pe.transpose(bank[i][:, 0:CHUNKS], turned[i], identity[0:CHUNKS, 0:CHUNKS])
                    m.then_inc(win_turned, 1)

        with ExitStack() as ctx:
            sb = tensors(ctx, "stats")
            RING = 3
            xs = [sb(f"xs{i}", [P, D]) for i in range(RING)]
            xsq = [sb(f"xsq{i}", [P, D]) for i in range(RING)]
            x_sum = sb("x_sum", [P, D])
            mean, var, tmp = sb("mean", [P, D]), sb("var", [P, D]), sb("tmp", [P, D])
            gain, shift = sb("gain", [P, D]), sb("shift", [P, D])
            loaded, consts = sems("s_x_loaded", RING), sem("s_consts")
            summed, squared, sq_summed = sem("s_summed"), sem("s_squared"), sem("s_sq_summed")
            sum_cleared, totals, affine = sem("s_sum_cleared"), sem("s_totals"), sem("s_affine")
            root = sem("s_root")
            with nc.Block() as block:
                @block.sync
                def _(sp):
                    sp.dma_start(gain[:, :], row_on_all(g1)).then_inc(consts, 16)
                    sp.dma_start(shift[:, :], row_on_all(b1)).then_inc(consts, 16)

                    def load(s):
                        if s.reaches(RING):
                            sp.wait_ge(summed, s.n - RING + 1)
                            sp.wait_ge(squared, s.n - RING + 1)
                        sp.dma_start(xs[s.slot][0:rows(s), :], node_rows(x, s)).then_inc(loaded[s.slot], 16)
                    steps(sp, TILES, RING, load)

                @block.vector
                def _(dve):
                    dve.memset(x_sum[:, :], 0.0).then_inc(sum_cleared, 1)
                    dve.wait_ge(sum_cleared, 1)

                    def add(s):
                        r = rows(s)
                        dve.wait_ge(loaded[s.slot], landed(s, loaded))
                        if s.reaches(1):
                            dve.wait_ge(summed, s.n)
                        dve.tensor_tensor(x_sum[0:r, :], x_sum[0:r, :], xs[s.slot][0:r, :], ALU.add).then_inc(summed, 1)
                    steps(dve, TILES, RING, add)
                    dve.wait_ge(totals, 1)
                    dve.tensor_scalar(mean[:, :], bank[0][:, :], 1.0 / N, None, ALU.mult).then_inc(affine, 1)
                    dve.tensor_scalar(var[:, :], bank[1][:, :], 1.0 / N, EPS, ALU.mult, ALU.add).then_inc(affine, 1)
                    dve.wait_ge(affine, 2)
                    dve.tensor_tensor(tmp[:, :], mean[:, :], mean[:, :], ALU.mult).then_inc(affine, 1)
                    dve.wait_ge(affine, 3)
                    dve.tensor_tensor(var[:, :], var[:, :], tmp[:, :], ALU.subtract).then_inc(affine, 1)
                    dve.wait_ge(root, 1)
                    dve.reciprocal(tmp[:, :], var[:, :]).then_inc(affine, 1)
                    dve.wait_ge(affine, 5)
                    dve.wait_ge(consts, 32)
                    dve.tensor_tensor(norm1_mul[:, :], tmp[:, :], gain[:, :], ALU.mult).then_inc(affine, 1)
                    dve.wait_ge(affine, 6)
                    dve.tensor_tensor(tmp[:, :], mean[:, :], norm1_mul[:, :], ALU.mult).then_inc(affine, 1)
                    dve.wait_ge(affine, 7)
                    dve.tensor_tensor(norm1_add[:, :], shift[:, :], tmp[:, :], ALU.subtract).then_inc(affine, 1)

                @block.scalar
                def _(act):
                    def square(s):
                        r = rows(s)
                        act.wait_ge(loaded[s.slot], landed(s, loaded))
                        if s.reaches(RING):
                            act.wait_ge(sq_summed, s.n - RING + 1)
                        act.activation(xsq[s.slot][0:r, :], xs[s.slot][0:r, :], ACT.Square).then_inc(squared, 1)
                    steps(act, TILES, RING, square)
                    act.wait_ge(affine, 4)
                    act.activation(var[:, :], var[:, :], ACT.Sqrt).then_inc(root, 1)

                @block.tensor
                def _(pe):
                    def total_squares(s):
                        r = rows(s)
                        pe.wait_ge(squared, s.n + 1)
                        first = isinstance(s.n, int) and s.n == 0
                        last = isinstance(s.n, int) and s.n == TILES - 1
                        pe.matmul(bank[1][:, :], ones[0:r, :], xsq[s.slot][0:r, :], start=first, stop=last).then_inc(sq_summed, 1)
                    steps(pe, TILES, RING, total_squares)
                    pe.wait_ge(summed, TILES)
                    pe.matmul(bank[0][:, :], ones[:, :], x_sum[:, :], start=True, stop=True).then_inc(totals, 1)

        with ExitStack() as ctx:
            sb = tensors(ctx, "favor")
            R = 32
            h = sb("h", [R, D])
            hT = sb("hT", [P, KC, R])
            fw = {n: sb(f"fw_{n}", [P, KC, D]) for n in "qkvo"}
            pT = sb("pT", [P, NF])
            rowform = {n: sb(f"row_{n}", [R, D]) for n in "qk"}
            colform = {n: sb(f"col_{n}", [P, KC, R]) for n in "qk"}
            v_one = sb("v_one", [R, HEADS, DH + 1])
            sq = {n: sb(f"sq_{n}", [R, D]) for n in "qk"}
            diag = {n: sb(f"diag_{n}", [R, HEADS]) for n in "qk"}
            peak = {n: sb(f"peak_{n}", [R, HEADS]) for n in "qk"}
            peak_all = sb("peak_all", [R, HEADS])
            bias = {n: sb(f"bias_{n}", [R, HEADS]) for n in "qk"}
            feat = {n: sb(f"feat_{n}", [R, HEADS, NF]) for n in "qk"}
            featT = sb("featT", [P, 2 * HEADS, R])
            kv = sb("kv", [P, 2 * HEADS, DH + 1])
            den = sb("den", [R, HEADS])
            inv = sb("inv", [R, HEADS])
            av = sb("av", [R, D])
            avT = sb("avT", [P, KC, R])
            avD = sb("avD", [P, KC, R])
            f_loaded, f_turned, f_hT, f_proj, f_colp = (sem(n) for n in ("f_loaded", "f_turned", "f_hT", "f_proj", "f_colp"))
            f_vec, f_u, f_peak, f_exp, f_featT = (sem(n) for n in ("f_vec", "f_u", "f_peak", "f_exp", "f_featT"))
            f_kv, f_kvs, f_attn, f_avT, f_out = (sem(n) for n in ("f_kv", "f_kvs", "f_attn", "f_avT", "f_out"))
            f_copied, f_one, f_zeroed = sem("f_copied"), sem("f_one"), sem("f_zeroed")
            TEMPER = float(DH) ** -0.25

            def features(b, hd):
                return bank[4 * b + 2 * (hd % 2) + hd // 4][0:R, (hd // 2 % 2) * NF:(hd // 2 % 2 + 1) * NF]

            with nc.Block() as block:
                @block.sync
                def _(sp):
                    sp.dma_start(h[:, :], x[0:R, :]).then_inc(f_loaded, 16)
                    for n, w in zip("qkvo", (fq, fk, fv, fo)):
                        sp.dma_start(fw[n][:, :, :], w.rearrange("(k p) n -> p k n", p=P)).then_inc(f_loaded, 16)
                    for half in range(2):
                        sp.dma_start(pT[half * DH:(half + 1) * DH, :], projT).then_inc(f_loaded, 16)
                    sp.dma_start(aggregated.rearrange("(i p) n -> p i n", p=P), all_zero).then_inc(f_zeroed, 16)
                    sp.wait_ge(f_zeroed, 16)

                @block.tensor
                def _(pe):
                    pe.wait_ge(f_loaded, 7 * 16)
                    for k in range(KC):
                        m = pe.transpose(bank[0][:, k * R:(k + 1) * R], h[:, k * P:(k + 1) * P], identity[0:R, 0:R])
                    m.then_inc(f_turned, 1)
                    pe.wait_ge(f_hT, 1)
                    for b, n in enumerate("qkv"):
                        for k in range(KC):
                            m = pe.matmul(bank[1 + b][0:R, :], hT[:, k, :], fw[n][:, k, :], start=k == 0, stop=k == KC - 1)
                    m.then_inc(f_proj, 1)
                    for b, n in enumerate("qk"):
                        for c in range(KC):
                            for k in range(KC):
                                m = pe.matmul(bank[4 + b][:, c * R:(c + 1) * R], fw[n][:, k, c * P:(c + 1) * P], hT[:, k, :], start=k == 0, stop=k == KC - 1)
                    m.then_inc(f_colp, 1)
                    pe.wait_ge(f_copied, 5)
                    for b, n in enumerate("qk"):
                        for hd in range(HEADS):
                            o = (hd % 2) * DH
                            m = pe.matmul(features(b, hd), 
                                          colform[n][o:o + DH, hd // 2, :], pT[o:o + DH, :], start=True, stop=True)
                        m.then_inc(f_u, 1)
                    pe.wait_ge(f_exp, 6)
                    for hd in range(HEADS):
                        for half in range(2):
                            i = 2 * hd + half
                            m = pe.transpose(bank[0][:, i * R:(i + 1) * R], feat["q"][:, hd, half * P:(half + 1) * P], identity[0:R, 0:R])
                    m.then_inc(f_featT, 1)
                    for hd in range(HEADS):
                        for half in range(2):
                            i = 2 * hd + half
                            m = pe.matmul(bank[1 + i // 4][:, (i % 4) * (DH + 1):(i % 4 + 1) * (DH + 1)],
                                          feat["k"][:, hd, half * P:(half + 1) * P], v_one[:, hd, :], start=True, stop=True)
                    m.then_inc(f_kv, 1)
                    pe.wait_ge(f_kvs, 5)
                    for hd in range(HEADS):
                        for half in range(2):
                            i = 2 * hd + half
                            m = pe.matmul(bank[5 + hd // 4][0:R, (hd % 4) * (DH + 1):(hd % 4 + 1) * (DH + 1)],
                                          featT[:, i, :], kv[:, i, :], start=half == 0, stop=half == 1)
                    m.then_inc(f_attn, 1)
                    pe.wait_ge(f_vec, 8)
                    for k in range(KC):
                        m = pe.transpose(bank[7][:, k * R:(k + 1) * R], av[:, k * P:(k + 1) * P], identity[0:R, 0:R])
                    m.then_inc(f_avT, 1)
                    pe.wait_ge(f_vec, 13)
                    for k in range(KC):
                        m = pe.matmul(bank[0][0:R, :], avD[:, k, :], fw["o"][:, k, :], start=k == 0, stop=k == KC - 1)
                    m.then_inc(f_out, 1)

                @block.scalar
                def _(act):
                    for i, n in enumerate("qk"):
                        act.wait_ge(f_peak, i + 1)
                        for hd in range(HEADS):
                            m = act.activation(feat[n][:, hd, :], features(i, hd), ACT.Exp, bias=bias[n][:, hd:hd + 1])
                        m.then_inc(f_exp, 1)

                @block.gpsimd
                def _(pool):
                    pool.memset(v_one[:, :, DH:DH + 1], 1.0).then_inc(f_one, 1)
                    pool.wait_ge(f_vec, 5)
                    pool.partition_all_reduce(peak_all[:, :], peak["k"][:, :], R, RMAX).then_inc(f_one, 1)

                @block.vector
                def _(dve):
                    dve.wait_ge(f_turned, 1)
                    dve.tensor_copy(hT[:, :, :], bank[0][:, 0:KC * R].rearrange("p (k r) -> p k r", k=KC)).then_inc(f_hT, 1)
                    dve.wait_ge(f_proj, 1)
                    for b, n in enumerate("qk"):
                        dve.tensor_scalar(rowform[n][:, :], bank[1 + b][0:R, :], TEMPER, None, ALU.mult).then_inc(f_copied, 1)
                    dve.tensor_copy(v_one[:, :, 0:DH], bank[3][0:R, :].rearrange("p (h d) -> p h d", h=HEADS)).then_inc(f_copied, 1)
                    dve.wait_ge(f_colp, 1)
                    for b, n in enumerate("qk"):
                        dve.tensor_scalar(colform[n][:, :, :], bank[4 + b][:, 0:KC * R].rearrange("p (k r) -> p k r", k=KC), TEMPER, None, ALU.mult).then_inc(f_copied, 1)
                    dve.wait_ge(f_copied, 2)
                    for n in "qk":
                        dve.tensor_tensor(sq[n][:, :], rowform[n][:, :], rowform[n][:, :], ALU.mult).then_inc(f_vec, 1)
                    dve.wait_ge(f_vec, 2)
                    for n in "qk":
                        dve.tensor_reduce(diag[n][:, :], sq[n][:, :].rearrange("p (h d) -> p h d", h=HEADS), AX.X, ALU.add).then_inc(f_vec, 1)
                    dve.wait_ge(f_u, 2)
                    for i, n in ((1, "k"), (0, "q")):
                        for b in range(4):
                            first = 4 * (b % 2) + b // 2
                            m = dve.tensor_reduce(peak[n][:, first:first + 3:2], bank[4 * i + b][0:R, :].rearrange("p (h m) -> p h m", h=2), AX.X, ALU.max)
                        m.then_inc(f_vec, 1)
                    dve.wait_ge(f_vec, 6)
                    dve.scalar_tensor_tensor(bias["q"][:, :], diag["q"][:, :], -0.5, peak["q"][:, :], ALU.mult, ALU.subtract).then_inc(f_peak, 1)
                    dve.wait_ge(f_one, 2)
                    dve.scalar_tensor_tensor(bias["k"][:, :], diag["k"][:, :], -0.5, peak_all[:, :], ALU.mult, ALU.subtract).then_inc(f_peak, 1)
                    dve.wait_ge(f_exp, 2)
                    for n in "qk":
                        f = feat[n][:, :, :]
                        for half in range(2):
                            fh = feat[n][:, half * 4:half * 4 + 4, :]
                            dve.tensor_scalar(fh, fh, float(1.0 / np.sqrt(NF)), KEPS, ALU.mult, ALU.add).then_inc(f_exp, 1)
                    dve.wait_ge(f_featT, 1)
                    dve.tensor_copy(featT[:, :, :], bank[0][:, :].rearrange("p (i r) -> p i r", r=R)).then_inc(f_kvs, 1)
                    dve.wait_ge(f_kv, 1)
                    for b in range(4):
                        dve.tensor_copy(kv[:, 4 * b:4 * b + 4, :], bank[1 + b][:, 0:4 * (DH + 1)].rearrange("p (i d) -> p i d", i=4)).then_inc(f_kvs, 1)
                    dve.wait_ge(f_attn, 1)
                    for b in range(2):
                        m = dve.tensor_scalar(den[:, 4 * b:4 * b + 4], bank[5 + b][0:R, 0:4 * (DH + 1)].rearrange("p (i d) -> p i d", i=4)[:, :, DH], KEPS, None, ALU.add)
                    m.then_inc(f_vec, 1)
                    dve.wait_ge(f_vec, 7)
                    dve.reciprocal(inv[:, :], den[:, :]).then_inc(f_one, 1)
                    dve.wait_ge(f_one, 3)
                    for b in range(2):
                        m = dve.tensor_tensor(av[:, b * 4 * DH:(b + 1) * 4 * DH].rearrange("p (i d) -> p i d", i=4),
                                              bank[5 + b][0:R, 0:4 * (DH + 1)].rearrange("p (i d) -> p i d", i=4)[:, :, 0:DH],
                                              inv[:, 4 * b:4 * b + 4].rearrange("p (i d) -> p i d", d=1).to_broadcast([R, 4, DH]), ALU.mult)
                    m.then_inc(f_vec, 1)
                    dve.wait_ge(f_avT, 1)
                    dve.tensor_copy(avT[:, :, :], bank[7][:, 0:KC * R].rearrange("p (k r) -> p k r", k=KC)).then_inc(f_vec, 1)
                    dve.wait_ge(f_vec, 9)
                    for k in range(KC):
                        dve.tensor_scalar(avD[:, k, :], avT[:, k, :], avT[:, k, R - 1:R], None, ALU.subtract).then_inc(f_vec, 1)
                    dve.wait_ge(f_out, 1)
                    dve.tensor_copy(favor_out[:, :], bank[0][0:R, :]).then_inc(f_vec, 1)

        next_stage()
        with ExitStack() as ctx:
            sb = tensors(ctx, "gather")
            RING, AHEAD = 6, 4
            window = [sb(f"window{i}", [P, P]) for i in range(RING)]
            same = [sb(f"same{i}", [P, P]) for i in range(RING)]
            idx = [sb(f"idx{i}", [P, 4], I32) for i in range(RING)]
            xg = [sb(f"xg{i}", [P, D]) for i in range(RING)]
            count = [sb(f"count{i}", [P, 1]) for i in range(RING)]
            inv_count = [sb(f"inv_count{i}", [P, 1]) for i in range(RING)]
            mean_mul = [sb(f"mean_mul{i}", [P, D]) for i in range(3)]
            mean_row = [sb(f"mean_row{i}", [P, D]) for i in range(RING)]
            window_loaded, gathered, scattered = sems("window_loaded", RING), sems("gathered", RING), sems("scattered", RING)
            cleared, indexed, same_ready, passed = sem("cleared"), sem("indexed"), sem("same_ready"), sem("passed")
            carried, summed = sem("carried"), sem("summed")
            inverted, scaled, mean_ready = sem("inverted"), sem("scaled"), sem("mean_ready")
            sums = [bank[i] for i in range(3)]
            counts = [bank[3 + i][:, 0:1] for i in range(3)]
            with nc.Block() as block:
                @block.sync
                def _(sp):
                    def load(s):
                        wait_before(sp, same_ready, s, RING)
                        sp.dma_start(window[s.slot][:, :], window_on_all(dst_f, s)).then_inc(window_loaded[s.slot], 16)
                    steps(sp, CHUNKS, RING, load)

                @block.gpsimd
                def _(pool):
                    limit = pool.to_reg(N - 1)

                    def gather(s):
                        wait_landed_before(pool, scattered, s)
                        pool.tensor_copy(idx[s.slot][:, :], edge_index[:, bass.ds(s.n, 1), :].rearrange("p a b -> p (a b)")).then_inc(indexed, 1)
                        wait_before(pool, summed, s, RING)
                        wait_alone(pool, indexed, s.n + 1, passed)
                        pool.indirect_dma_start(out=xg[s.slot][:, :], out_offset=None, in_=x,
                                                in_offset=bass.IndirectOffsetOnAxis(ap=idx[s.slot][:, 0:1], axis=0),
                                                bounds_check=limit, oob_is_err=False).then_inc(gathered[s.slot], 16)

                    def scatter(s):
                        if s.reaches(1):
                            wait_landed(pool, scattered, s.before())
                        wait_alone(pool, mean_ready, s.n + 1, passed)
                        pool.indirect_dma_start(out=aggregated, out_offset=bass.IndirectOffsetOnAxis(ap=idx[s.slot][:, 2:3], axis=0),
                                                in_=mean_row[s.slot][:, :], in_offset=None,
                                                bounds_check=limit, oob_is_err=False).then_inc(scattered[s.slot], 16)

                    for i in range(RING):
                        pool.memset(xg[i][:, :], 0.0).then_inc(cleared, 1)
                        pool.memset(count[i][:, :], 1.0).then_inc(cleared, 1)
                    pool.wait_ge(cleared, 2 * RING)
                    for n in range(AHEAD):
                        gather(Step(RING, 0, n))

                    def turn(s):
                        if s.ahead(AHEAD).within(CHUNKS):
                            gather(s.ahead(AHEAD))
                        scatter(s)
                    steps(pool, CHUNKS, RING, turn, peel_last=AHEAD)
                    wait_all(pool, scattered, CHUNKS, RING)

                @block.vector
                def _(dve):
                    def compare(s):
                        u = s.slot
                        wait_landed(dve, window_loaded, s)
                        wait_before(dve, summed, s, RING)
                        dve.tensor_scalar(same[u][:, :], window[u][:, ::-1], dst_col[:, bass.ds(s.n, 1)], None, ALU.is_equal).then_inc(same_ready, 1)

                    def normalize(s):
                        u = s.slot
                        if isinstance(s.n, int) and s.n == CHUNKS - 1:
                            dve.wait_ge(summed, s.n + 1)
                        else:
                            dve.wait_ge(carried, s.n + 1)
                        dve.reciprocal(inv_count[u][:, :], at(counts, s)).then_inc(inverted, 1)
                        dve.wait_ge(inverted, s.n + 1)
                        dve.scalar_tensor_tensor(at(mean_mul, s)[:, :], at(sums, s)[:, :], inv_count[u][:, 0:1], norm1_mul[:, :], ALU.mult, ALU.mult).then_inc(scaled, 1)
                        dve.wait_ge(scaled, s.n + 1)
                        wait_landed_before(dve, scattered, s)
                        dve.tensor_tensor(mean_row[u][:, :], at(mean_mul, s)[:, :], norm1_add[:, :], ALU.add).then_inc(mean_ready, 1)

                    compare(Step(RING, 0, 0))
                    compare(Step(RING, 0, 1))

                    def turn(s):
                        if s.ahead(2).within(CHUNKS):
                            compare(s.ahead(2))
                        normalize(s)
                    steps(dve, CHUNKS, RING, turn, peel_last=2)

                @block.tensor
                def _(pe):
                    def total(s):
                        u = s.slot
                        pe.wait_ge(same_ready, s.n + 1)
                        wait_landed(pe, gathered, s)
                        wait_before(pe, scaled, s, 3)
                        if s.reaches(1):
                            pe.wait_ge(carried, s.n)
                        else:
                            pe.wait_ge(cleared, 2 * RING)
                        pe.matmul(at(counts, s), same[u][:, :], count[u][:, :], start=True, stop=True)
                        pe.matmul(at(sums, s)[:, :], same[u][:, :], xg[u][:, :], start=True, stop=True).then_inc(summed, 1)
                    steps(pe, CHUNKS, RING, total)

                @block.scalar
                def _(act):
                    act.wait_ge(cleared, 2 * RING)

                    def carry(s):
                        to = s.ahead(1)
                        wait_landed(act, gathered, to)
                        act.wait_ge(summed, s.n + 1)
                        act.activation(count[to.slot][0:1, :], at(counts, s)[0:1, :], ACT.Copy)
                        act.activation(xg[to.slot][0:1, :], at(sums, s)[0:1, :], ACT.Copy).then_inc(carried, 1)
                    steps(act, CHUNKS - 1, RING, carry)

        def turn_tile(pe, psum, tile, r):
            for k in range(KC):
                m = pe.transpose(psum[:, k * P:k * P + r], tile[0:r, k * P:(k + 1) * P], identity[0:r, 0:r])
            return m

        def product(pe, psum, hi, lo, name, r):
            wh, wl = split[name]
            passes = [(hi, wh), (hi, wl), (lo, wh)]
            for i, (a, w) in enumerate(passes):
                for k in range(KC):
                    m = pe.matmul(psum[0:r, :], a[:, k * P:k * P + r], w[:, k, :],
                                  start=i == 0 and k == 0, stop=i == 2 and k == KC - 1)
            return m

        def blocks_of(t, r):
            return t[:, :].rearrange("p (k n) -> p k n", k=KC)[:, :, 0:r]

        next_stage()
        with ExitStack() as ctx:
            sb = tensors(ctx, "conv")
            RING = 4
            ag = [sb(f"ag{i}", [P, D]) for i in range(4)]
            xb = [sb(f"xb{i}", [P, D]) for i in range(4)]
            hi = [sb(f"hi{i}", [P, D], F32R) for i in range(2)]
            lo = [sb(f"lo{i}", [P, D], F32R) for i in range(2)]
            pre = [sb(f"pre{i}", [P, D]) for i in range(2)]
            y = [sb(f"y{i}", [P, D]) for i in range(4)]
            ysq = [sb(f"ysq{i}", [P, D]) for i in range(4)]
            bias_c = sb("bias_c", [P, D])
            ag_loaded, x_loaded, y_stored, consts = sems("ag_loaded", 4), sems("x_loaded", 4), sems("y_stored", 4), sem("consts")
            turned, hi_ready, lo_ready, made = sem("turned"), sem("hi_ready"), sem("lo_ready"), sem("made")
            biased, y_ready, squared, summed, sq_summed = sem("biased"), sem("y_ready"), sem("squared"), sem("summed"), sem("sq_summed")
            cleared, sq_cleared, favored = sem("cleared"), sem("sq_cleared"), sem("favored")
            tpose, acc = [bank[0], bank[1]], [bank[2], bank[3]]
            with nc.Block() as block:
                @block.sync
                def _(sp):
                    sp.dma_start(bias_c[:, :], row_on_all(b_conv)).then_inc(consts, 16)

                    def load(s):
                        r = rows(s)
                        wait_before(sp, turned, s, 4)
                        sp.dma_start(at(ag, s)[0:r, :], node_rows(aggregated, s)).then_inc(at(ag_loaded, s), 16)
                        wait_before(sp, y_ready, s, 4)
                        sp.dma_start(at(xb, s)[0:r, :], node_rows(x, s)).then_inc(at(x_loaded, s), 16)
                    steps(sp, TILES, RING, load)

                @block.tensor
                def _(pe):
                    def turn(s):
                        wait_landed(pe, ag_loaded, s)
                        wait_before(pe, lo_ready, s, 2)
                        turn_tile(pe, at(tpose, s), at(ag, s), rows(s)).then_inc(turned, 1)

                    def multiply(s):
                        pe.wait_ge(lo_ready, s.n + 1)
                        wait_before(pe, biased, s, 2)
                        product(pe, at(acc, s), at(hi, s), at(lo, s), "conv", rows(s)).then_inc(made, 1)

                    turn(Step(RING, 0, 0))

                    def both(s):
                        if s.ahead(1).within(TILES):
                            turn(s.ahead(1))
                        multiply(s)
                    steps(pe, TILES, RING, both, peel_last=2)

                @block.scalar
                def _(act):
                    def copy_hi(s):
                        r = rows(s)
                        act.wait_ge(turned, s.n + 1)
                        wait_before(act, made, s, 2)
                        act.activation(blocks_of(at(hi, s), r), blocks_of(at(tpose, s), r), ACT.Copy).then_inc(hi_ready, 1)

                    def finish(s):
                        r = rows(s)
                        act.wait_ge(y_ready, s.n + 1)
                        act.dma_start(node_rows(y_dram, s), at(y, s)[0:r, :]).then_inc(at(y_stored, s), 16)
                        wait_before(act, sq_summed, s, 4)
                        act.activation(at(ysq, s)[0:r, :], at(y, s)[0:r, :], ACT.Square).then_inc(squared, 1)

                    copy_hi(Step(RING, 0, 0))

                    def both(s):
                        if s.ahead(1).within(TILES):
                            copy_hi(s.ahead(1))
                        finish(s)
                    steps(act, TILES, RING, both, peel_last=2)
                    wait_all(act, y_stored, TILES, RING)

                @block.vector
                def _(dve):
                    dve.memset(y_sum[:, :], 0.0).then_inc(cleared, 1)
                    dve.wait_ge(cleared, 1)
                    dve.wait_ge(consts, 16)

                    def take_lo(s):
                        r = rows(s)
                        dve.wait_ge(hi_ready, s.n + 1)
                        dve.tensor_tensor(blocks_of(at(lo, s), r), blocks_of(at(tpose, s), r), blocks_of(at(hi, s), r).bitcast(F32), ALU.subtract).then_inc(lo_ready, 1)

                    def finish(s):
                        r = rows(s)
                        yt, pt, xt = at(y, s), at(pre, s), at(xb, s)
                        dve.wait_ge(made, s.n + 1)
                        dve.tensor_tensor(pt[0:r, :], at(acc, s)[0:r, :], bias_c[0:r, :], ALU.add).then_inc(biased, 1)
                        wait_landed(dve, x_loaded, s)
                        wait_landed_before(dve, y_stored, s)
                        wait_before(dve, squared, s, 4)
                        dve.wait_ge(biased, s.n + 1)
                        if isinstance(s.n, int) and s.n == 0:
                            dve.scalar_tensor_tensor(yt[0:r, :], pt[0:r, :], 0.0, xt[0:r, :], ALU.max, ALU.add).then_inc(favored, 1)
                            dve.wait_ge(favored, 1)
                            dve.tensor_tensor(yt[0:32, :], yt[0:32, :], favor_out[:, :], ALU.add).then_inc(y_ready, 1)
                        else:
                            dve.scalar_tensor_tensor(yt[0:r, :], pt[0:r, :], 0.0, xt[0:r, :], ALU.max, ALU.add).then_inc(y_ready, 1)
                        dve.wait_ge(y_ready, s.n + 1)
                        dve.tensor_tensor(y_sum[0:r, :], y_sum[0:r, :], yt[0:r, :], ALU.add).then_inc(summed, 1)

                    take_lo(Step(RING, 0, 0))

                    def both(s):
                        if s.ahead(1).within(TILES):
                            take_lo(s.ahead(1))
                        finish(s)
                    steps(dve, TILES, RING, both, peel_last=2)

                @block.gpsimd
                def _(pool):
                    pool.memset(y_sq_sum[:, :], 0.0).then_inc(sq_cleared, 1)
                    pool.wait_ge(sq_cleared, 1)

                    def add(s):
                        r = rows(s)
                        wait_before(pool, sq_summed, s, 1)
                        pool.wait_ge(squared, s.n + 1)
                        pool.tensor_tensor(y_sq_sum[0:r, :], y_sq_sum[0:r, :], at(ysq, s)[0:r, :], ALU.add).then_inc(sq_summed, 1)
                    steps(pool, TILES, RING, add)

        next_stage()
        with ExitStack() as ctx:
            sb = tensors(ctx, "qkv")
            RING = 4
            yb = [sb(f"yb{i}", [P, D]) for i in range(4)]
            xc = [sb(f"xc{i}", [P, D]) for i in range(4)]
            ym = [sb(f"ym{i}", [P, D]) for i in range(2)]
            z = [sb(f"z{i}", [P, D]) for i in range(2)]
            x1 = [sb(f"x1_{i}", [P, D]) for i in range(4)]
            stat = [sb(f"stat{i}", [P, 6]) for i in range(2)]
            mv = [sb(f"mv{i}", [P, 2]) for i in range(2)]
            rstd = [sb(f"rstd{i}", [P, 1]) for i in range(2)]
            veps = [sb(f"veps{i}", [P, 1]) for i in range(2)]
            nmr = [sb(f"nmr{i}", [P, 1]) for i in range(2)]
            minus_half = sb("minus_half", [P, 1])
            hi = [sb(f"hi{i}", [P, D], F32R) for i in range(2)]
            lo = [sb(f"lo{i}", [P, D], F32R) for i in range(2)]
            qo = [sb(f"qo{i}", [P, D]) for i in range(2)]
            kvo = [sb(f"kvo{i}", [P, 2 * D]) for i in range(2)]
            bias_q, bias_kv = sb("bias_q", [P, D]), sb("bias_kv", [P, 2 * D])
            mean, var, tmp = sb("mean", [P, D]), sb("var", [P, D]), sb("tmp", [P, D])
            gain, shift = sb("gain", [P, D]), sb("shift", [P, D])
            norm2_mul, norm2_add = sb("norm2_mul", [P, D]), sb("norm2_add", [P, D])
            y_loaded, x_loaded, consts = sems("y_loaded", 4), sems("x_loaded", 4), sem("consts")
            q_stored, kv_stored, x1_stored, zeroed = sems("q_stored", 2), sems("kv_stored", 2), sems("x1_stored", 4), sem("zeroed")
            totals, affine, root, x_shifted, y_scaled, z_ready = (sem(n) for n in ("totals", "affine", "root", "x_shifted", "y_scaled", "z_ready"))
            stat_ready, mv_ready, veps_ready, rstd_ready, nmr_ready, x1_ready = (sem(n) for n in ("stat_ready", "mv_ready", "veps_ready", "rstd_ready", "nmr_ready", "x1_ready"))
            turned, hi_ready, lo_ready, q_ready, kv_ready, half_ready, passed = (sem(n) for n in ("turned", "hi_ready", "lo_ready", "q_ready", "kv_ready", "half_ready", "passed"))
            q_made, k_made, v_made = sem("q_made"), sem("k_made"), sem("v_made")
            tpose = [bank[0], bank[1]]
            pq, pk, pv = [bank[2], bank[3]], [bank[4], bank[5]], [bank[6], bank[7]]
            with nc.Block() as block:
                @block.sync
                def _(sp):
                    for t, v in ((gain, g2), (shift, b2), (bias_q, bq), (bias_kv, bkv)):
                        sp.dma_start(t[:, :], row_on_all(v)).then_inc(consts, 16)

                    def load(s):
                        r = rows(s)
                        wait_before(sp, y_scaled, s, 4)
                        sp.dma_start(at(yb, s)[0:r, :], node_rows(y_dram, s)).then_inc(at(y_loaded, s), 16)
                        wait_before(sp, z_ready, s, 4)
                        sp.dma_start(at(xc, s)[0:r, :], node_rows(x, s)).then_inc(at(x_loaded, s), 16)

                    def store(s):
                        r = rows(s)
                        sp.wait_ge(x1_ready, s.n + 1)
                        sp.dma_start(node_rows(x1_dram, s), at(x1, s)[0:r, :]).then_inc(at(x1_stored, s), 16)
                        sp.dma_start(node_rows(attended, s), zeros[0:r, :]).then_inc(zeroed, 16)

                    for n in range(4):
                        load(Step(RING, 0, n))

                    def both(s):
                        store(s)
                        if s.ahead(4).within(TILES):
                            load(s.ahead(4))
                    steps(sp, TILES, RING, both, peel_last=5)
                    wait_all(sp, x1_stored, TILES, RING)
                    sp.wait_ge(zeroed, 16 * TILES)

                @block.gpsimd
                def _(pool):
                    pool.memset(minus_half[:, :], -0.5).then_inc(half_ready, 1)
                    pool.wait_ge(half_ready, 1)
                    pool.wait_ge(affine, 8)

                    def shift_x(s):
                        r = rows(s)
                        wait_landed(pool, x_loaded, s)
                        pool.tensor_tensor(at(xc, s)[0:r, :], at(xc, s)[0:r, :], norm2_add[0:r, :], ALU.add).then_inc(x_shifted, 1)

                    def inverse_root(s):
                        r = rows(s)
                        pool.wait_ge(veps_ready, s.n + 1)
                        pool.tensor_tensor(at(rstd, s)[0:r, :], at(veps, s)[0:r, :], minus_half[0:r, :], ALU.pow).then_inc(rstd_ready, 1)

                    first = [Step(RING, 0, n) for n in range(3)]
                    shift_x(first[0])
                    shift_x(first[1])
                    inverse_root(first[0])
                    inverse_root(first[1])
                    shift_x(first[2])

                    def both(s):
                        if s.ahead(3).within(TILES):
                            shift_x(s.ahead(3))
                        if s.ahead(2).within(TILES):
                            inverse_root(s.ahead(2))
                    steps(pool, TILES, RING, both, peel_last=4)

                @block.tensor
                def _(pe):
                    pe.matmul(bank[2][:, :], ones[:, :], y_sum[:, :], start=True, stop=True)
                    pe.matmul(bank[3][:, :], ones[:, :], y_sq_sum[:, :], start=True, stop=True).then_inc(totals, 1)

                    def turn(s):
                        pe.wait_ge(x1_ready, s.n + 1)
                        wait_before(pe, lo_ready, s, 2)
                        turn_tile(pe, at(tpose, s), at(x1, s), rows(s)).then_inc(turned, 1)

                    def multiply(s):
                        r = rows(s)
                        pe.wait_ge(lo_ready, s.n + 1)
                        wait_before(pe, kv_ready, s, 2)
                        product(pe, at(pq, s), at(hi, s), at(lo, s), "q", r).then_inc(q_made, 1)
                        product(pe, at(pk, s), at(hi, s), at(lo, s), "k", r).then_inc(k_made, 1)
                        product(pe, at(pv, s), at(hi, s), at(lo, s), "v", r).then_inc(v_made, 1)

                    pe.wait_ge(affine, 2)
                    turn(Step(RING, 0, 0))

                    def both(s):
                        if s.ahead(1).within(TILES):
                            turn(s.ahead(1))
                        multiply(s)
                    steps(pe, TILES, RING, both, peel_last=2)

                @block.scalar
                def _(act):
                    act.wait_ge(affine, 4)
                    act.activation(var[:, :], var[:, :], ACT.Sqrt).then_inc(root, 1)

                    def normalize(s):
                        r = rows(s)
                        wait_landed_before(act, x1_stored, s)
                        wait_before(act, turned, s, 4)
                        act.wait_ge(rstd_ready, s.n + 1)
                        act.wait_ge(nmr_ready, s.n + 1)
                        act.activation(at(x1, s)[0:r, :], at(z, s)[0:r, :], ACT.Identity, bias=at(nmr, s)[0:r, 0:1], scale=at(rstd, s)[0:r, 0:1]).then_inc(x1_ready, 1)

                    def copy_hi(s):
                        r = rows(s)
                        wait_before(act, v_made, s, 2)
                        act.wait_ge(turned, s.n + 1)
                        act.activation(blocks_of(at(hi, s), r), blocks_of(at(tpose, s), r), ACT.Copy).then_inc(hi_ready, 1)

                    def store(s):
                        r = rows(s)
                        act.wait_ge(q_ready, s.n + 1)
                        act.dma_start(node_rows(q_dram, s), at(qo, s)[0:r, :]).then_inc(at(q_stored, s), 16)
                        act.wait_ge(kv_ready, s.n + 1)
                        act.dma_start(node_rows(kv_dram, s), at(kvo, s)[0:r, :]).then_inc(at(kv_stored, s), 16)

                    normalize(Step(RING, 0, 0))
                    normalize(Step(RING, 0, 1))
                    copy_hi(Step(RING, 0, 0))

                    def all3(s):
                        if s.ahead(1).within(TILES):
                            copy_hi(s.ahead(1))
                        if s.ahead(2).within(TILES):
                            normalize(s.ahead(2))
                        store(s)
                    steps(act, TILES, RING, all3, peel_last=3)
                    wait_all(act, q_stored, TILES, RING)
                    wait_all(act, kv_stored, TILES, RING)

                @block.vector
                def _(dve):
                    dve.wait_ge(totals, 1)
                    dve.tensor_scalar(mean[:, :], bank[2][:, :], 1.0 / N, None, ALU.mult).then_inc(affine, 1)
                    dve.tensor_scalar(var[:, :], bank[3][:, :], 1.0 / N, EPS, ALU.mult, ALU.add).then_inc(affine, 1)
                    dve.wait_ge(affine, 2)
                    dve.tensor_tensor(tmp[:, :], mean[:, :], mean[:, :], ALU.mult).then_inc(affine, 1)
                    dve.wait_ge(affine, 3)
                    dve.tensor_tensor(var[:, :], var[:, :], tmp[:, :], ALU.subtract).then_inc(affine, 1)
                    dve.wait_ge(root, 1)
                    dve.reciprocal(tmp[:, :], var[:, :]).then_inc(affine, 1)
                    dve.wait_ge(affine, 5)
                    dve.wait_ge(consts, 64)
                    dve.tensor_tensor(norm2_mul[:, :], tmp[:, :], gain[:, :], ALU.mult).then_inc(affine, 1)
                    dve.wait_ge(affine, 6)
                    dve.tensor_tensor(tmp[:, :], mean[:, :], norm2_mul[:, :], ALU.mult).then_inc(affine, 1)
                    dve.wait_ge(affine, 7)
                    dve.tensor_tensor(norm2_add[:, :], shift[:, :], tmp[:, :], ALU.subtract).then_inc(affine, 1)

                    def residual(s):
                        r = rows(s)
                        zt, mt = at(z, s), at(mv, s)
                        wait_landed(dve, y_loaded, s)
                        dve.tensor_tensor(at(ym, s)[0:r, :], at(yb, s)[0:r, :], norm2_mul[0:r, :], ALU.mult).then_inc(y_scaled, 1)
                        wait_before(dve, x1_ready, s, 2)
                        dve.wait_ge(x_shifted, s.n + 1)
                        dve.wait_ge(y_scaled, s.n + 1)
                        dve.tensor_tensor(zt[0:r, :], at(ym, s)[0:r, :], at(xc, s)[0:r, :], ALU.add).then_inc(z_ready, 1)
                        dve.wait_ge(z_ready, s.n + 1)
                        dve.bn_stats(at(stat, s)[0:r, :], zt[0:r, :]).then_inc(stat_ready, 1)
                        wait_alone(dve, stat_ready, s.n + 1, passed)
                        dve.bn_aggr(mt[0:r, :], at(stat, s)[0:r, :]).then_inc(mv_ready, 1)
                        dve.wait_ge(mv_ready, s.n + 1)
                        dve.tensor_scalar(at(veps, s)[0:r, :], mt[0:r, 1:2], EPS, None, ALU.add).then_inc(veps_ready, 1)

                    def scaled_mean(s):
                        r = rows(s)
                        dve.wait_ge(rstd_ready, s.n + 1)
                        dve.scalar_tensor_tensor(at(nmr, s)[0:r, :], at(mv, s)[0:r, 0:1], -1.0, at(rstd, s)[0:r, :], ALU.mult, ALU.mult).then_inc(nmr_ready, 1)

                    def take_lo(s):
                        r = rows(s)
                        dve.wait_ge(hi_ready, s.n + 1)
                        dve.tensor_tensor(blocks_of(at(lo, s), r), blocks_of(at(tpose, s), r), blocks_of(at(hi, s), r).bitcast(F32), ALU.subtract).then_inc(lo_ready, 1)

                    def bias_to_q(s):
                        r = rows(s)
                        wait_landed_before(dve, q_stored, s)
                        dve.wait_ge(q_made, s.n + 1)
                        dve.tensor_tensor(at(qo, s)[0:r, :], at(pq, s)[0:r, :], bias_q[0:r, :], ALU.add).then_inc(q_ready, 1)

                    def bias_to_kv(s):
                        r = rows(s)
                        wait_landed_before(dve, kv_stored, s)
                        dve.wait_ge(k_made, s.n + 1)
                        dve.tensor_tensor(at(kvo, s)[0:r, 0:D], at(pk, s)[0:r, :], bias_kv[0:r, 0:D], ALU.add)
                        dve.wait_ge(v_made, s.n + 1)
                        dve.tensor_tensor(at(kvo, s)[0:r, D:2 * D], at(pv, s)[0:r, :], bias_kv[0:r, D:2 * D], ALU.add).then_inc(kv_ready, 1)

                    for n in range(2):
                        residual(Step(RING, 0, n))
                        scaled_mean(Step(RING, 0, n))
                    take_lo(Step(RING, 0, 0))

                    def turn(s):
                        if s.ahead(1).within(TILES):
                            take_lo(s.ahead(1))
                        if s.ahead(2).within(TILES):
                            residual(s.ahead(2))
                        bias_to_q(s)
                        if s.ahead(2).within(TILES):
                            scaled_mean(s.ahead(2))
                        bias_to_kv(s)
                    steps(dve, TILES, RING, turn, peel_last=3)

        next_stage()
        with ExitStack() as ctx:
            sb = tensors(ctx, "attend")
            RING, AHEAD = 6, 4
            window = [sb(f"window{i}", [P, P]) for i in range(RING)]
            same = [sb(f"same{i}", [P, P]) for i in range(RING)]
            apart = [sb(f"apart{i}", [HEADS, P + 1]) for i in range(RING)]
            idx = [sb(f"idx{i}", [P, 4], I32) for i in range(RING)]
            qe = [sb(f"qe{i}", [P, D]) for i in range(RING)]
            kve = [sb(f"kve{i}", [P, 2 * D]) for i in range(RING)]
            qk = [sb(f"qk{i}", [P, D]) for i in range(2)]
            score = [sb(f"score{i}", [P, HEADS]) for i in range(RING)]
            scoreT = [sb(f"scoreT{i}", [HEADS, P]) for i in range(RING)]
            upto = [sb(f"upto{i}", [HEADS, P]) for i in range(2)]
            peakT = [sb(f"peakT{i}", [HEADS, P]) for i in range(2)]
            below = [sb(f"below{i}", [HEADS, P]) for i in range(RING)]
            probT = [sb(f"probT{i}", [HEADS, P]) for i in range(RING)]
            weight = [sb(f"weight{i}", [P, HEADS]) for i in range(RING)]
            prob = [sb(f"prob{i}", [P, HEADS]) for i in range(RING)]
            pv_e = [sb(f"pv_e{i}", [P, D]) for i in range(3)]
            inv = [sb(f"inv{i}", [P, HEADS]) for i in range(RING)]
            orow = [sb(f"orow{i}", [P, D]) for i in range(RING)]
            window_loaded, apart_loaded = sems("window_loaded", RING), sems("apart_loaded", RING)
            q_got, kv_got, scattered = sems("q_got", RING), sems("kv_got", RING), sems("scattered", RING)
            (cleared, indexed, passed, pe_passed, same_ready, qk_ready, score_ready, score_turned, scoreT_ready, upto_ready, peak_ready,
             below_ready, probT_ready, prob_turned, pv_ready, summed, inverted, o_ready, carried, score_carried) = (sem(n) for n in (
                 "cleared", "indexed", "passed", "pe_passed", "same_ready", "qk_ready", "score_ready", "score_turned", "scoreT_ready", "upto_ready", "peak_ready",
                 "below_ready", "probT_ready", "prob_turned", "pv_ready", "summed", "inverted", "o_ready", "carried", "score_carried"))
            sums = [bank[0], bank[1], bank[2]]
            dens = [bank[3][:, 0:HEADS], bank[4][:, 0:HEADS], bank[5][:, 0:HEADS]]
            scoreT_ps = bank[6][0:HEADS, 0:P]
            prob_ps = bank[7][:, 0:HEADS]
            SCALE = float(1.0 / np.sqrt(np.float32(DH)))

            def heads(t):
                return t.rearrange("p (h c) -> p h c", h=HEADS)

            def per_head(t):
                return t.rearrange("p (h c) -> p h c", c=1).to_broadcast([P, HEADS, DH])

            with nc.Block() as block:
                @block.sync
                def _(sp):
                    def load(s):
                        wait_before(sp, same_ready, s, RING)
                        sp.dma_start(window[s.slot][:, :], window_on_all(dst_f, s)).then_inc(window_loaded[s.slot], 16)
                        wait_before(sp, peak_ready, s, RING)
                        sp.dma_start(apart[s.slot][:, :], apart_dram[bass.ds(s.n, 1), :].to_broadcast([HEADS, P + 1])).then_inc(apart_loaded[s.slot], 16)
                    steps(sp, CHUNKS, RING, load)

                @block.gpsimd
                def _(pool):
                    limit = pool.to_reg(N - 1)

                    def gather(s):
                        u = s.slot
                        wait_landed_before(pool, scattered, s)
                        pool.tensor_copy(idx[u][:, :], edge_index[:, bass.ds(s.n, 1), :].rearrange("p a b -> p (a b)")).then_inc(indexed, 1)
                        wait_before(pool, summed, s, RING)
                        wait_alone(pool, indexed, s.n + 1, passed)
                        pool.indirect_dma_start(out=qe[u][:, :], out_offset=None, in_=q_dram[0:N, :],
                                                in_offset=bass.IndirectOffsetOnAxis(ap=idx[u][:, 1:2], axis=0),
                                                bounds_check=limit, oob_is_err=False).then_inc(q_got[u], 16)
                        pool.indirect_dma_start(out=kve[u][:, :], out_offset=None, in_=kv_dram[0:N, :],
                                                in_offset=bass.IndirectOffsetOnAxis(ap=idx[u][:, 0:1], axis=0),
                                                bounds_check=limit, oob_is_err=False).then_inc(kv_got[u], 16)

                    def scatter(s):
                        u = s.slot
                        if s.reaches(1):
                            wait_landed(pool, scattered, s.before())
                        wait_alone(pool, o_ready, s.n + 1, passed)
                        pool.indirect_dma_start(out=attended, out_offset=bass.IndirectOffsetOnAxis(ap=idx[u][:, 2:3], axis=0),
                                                in_=orow[u][:, :], in_offset=None,
                                                bounds_check=limit, oob_is_err=False).then_inc(scattered[u], 16)

                    for i in range(RING):
                        pool.memset(qe[i][:, :], 0.0).then_inc(cleared, 1)
                        pool.memset(kve[i][:, :], 0.0).then_inc(cleared, 1)
                        pool.memset(weight[i][:, :], 1.0).then_inc(cleared, 1)
                    pool.wait_ge(cleared, 3 * RING)
                    for n in range(AHEAD):
                        gather(Step(RING, 0, n))

                    def turn(s):
                        if s.ahead(AHEAD).within(CHUNKS):
                            gather(s.ahead(AHEAD))
                        scatter(s)
                    steps(pool, CHUNKS, RING, turn, peel_last=AHEAD)
                    wait_all(pool, scattered, CHUNKS, RING)

                @block.vector
                def _(dve):
                    dve.memset(scoreT[0][:, 0:1], -FAR).then_inc(score_carried, 1)

                    def scores(s):
                        u = s.slot
                        wait_landed(dve, window_loaded, s)
                        wait_before(dve, summed, s, RING)
                        dve.tensor_scalar(same[u][:, :], window[u][:, ::-1], dst_col[:, bass.ds(s.n, 1)], None, ALU.is_equal).then_inc(same_ready, 1)
                        wait_landed(dve, q_got, s)
                        wait_landed(dve, kv_got, s)
                        dve.tensor_tensor(at(qk, s)[:, :], qe[u][:, :], kve[u][:, 0:D], ALU.mult).then_inc(qk_ready, 1)
                        wait_before(dve, score_turned, s, RING)
                        dve.wait_ge(qk_ready, s.n + 1)
                        dve.tensor_reduce(score[u][:, :], heads(at(qk, s)[:, :]), AX.X, ALU.add).then_inc(score_ready, 1)

                    def peaks(s):
                        u, to = s.slot, s.ahead(1)
                        ut, pt = at(upto, s), at(peakT, s)
                        dve.wait_ge(scoreT_ready, s.n + 1)
                        dve.wait_ge(score_carried, s.n + 1)
                        wait_landed(dve, apart_loaded, s)
                        dve.tensor_tensor_scan(ut[:, :], apart[u][:, 0:P], scoreT[u][:, :], -FAR, ALU.add, ALU.max).then_inc(upto_ready, 1)
                        dve.wait_ge(upto_ready, s.n + 1)
                        dve.tensor_tensor_scan(pt[:, ::-1], apart[u][:, 1:P + 1][:, ::-1], ut[:, ::-1], -FAR, ALU.add, ALU.max).then_inc(peak_ready, 1)
                        wait_before(dve, probT_ready, s, RING)
                        dve.wait_ge(peak_ready, s.n + 1)
                        dve.tensor_tensor(below[u][:, :], scoreT[u][:, :], pt[:, :], ALU.subtract).then_inc(below_ready, 1)
                        dve.tensor_copy(scoreT[to.slot][:, 0:1], pt[:, P - 1:P]).then_inc(score_carried, 1)

                    def values(s):
                        u = s.slot
                        wait_before(dve, summed, s, 3)
                        dve.wait_ge(prob_turned, s.n + 1)
                        if s.reaches(1):
                            dve.wait_ge(carried, s.n)
                        dve.tensor_tensor(prob[u][:, :], prob_ps, weight[u][:, :], ALU.mult)
                        dve.tensor_tensor(heads(at(pv_e, s)[:, :]), heads(kve[u][:, D:2 * D]), per_head(prob_ps), ALU.mult).then_inc(pv_ready, 1)

                    def normalize(s):
                        u = s.slot
                        if isinstance(s.n, int) and s.n == CHUNKS - 1:
                            dve.wait_ge(summed, s.n + 1)
                        else:
                            dve.wait_ge(carried, s.n + 1)
                        dve.reciprocal(inv[u][:, :], at(dens, s)).then_inc(inverted, 1)
                        wait_landed_before(dve, scattered, s)
                        dve.wait_ge(inverted, s.n + 1)
                        dve.tensor_tensor(heads(orow[u][:, :]), heads(at(sums, s)[:, :]), per_head(inv[u][:, :]), ALU.mult).then_inc(o_ready, 1)

                    dve.wait_ge(cleared, 3 * RING)
                    scores(Step(RING, 0, 0))
                    scores(Step(RING, 0, 1))
                    peaks(Step(RING, 0, 0))

                    def turn(s):
                        values(s)
                        if s.reaches(1):
                            normalize(s.before())
                        if s.ahead(1).within(CHUNKS):
                            peaks(s.ahead(1))
                        if s.ahead(2).within(CHUNKS):
                            scores(s.ahead(2))
                    steps(dve, CHUNKS, RING, turn, peel_last=3)
                    normalize(Step(RING, (CHUNKS - 1) // RING, (CHUNKS - 1) % RING))

                @block.tensor
                def _(pe):
                    def turn_scores(s):
                        wait_before(pe, scoreT_ready, s, 1)
                        pe.wait_ge(score_ready, s.n + 1)
                        pe.transpose(scoreT_ps, score[s.slot][:, :], identity[:, :]).then_inc(score_turned, 1)

                    def turn_weights(s):
                        wait_before(pe, pv_ready, s, 1)
                        wait_alone(pe, probT_ready, s.n + 1, pe_passed)
                        pe.transpose(prob_ps, probT[s.slot][:, :], identity[0:HEADS, 0:HEADS]).then_inc(prob_turned, 1)

                    def total(s):
                        u = s.slot
                        wait_before(pe, o_ready, s, 3)
                        pe.wait_ge(pv_ready, s.n + 1)
                        pe.matmul(at(dens, s), same[u][:, :], prob[u][:, :], start=True, stop=True)
                        pe.matmul(at(sums, s)[:, :], same[u][:, :], at(pv_e, s)[:, :], start=True, stop=True).then_inc(summed, 1)

                    turn_scores(Step(RING, 0, 0))
                    turn_scores(Step(RING, 0, 1))
                    turn_weights(Step(RING, 0, 0))

                    def turn(s):
                        total(s)
                        if s.ahead(1).within(CHUNKS):
                            turn_weights(s.ahead(1))
                        if s.ahead(2).within(CHUNKS):
                            turn_scores(s.ahead(2))
                    steps(pe, CHUNKS, RING, turn, peel_last=3)

                @block.scalar
                def _(act):
                    act.wait_ge(cleared, 3 * RING)

                    def copy_scores(s):
                        wait_before(act, below_ready, s, RING)
                        act.wait_ge(score_turned, s.n + 1)
                        act.activation(scoreT[s.slot][:, 1:P], scoreT_ps[:, 1:P], ACT.Copy).then_inc(scoreT_ready, 1)

                    def exponent(s):
                        wait_before(act, prob_turned, s, RING)
                        act.wait_ge(below_ready, s.n + 1)
                        act.activation(probT[s.slot][:, :], below[s.slot][:, :], ACT.Exp, scale=SCALE).then_inc(probT_ready, 1)

                    def carry(s):
                        to = s.ahead(1)
                        wait_landed(act, kv_got, to)
                        act.wait_ge(summed, s.n + 1)
                        act.activation(weight[to.slot][0:1, :], at(dens, s)[0:1, :], ACT.Copy)
                        act.activation(kve[to.slot][0:1, D:2 * D], at(sums, s)[0:1, :], ACT.Copy).then_inc(carried, 1)

                    copy_scores(Step(RING, 0, 0))
                    copy_scores(Step(RING, 0, 1))
                    exponent(Step(RING, 0, 0))

                    def turn(s):
                        if s.ahead(1).within(CHUNKS):
                            exponent(s.ahead(1))
                            carry(s)
                        if s.ahead(2).within(CHUNKS):
                            copy_scores(s.ahead(2))
                    steps(act, CHUNKS, RING, turn, peel_last=3)

        next_stage()
        with ExitStack() as ctx:
            sb = tensors(ctx, "out")
            RING = 4
            ob = [sb(f"ob{i}", [P, D]) for i in range(4)]
            xr = [sb(f"xr{i}", [P, D]) for i in range(4)]
            z = [sb(f"z{i}", [P, D]) for i in range(4)]
            res = [sb(f"res{i}", [P, D]) for i in range(4)]
            stat = [sb(f"stat{i}", [P, 6]) for i in range(4)]
            mv = [sb(f"mv{i}", [P, 2]) for i in range(4)]
            rstd = [sb(f"rstd{i}", [P, 1]) for i in range(4)]
            veps = [sb(f"veps{i}", [P, 1]) for i in range(4)]
            nmr = [sb(f"nmr{i}", [P, 1]) for i in range(4)]
            minus_half = sb("minus_half", [P, 1])
            hi = [sb(f"hi{i}", [P, D], F32R) for i in range(2)]
            lo = [sb(f"lo{i}", [P, D], F32R) for i in range(2)]
            bias_o = sb("bias_o", [P, D])
            o_loaded, x_loaded, stored, consts = sems("o_loaded", 4), sems("x_loaded", 4), sems("stored", 4), sem("consts")
            (half_ready, x_biased, turned, hi_ready, lo_ready, made, z_ready, stat_ready, mv_ready, veps_ready, rstd_ready, nmr_ready, res_ready, passed) = (
                sem(n) for n in ("half_ready", "x_biased", "turned", "hi_ready", "lo_ready", "made", "z_ready", "stat_ready", "mv_ready",
                                 "veps_ready", "rstd_ready", "nmr_ready", "res_ready", "passed"))
            tpose, acc = [bank[0], bank[1]], [bank[2], bank[3]]

            final = Step(RING, (TILES - 1) // RING, (TILES - 1) % RING)
            with nc.Block() as block:
                @block.sync
                def _(sp):
                    sp.dma_start(bias_o[:, :], row_on_all(bo)).then_inc(consts, 16)

                    def load(s):
                        r = rows(s)
                        wait_before(sp, turned, s, 4)
                        sp.dma_start(at(ob, s)[0:r, :], node_rows(attended, s)).then_inc(at(o_loaded, s), 16)
                        wait_before(sp, z_ready, s, 4)
                        sp.dma_start(at(xr, s)[0:r, :], node_rows(x1_dram, s)).then_inc(at(x_loaded, s), 16)
                    steps(sp, TILES, RING, load)

                @block.gpsimd
                def _(pool):
                    pool.memset(minus_half[:, :], -0.5).then_inc(half_ready, 1)
                    pool.wait_ge(half_ready, 1)
                    pool.wait_ge(consts, 16)

                    def add_bias(s):
                        r = rows(s)
                        wait_landed(pool, x_loaded, s)
                        pool.tensor_tensor(at(xr, s)[0:r, :], at(xr, s)[0:r, :], bias_o[0:r, :], ALU.add).then_inc(x_biased, 1)

                    def inverse_root(s):
                        r = rows(s)
                        wait_before(pool, nmr_ready, s, 4)
                        pool.wait_ge(veps_ready, s.n + 1)
                        pool.tensor_tensor(at(rstd, s)[0:r, :], at(veps, s)[0:r, :], minus_half[0:r, :], ALU.pow).then_inc(rstd_ready, 1)

                    add_bias(Step(RING, 0, 0))

                    def both(s):
                        if s.ahead(1).within(TILES):
                            add_bias(s.ahead(1))
                        inverse_root(s)
                    steps(pool, TILES, RING, both, peel_last=2)

                @block.tensor
                def _(pe):
                    def turn(s):
                        wait_landed(pe, o_loaded, s)
                        wait_before(pe, lo_ready, s, 2)
                        turn_tile(pe, at(tpose, s), at(ob, s), rows(s)).then_inc(turned, 1)

                    def multiply(s):
                        pe.wait_ge(lo_ready, s.n + 1)
                        wait_before(pe, z_ready, s, 2)
                        product(pe, at(acc, s), at(hi, s), at(lo, s), "o", rows(s)).then_inc(made, 1)

                    turn(Step(RING, 0, 0))

                    def both(s):
                        if s.ahead(1).within(TILES):
                            turn(s.ahead(1))
                        multiply(s)
                    steps(pe, TILES, RING, both, peel_last=2)

                @block.scalar
                def _(act):
                    def copy_hi(s):
                        r = rows(s)
                        wait_before(act, made, s, 2)
                        act.wait_ge(turned, s.n + 1)
                        act.activation(blocks_of(at(hi, s), r), blocks_of(at(tpose, s), r), ACT.Copy).then_inc(hi_ready, 1)

                    def finish(s):
                        r = rows(s)
                        wait_landed_before(act, stored, s)
                        act.wait_ge(rstd_ready, s.n + 1)
                        act.wait_ge(nmr_ready, s.n + 1)
                        act.activation(at(res, s)[0:r, :], at(z, s)[0:r, :], ACT.Identity, bias=at(nmr, s)[0:r, 0:1], scale=at(rstd, s)[0:r, 0:1]).then_inc(res_ready, 1)
                        act.wait_ge(res_ready, s.n + 1)
                        act.dma_start(node_rows(out, s), at(res, s)[0:r, :]).then_inc(at(stored, s), 16)

                    copy_hi(Step(RING, 0, 0))

                    def both(s):
                        if s.ahead(1).within(TILES):
                            copy_hi(s.ahead(1))
                        if s.reaches(1):
                            finish(s.before())
                    steps(act, TILES, RING, both, peel_last=2)
                    finish(final)
                    wait_all(act, stored, TILES, RING)

                @block.vector
                def _(dve):
                    def take_lo(s):
                        r = rows(s)
                        dve.wait_ge(hi_ready, s.n + 1)
                        dve.tensor_tensor(blocks_of(at(lo, s), r), blocks_of(at(tpose, s), r), blocks_of(at(hi, s), r).bitcast(F32), ALU.subtract).then_inc(lo_ready, 1)

                    def residual(s):
                        r = rows(s)
                        zt, mt = at(z, s), at(mv, s)
                        wait_before(dve, res_ready, s, 4)
                        dve.wait_ge(x_biased, s.n + 1)
                        dve.wait_ge(made, s.n + 1)
                        dve.tensor_tensor(zt[0:r, :], at(acc, s)[0:r, :], at(xr, s)[0:r, :], ALU.add).then_inc(z_ready, 1)
                        dve.wait_ge(z_ready, s.n + 1)
                        dve.bn_stats(at(stat, s)[0:r, :], zt[0:r, :]).then_inc(stat_ready, 1)
                        wait_alone(dve, stat_ready, s.n + 1, passed)
                        dve.bn_aggr(mt[0:r, :], at(stat, s)[0:r, :]).then_inc(mv_ready, 1)
                        dve.wait_ge(mv_ready, s.n + 1)
                        dve.tensor_scalar(at(veps, s)[0:r, :], mt[0:r, 1:2], EPS, None, ALU.add).then_inc(veps_ready, 1)

                    def scaled_mean(s):
                        r = rows(s)
                        dve.wait_ge(rstd_ready, s.n + 1)
                        dve.scalar_tensor_tensor(at(nmr, s)[0:r, :], at(mv, s)[0:r, 0:1], -1.0, at(rstd, s)[0:r, :], ALU.mult, ALU.mult).then_inc(nmr_ready, 1)

                    take_lo(Step(RING, 0, 0))

                    def turn(s):
                        if s.ahead(1).within(TILES):
                            take_lo(s.ahead(1))
                        if s.reaches(1):
                            scaled_mean(s.before())
                        residual(s)
                    steps(dve, TILES, RING, turn, peel_last=2)
                    scaled_mean(final)


def kernel(**inputs):
    import concourse.bacc as bacc
    from concourse.bass_utils import run_bass_kernel_spmd

    a = {k: np.asarray(v) for k, v in inputs.items()}
    wkv, bkv = a["L1_gnn_Wkv"], a["L1_gnn_bkv"]
    wkv = wkv.reshape(HEADS, 2, DH, D).transpose(1, 0, 2, 3).reshape(2 * D, D)
    bkv = bkv.reshape(HEADS, 2, DH).transpose(1, 0, 2).reshape(2 * D)
    arrays = {
        "x": a["x"], "src": a["src"], "dst": a["dst"],
        "g1": a["L0_gnn_norm1_g"], "b1": a["L0_gnn_norm1_b"], "g2": a["L0_gnn_norm2_g"], "b2": a["L0_gnn_norm2_b"],
        "w_conv": a["L0_gnn_W_conv"], "b_conv": a["L0_gnn_b_conv"],
        "fq": a["L0_gnn_Wq"], "fk": a["L0_gnn_Wk"], "fv": a["L0_gnn_Wv"], "fo": a["L0_gnn_Wo"],
        "projT": a["L0_gnn_proj"].T,
        "wqT": a["L1_gnn_Wq"].T, "bq": a["L1_gnn_bq"], "wkvT": wkv.T, "bkv": bkv,
        "woT": a["L1_gnn_Wo"].T, "bo": a["L1_gnn_bo"],
    }
    arrays = {f"in_{k}": np.ascontiguousarray(v) for k, v in arrays.items()}
    nc = bacc.Bacc("TRN2", target_bir_lowering=False, num_devices=1)
    args = [nc.dram_tensor(k, v.shape, mybir.dt.from_np(v.dtype), kind="ExternalInput").ap() for k, v in arrays.items()]
    out = nc.dram_tensor("out_dram", list(a["x"].shape), F32, kind="ExternalOutput").ap()
    gnn_program(nc, *args, out)
    r = run_bass_kernel_spmd(nc, [arrays], core_ids=[0])
    return r.results[0]["out_dram"]
```

```python
from contextlib import ExitStack

import numpy as np
import concourse.bass as bass
from concourse import mybir

F32 = mybir.dt.float32
F32R = mybir.dt.float32r
I32 = mybir.dt.int32
ACT = mybir.ActivationFunctionType
ALU = mybir.AluOpType
AX = mybir.AxisListType
RMAX = bass.bass_isa.ReduceOp.max

P = 128
D = 512
KC = D // P
HEADS = 8
DH = D // HEADS
NF = 256
EPS = 1e-5
KEPS = 1e-6
BIG = 20000.0
FAR = 1e30


class Step:

    def __init__(self, ring, j, slot, least=None):
        self.ring, self.j, self.slot, self.least = ring, j, slot, least
        self.n = j * ring + slot

    def ahead(self, k):
        least = None if self.least is None else self.least + k
        return Step(self.ring, self.j + (self.slot + k) // self.ring, (self.slot + k) % self.ring, least)

    def reaches(self, k):
        if self.least is None:
            return self.n >= k
        assert self.least >= k, "more first steps must be peeled"
        return True

    def before(self):
        return self.ahead(-1)

    def within(self, total):
        return not isinstance(self.n, int) or self.n < total


def steps(engine, total, ring, body, peel_last=1, peel_rings=1, between=None):
    between = between or {}
    rings = (total - peel_last) // ring

    def straight(first, end):
        for n in range(first, end):
            if n in between:
                between[n]()
            body(Step(ring, n // ring, n % ring))

    split = {n // ring for n in between}
    straight(0, ring * peel_rings)
    first = peel_rings
    while first < rings:
        end = first + 1
        if first in split:
            straight(ring * first, ring * end)
        else:
            while end < rings and end not in split:
                end += 1
            with engine.Fori(first, end) as j:
                for slot in range(ring):
                    body(Step(ring, j, slot, least=ring * first + slot))
        first = end
    straight(rings * ring, total)


def staged(total, step, parts):
    for part, lag in parts:
        near = step.ahead(lag)
        if step.reaches(-lag) and near.within(total):
            part(near)


def wait_alone(engine, semaphore, value, passed):
    engine.wait_ge(semaphore, value)
    engine.sem_inc(passed, 1)


def landed(step, semaphores):
    n = len(semaphores)
    return 16 * (step.j * (step.ring // n) + step.slot // n + 1)


def at(buffers, step):
    return buffers[step.slot % len(buffers)]


def wait_landed(engine, semaphores, step):
    engine.wait_ge(at(semaphores, step), landed(step, semaphores))


def wait_landed_before(engine, semaphores, step):
    if step.reaches(len(semaphores)):
        engine.wait_ge(at(semaphores, step), landed(step, semaphores) - 16)


def wait_all(engine, semaphores, total, ring):
    for n in range(total - len(semaphores), total):
        wait_landed(engine, semaphores, Step(ring, n // ring, n % ring))


def wait_before(engine, semaphore, step, distance):
    if step.reaches(distance):
        engine.wait_ge(semaphore, step.n - distance + 1)


def gnn_program(nc, x, src, dst, g1, b1, g2, b2, w_conv, b_conv, fq, fk, fv, fo, projT,
                wqT, bq, wkvT, bkv, woT, bo, out):
    N = x.shape[0]
    E = src.shape[0]
    TILES = -(-N // P)
    LAST_ROWS = N - (TILES - 1) * P
    EPC = P - 1
    CHUNKS = -(-E // EPC)
    PADDED = CHUNKS * EPC + 2
    NODES = TILES * P

    def rows(step):
        return LAST_ROWS if isinstance(step.n, int) and step.n == TILES - 1 else P

    y_dram = nc.dram_tensor("y_dram", [NODES, D], F32, kind="Internal").ap()
    xb_dram = nc.dram_tensor("xb_dram", [NODES, D], F32, kind="Internal").ap()
    q_dram = nc.dram_tensor("q_dram", [NODES, D], F32, kind="Internal").ap()
    apart_dram = nc.dram_tensor("apart_dram", [CHUNKS, P + 1], F32, kind="Internal").ap()
    same_dram = nc.dram_tensor("same_dram", [CHUNKS * P, P], F32, kind="Internal").ap()
    kv_dram = nc.dram_tensor("kv_dram", [NODES, 2 * D], F32, kind="Internal").ap()
    dst_f = nc.dram_tensor("dst_f", [1, PADDED], F32, kind="Internal").ap()
    src_f = nc.dram_tensor("src_f", [1, PADDED], F32, kind="Internal").ap()

    def node_rows(t, step):
        return t[bass.ds(step.n * P, rows(step)), :]

    def windows(t, shift):
        return bass.AP(tensor=t.tensor, offset=shift, ap=[[EPC, CHUNKS], [1, P]])

    def window_on_all(t, step):
        return t[0:1, bass.ds(step.n * EPC, P)].to_broadcast([P, P])

    def row_on_all(t):
        return t.rearrange("(a n) -> a n", a=1).to_broadcast([P, t.shape[0]])

    top = ExitStack()
    with top:
        def tensors(ctx, stage):
            def sb(name, shape, dt=F32):
                return ctx.enter_context(nc.sbuf_tensor(f"{stage}_{name}", shape, dt))
            return sb

        stage_sems = []

        def sem(name):
            stage_sems.append(nc.alloc_semaphore(f"{name}_{nc.next_id()}"))
            return stage_sems[-1]

        def sems(name, n):
            return [sem(f"{name}{i}") for i in range(n)]

        sb = tensors(top, "kept")
        bank = [top.enter_context(nc.psum_tensor(f"bank{i}", [P, D], F32)) for i in range(8)]

        identity = sb("identity", [P, P])
        ones = sb("ones", [P, P])
        split = {}
        for name in ("conv", "q", "k", "v", "o"):
            split[name] = (sb(f"w_{name}_hi", [P, KC, D], F32R), sb(f"w_{name}_lo", [P, KC, D], F32R))
        norm1_mul = sb("norm1_mul", [P, D])
        norm1_add = sb("norm1_add", [P, D])
        bias_conv = sb("bias_conv", [P, D])
        conv_shift = sb("conv_shift", [P, D])
        y_sq_sum = sb("y_sq_sum", [P, D])
        favor_out = sb("favor_out", [32, D])
        dst_col = sb("dst_col", [P, CHUNKS])
        edge_index = sb("edge_index", [P, CHUNKS, 4], I32)

        def next_stage():
            nc.clear_and_free_semaphores(stage_sems)
            nc.all_engine_barrier()
            stage_sems.clear()

        with ExitStack() as ctx:
            sb = tensors(ctx, "setup")
            stage = [sb(f"stage{i}", [P, KC, D]) for i in range(2)]
            e_int = [sb(f"e_int{i}", [100, E // 100], I32) for i in range(2)]
            e_flt = [sb(f"e_flt{i}", [100, E // 100]) for i in range(2)]
            pads = sb("pads", [1, P])
            win = [sb(f"win{i}", [CHUNKS, P]) for i in range(3)]
            win_back = [sb(f"win_back{i}", [CHUNKS, P]) for i in range(2)]
            apart = sb("apart", [CHUNKS, P + 1])
            cols = [sb(f"cols{i}", [P, CHUNKS]) for i in range(4)]
            not_last = sb("not_last", [P, CHUNKS])
            below = sb("below", [P, CHUNKS])
            back_f = sb("back_f", [P, CHUNKS])
            index_f = sb("index_f", [P, CHUNKS, 4])
            weights = [("q", wqT), ("k", wkvT[:, 0:D]), ("v", wkvT[:, D:2 * D]), ("o", woT)]
            weight_loaded, apart_ready, apart_stored = sems("weight_loaded", 2), sem("apart_ready"), sem("apart_stored")
            edges_loaded, padded, windowed = sem("edges_loaded"), sem("padded"), sem("windowed")
            ident_ready, pad_ready, reversed_ready = sem("ident_ready"), sem("pad_ready"), sem("reversed_ready")
            edges_float, hi_ready, lo_ready = sem("edges_float"), sem("hi_ready"), sem("lo_ready")
            win_turned, cols_ready, table_step = sem("win_turned"), sem("cols_ready"), sem("table_step")

            with nc.Block() as block:
                @block.sync
                def _(sp):
                    for i, t in enumerate((dst, src)):
                        sp.dma_start(e_int[i][:, :], t.rearrange("(a n) -> a n", a=100)).then_inc(edges_loaded, 16)
                    for n, (name, w) in enumerate(weights):
                        if n >= 2:
                            sp.wait_ge(lo_ready, n - 1)
                        sp.dma_start(stage[n % 2][:, :, :], w.rearrange("(k p) n -> p k n", p=P)).then_inc(weight_loaded[n % 2], 16)
                        if n == 1:
                            sp.wait_ge(edges_float, 2)
                            sp.wait_ge(pad_ready, 3)
                            for i, t in enumerate((dst_f, src_f)):
                                sp.dma_start(t[0:1, 1:E + 1].rearrange("a (p n) -> (a p) n", p=100), e_flt[i][:, :]).then_inc(padded, 16)
                                sp.dma_start(t[0:1, 0:1], pads[0:1, 0:1]).then_inc(padded, 16)
                                sp.dma_start(t[0:1, E + 1:PADDED], pads[0:1, 1:PADDED - E]).then_inc(padded, 16)
                            sp.wait_ge(padded, 96)
                            for i, (t, shift) in enumerate(((dst_f, 0), (dst_f, 1), (src_f, 0))):
                                sp.dma_start(win[i][:, :], windows(t, shift)).then_inc(windowed, 16)
                    sp.dma_start(bias_conv[:, :], row_on_all(b_conv)).then_inc(apart_stored, 16)
                    sp.wait_ge(apart_ready, 3)
                    sp.dma_start(apart_dram, apart[:, :]).then_inc(apart_stored, 16)
                    sp.wait_ge(apart_stored, 32)

                @block.gpsimd
                def _(pool):
                    pool.memset(ones[:, :], 1.0).then_inc(pad_ready, 1)
                    pool.memset(pads[:, :], -2.0).then_inc(pad_ready, 1)
                    pool.wait_ge(pad_ready, 2)
                    pool.memset(pads[0:1, 0:1], -1.0).then_inc(pad_ready, 1)
                    pool.memset(identity[:, :], 0.0).then_inc(ident_ready, 1)
                    pool.wait_ge(ident_ready, 1)
                    pool.affine_select(out=identity[:, :], in_=identity[:, :], compare_op=ALU.not_equal, fill=1.0,
                                       base=0, pattern=[[-1, P]], channel_multiplier=1).then_inc(ident_ready, 1)

                @block.scalar
                def _(act):
                    for n, (name, _) in enumerate(weights):
                        act.wait_ge(weight_loaded[n % 2], 16 * (n // 2 + 1))
                        act.activation(split[name][0][:, :, :], stage[n % 2][:, :, :], ACT.Copy).then_inc(hi_ready, 1)

                @block.vector
                def _(dve):
                    dve.wait_ge(edges_loaded, 32)
                    for i in range(2):
                        dve.tensor_copy(e_flt[i][:, :], e_int[i][:, :]).then_inc(edges_float, 1)

                    def split_weight(n):
                        hi, lo = split[weights[n][0]]
                        dve.wait_ge(hi_ready, n + 1)
                        dve.tensor_tensor(lo[:, :, :], stage[n % 2][:, :, :], hi[:, :, :].bitcast(F32), ALU.subtract).then_inc(lo_ready, 1)

                    split_weight(0)
                    split_weight(1)
                    dve.wait_ge(windowed, 48)
                    for i in range(2):
                        dve.tensor_copy(win_back[i][:, :], win[i][:, ::-1]).then_inc(reversed_ready, 1)
                    dve.memset(apart[:, 0:1], 0.0).then_inc(apart_ready, 1)
                    dve.tensor_tensor(apart[:, 1:P + 1], win[0][:, :], win[1][:, :], ALU.not_equal).then_inc(apart_ready, 1)
                    dve.wait_ge(apart_ready, 2)
                    dve.tensor_scalar(apart[:, 1:P + 1], apart[:, 1:P + 1], -FAR, None, ALU.mult).then_inc(apart_ready, 1)
                    dve.wait_ge(win_turned, 1)
                    for i in range(4):
                        dve.tensor_copy(cols[i][:, :], bank[i][:, 0:CHUNKS]).then_inc(cols_ready, 1)
                    dve.wait_ge(cols_ready, 4)
                    dcol, dback, dnext, scol = cols
                    dve.tensor_copy(dst_col[:, :], dcol[:, :]).then_inc(table_step, 1)
                    dve.tensor_tensor(not_last[:, :], dback[:, :], dnext[:, :], ALU.is_equal).then_inc(table_step, 1)
                    dve.tensor_scalar(below[:, :], dcol[:, :], 0.0, BIG, ALU.is_lt, ALU.mult).then_inc(table_step, 1)
                    dve.wait_ge(table_step, 3)
                    dve.tensor_tensor(index_f[:, :, 1], dcol[:, :], below[:, :], ALU.add).then_inc(table_step, 1)
                    dve.memset(index_f[:, :, 3], 0.0).then_inc(table_step, 1)
                    dve.wait_ge(table_step, 5)
                    dve.tensor_scalar(below[:, :], scol[:, :], 0.0, BIG, ALU.is_lt, ALU.mult).then_inc(table_step, 1)
                    dve.wait_ge(table_step, 6)
                    dve.tensor_tensor(index_f[:, :, 0], scol[:, :], below[:, :], ALU.add).then_inc(table_step, 1)
                    dve.wait_ge(table_step, 7)
                    dve.tensor_scalar(below[:, :], dback[:, :], 0.0, BIG, ALU.is_lt, ALU.mult).then_inc(table_step, 1)
                    dve.scalar_tensor_tensor(back_f[:, :], not_last[:, :], BIG, dback[:, :], ALU.mult, ALU.add).then_inc(table_step, 1)
                    dve.wait_ge(table_step, 9)
                    dve.tensor_tensor(index_f[:, :, 2], back_f[:, :], below[:, :], ALU.add).then_inc(table_step, 1)
                    dve.memset(index_f[0:1, :, 0:2], BIG).then_inc(table_step, 1)
                    dve.wait_ge(table_step, 11)
                    dve.tensor_copy(edge_index[:, :, :], index_f[:, :, :]).then_inc(table_step, 1)
                    for n in range(2, len(weights)):
                        split_weight(n)

                @block.tensor
                def _(pe):
                    pe.wait_ge(ident_ready, 2)
                    pe.wait_ge(windowed, 48)
                    pe.wait_ge(reversed_ready, 2)
                    turned = (win[0][:, :], win_back[0][:, :], win_back[1][:, :], win[2][:, :])
                    for i in range(4):
                        m = pe.transpose(bank[i][:, 0:CHUNKS], turned[i], identity[0:CHUNKS, 0:CHUNKS])
                    m.then_inc(win_turned, 1)

        square_total, x_total = bank[7], bank[3]
        fold = ExitStack()
        sb = tensors(fold, "fold")
        gain, shift = sb("gain", [P, D]), sb("shift", [P, D])
        w_raw, w_scaled = sb("w_raw", [P, KC, D]), sb("w_scaled", [P, KC, D])
        fw_alias = {"q": w_raw, "k": w_scaled}

        with ExitStack() as ctx:
            sb = tensors(ctx, "stats")
            RING = 6
            xs = [sb(f"xs{i}", [P, D]) for i in range(RING)]
            xsq = [sb(f"xsq{i}", [P, D]) for i in range(3)]
            y_first = [sb(f"y_first{i}", [P, D]) for i in range(3)]
            relu_row = sb("relu_row", [P, D])
            x_sum = sb("x_sum", [P, D])
            loaded, consts = sems("s_x_loaded", RING), sem("s_consts")
            summed, squared, sq_summed = sem("s_summed"), sem("s_squared"), sem("s_sq_summed")
            sum_cleared = sem("s_sum_cleared")
            rectified, filled, y_stored = sem("s_rectified"), sem("s_filled"), sems("s_y_stored", 3)

            R = 32
            h = sb("h", [R, D])
            hT = sb("hT", [P, KC, R])
            fw = {**fw_alias, **{n: sb(f"fw_{n}", [P, KC, D]) for n in "vo"}}
            pT = sb("pT", [P, NF])
            rowform = {n: sb(f"row_{n}", [R, D]) for n in "qk"}
            colform = {n: sb(f"col_{n}", [P, KC, R]) for n in "qk"}
            v_one = sb("v_one", [R, HEADS, DH + 1])
            sq = {n: sb(f"sq_{n}", [R, D]) for n in "qk"}
            diag = {n: sb(f"diag_{n}", [R, HEADS]) for n in "qk"}
            peak = {n: sb(f"peak_{n}", [R, HEADS]) for n in "qk"}
            peak_all = sb("peak_all", [R, HEADS])
            bias = {n: sb(f"bias_{n}", [R, HEADS]) for n in "qk"}
            feat = {n: sb(f"feat_{n}", [R, HEADS, NF]) for n in "qk"}
            featT = sb("featT", [P, 2 * HEADS, R])
            kv = sb("kv", [P, 2 * HEADS, DH + 1])
            den = sb("den", [R, HEADS])
            inv = sb("inv", [R, HEADS])
            av = sb("av", [R, D])
            avT = sb("avT", [P, KC, R])
            avD = sb("avD", [P, KC, R])
            f_h, f_pT, f_turned, f_hT, f_proj, f_colp = (sem(n) for n in ("f_h", "f_pT", "f_turned", "f_hT", "f_proj", "f_colp"))
            f_w = {n: sem(f"f_w_{n}") for n in "qkvo"}
            f_cols, f_rows, f_squares, f_diag, f_one = (sem(n) for n in ("f_cols", "f_rows", "f_squares", "f_diag", "f_one"))
            f_u = {n: sem(f"f_u_{n}") for n in "qk"}
            f_peak = {n: sem(f"f_peak_{n}") for n in "qk"}
            f_bias = {n: sem(f"f_bias_{n}") for n in "qk"}
            f_exp = {n: sem(f"f_exp_{n}") for n in "qk"}
            f_feat = {n: sem(f"f_feat_{n}") for n in "qk"}
            f_all, f_featT, f_kv, f_kvs, f_attn, f_den, f_inv = (sem(n) for n in ("f_all", "f_featT", "f_kv", "f_kvs", "f_attn", "f_den", "f_inv"))
            f_av, f_avT, f_avTs, f_avD, f_out, f_outs = (sem(n) for n in ("f_av", "f_avT", "f_avTs", "f_avD", "f_out", "f_outs"))
            conv_loaded = sem("conv_loaded")
            TEMPER = float(DH) ** -0.25

            def features(hd):
                return bank[2 * (hd % 2) + hd // 4][0:R, (hd // 2 % 2) * NF:(hd // 2 % 2 + 1) * NF]

            def by_head(t, heads):
                return t.rearrange("p (h d) -> p h d", h=heads)

            with nc.Block() as block:
                @block.sync
                def _(sp):
                    def load(s):
                        wait_before(sp, summed, s, RING)
                        wait_before(sp, squared, s, RING)
                        wait_before(sp, filled, s, RING)
                        sp.dma_start(xs[s.slot][0:rows(s), :], node_rows(x, s)).then_inc(loaded[s.slot], 16)

                    def store(s):
                        sp.wait_ge(filled, s.n + 1)
                        sp.dma_start(node_rows(y_dram, s), at(y_first, s)[0:rows(s), :]).then_inc(at(y_stored, s), 16)

                    def load_weight(n, w):
                        sp.dma_start(fw[n][:, :, :], w.rearrange("(k p) n -> p k n", p=P)).then_inc(f_w[n], 16)

                    for n in range(4):
                        load(Step(RING, 0, n))
                    for t, v in ((gain, g1), (shift, b1)):
                        sp.dma_start(t[:, :], row_on_all(v)).then_inc(consts, 16)
                    sp.dma_start(h[:, :], x[0:R, :]).then_inc(f_h, 16)
                    load_weight("q", fq)

                    def load_conv_weight():
                        sp.wait_ge(f_colp, 2)
                        sp.dma_start(w_raw[:, :, :], w_conv.rearrange("(k p) n -> p k n", p=P)).then_inc(conv_loaded, 16)

                    def load_random():
                        for half in range(2):
                            sp.dma_start(pT[half * DH:(half + 1) * DH, :], projT).then_inc(f_pT, 16)
                        load_weight("o", fo)
                    steps(sp, TILES, RING, lambda s: staged(TILES, s, ((load, 4), (store, 0))), peel_last=5, between={
                        4: lambda: load_weight("k", fk), 8: lambda: load_weight("v", fv), 18: load_random, 30: load_conv_weight})
                    sp.wait_ge(consts, 32)
                    sp.wait_ge(conv_loaded, 16)
                    wait_all(sp, y_stored, TILES, RING)

                @block.gpsimd
                def _(pool):
                    pool.memset(v_one[:, :, DH:DH + 1], 1.0).then_inc(f_one, 1)
                    pool.wait_ge(rectified, 1)

                    def fill(s):
                        wait_landed(pool, loaded, s)
                        wait_landed_before(pool, y_stored, s)
                        r = rows(s)
                        pool.tensor_tensor(at(y_first, s)[0:r, :], xs[s.slot][0:r, :], relu_row[0:r, :], ALU.add).then_inc(filled, 1)

                    def largest_of_all():
                        pool.wait_ge(f_peak["k"], 1)
                        pool.partition_all_reduce(peak_all[:, :], peak["k"][:, :], R, RMAX).then_inc(f_all, 1)
                    steps(pool, TILES, RING, fill, between={43: largest_of_all})

                @block.vector
                def _(dve):
                    dve.memset(x_sum[:, :], 0.0).then_inc(sum_cleared, 1)
                    dve.wait_ge(sum_cleared, 1)

                    def add(s):
                        r = rows(s)
                        dve.wait_ge(loaded[s.slot], landed(s, loaded))
                        if s.reaches(1):
                            dve.wait_ge(summed, s.n)
                        dve.tensor_tensor(x_sum[0:r, :], x_sum[0:r, :], xs[s.slot][0:r, :], ALU.add).then_inc(summed, 1)

                    def copy_hT():
                        dve.wait_ge(f_turned, 1)
                        dve.tensor_copy(hT[:, :, :], bank[0][:, 0:KC * R].rearrange("p (k r) -> p k r", k=KC)).then_inc(f_hT, 1)

                    def copy_rows():
                        dve.wait_ge(f_proj, 3)
                        for b, n in enumerate("qk"):
                            dve.tensor_scalar(rowform[n][:, :], bank[1 + b][0:R, :], TEMPER, None, ALU.mult).then_inc(f_rows, 1)
                        dve.tensor_copy(v_one[:, :, 0:DH], by_head(bank[3][0:R, :], HEADS)).then_inc(f_rows, 1)

                    def copy_columns():
                        dve.wait_ge(f_colp, 2)
                        for b, n in enumerate("qk"):
                            dve.tensor_scalar(colform[n][:, :, :], bank[4 + b][:, 0:KC * R].rearrange("p (k r) -> p k r", k=KC), TEMPER, None, ALU.mult).then_inc(f_cols, 1)

                    def square_norms():
                        for i, n in enumerate("qk"):
                            dve.wait_ge(f_rows, i + 1)
                            dve.tensor_tensor(sq[n][:, :], rowform[n][:, :], rowform[n][:, :], ALU.mult).then_inc(f_squares, 1)
                        for i, n in enumerate("qk"):
                            dve.wait_ge(f_squares, i + 1)
                            dve.tensor_reduce(diag[n][:, :], by_head(sq[n][:, :], HEADS), AX.X, ALU.add).then_inc(f_diag, 1)

                    def largest(n):
                        dve.wait_ge(f_u[n], 1)
                        for b in range(4):
                            first = 4 * (b % 2) + b // 2
                            m = dve.tensor_reduce(peak[n][:, first:first + 3:2], bank[b][0:R, :].rearrange("p (h m) -> p h m", h=2), AX.X, ALU.max)
                        m.then_inc(f_peak[n], 1)

                    def largest_q():
                        largest("q")
                        dve.wait_ge(f_diag, 2)
                        dve.wait_ge(f_peak["q"], 1)
                        dve.scalar_tensor_tensor(bias["q"][:, :], diag["q"][:, :], -0.5, peak["q"][:, :], ALU.mult, ALU.subtract).then_inc(f_bias["q"], 1)

                    def shift_feature(n):
                        dve.wait_ge(f_exp[n], 1)
                        for half in range(2):
                            fh = feat[n][:, half * 4:half * 4 + 4, :]
                            dve.tensor_scalar(fh, fh, float(1.0 / np.sqrt(NF)), KEPS, ALU.mult, ALU.add).then_inc(f_feat[n], 1)

                    def largest_k():
                        largest("k")

                    def bias_k():
                        dve.wait_ge(f_all, 1)
                        dve.scalar_tensor_tensor(bias["k"][:, :], diag["k"][:, :], -0.5, peak_all[:, :], ALU.mult, ALU.subtract).then_inc(f_bias["k"], 1)

                    def copy_kv():
                        dve.wait_ge(f_featT, 1)
                        dve.tensor_copy(featT[:, :, :], bank[4][:, :].rearrange("p (i r) -> p i r", r=R)).then_inc(f_kvs, 1)
                        dve.wait_ge(f_kv, 1)
                        for b in range(4):
                            dve.tensor_copy(kv[:, 4 * b:4 * b + 4, :], by_head(bank[b][:, 0:4 * (DH + 1)], 4)).then_inc(f_kvs, 1)

                    def divide():
                        dve.wait_ge(f_attn, 1)
                        for b in range(2):
                            m = dve.tensor_scalar(den[:, 4 * b:4 * b + 4], by_head(bank[5 + b][0:R, 0:4 * (DH + 1)], 4)[:, :, DH], KEPS, None, ALU.add)
                        m.then_inc(f_den, 1)
                        dve.wait_ge(f_den, 1)
                        dve.reciprocal(inv[:, :], den[:, :]).then_inc(f_inv, 1)
                        dve.wait_ge(f_inv, 1)
                        for b in range(2):
                            m = dve.tensor_tensor(by_head(av[:, b * 4 * DH:(b + 1) * 4 * DH], 4),
                                                  by_head(bank[5 + b][0:R, 0:4 * (DH + 1)], 4)[:, :, 0:DH],
                                                  inv[:, 4 * b:4 * b + 4].rearrange("p (i d) -> p i d", d=1).to_broadcast([R, 4, DH]), ALU.mult)
                        m.then_inc(f_av, 1)

                    def subtract_common():
                        dve.wait_ge(f_avT, 1)
                        dve.tensor_copy(avT[:, :, :], bank[4][:, 0:KC * R].rearrange("p (k r) -> p k r", k=KC)).then_inc(f_avTs, 1)
                        dve.wait_ge(f_avTs, 1)
                        for k in range(KC):
                            dve.tensor_scalar(avD[:, k, :], avT[:, k, :], avT[:, k, R - 1:R], None, ALU.subtract).then_inc(f_avD, 1)

                    steps(dve, TILES, RING, add, between={
                        7: copy_hT, 18: copy_rows, 20: square_norms, 27: copy_columns, 32: largest_q, 37: lambda: shift_feature("q"),
                        41: largest_k, 48: bias_k, 55: lambda: shift_feature("k"), 62: copy_kv, 68: divide, 74: subtract_common})
                    dve.wait_ge(f_out, 1)
                    dve.tensor_copy(favor_out[:, :], bank[0][0:R, :]).then_inc(f_outs, 1)
                @block.scalar
                def _(act):
                    act.activation(relu_row[:, :], bias_conv[:, :], ACT.Relu).then_inc(rectified, 1)

                    def square(s):
                        r = rows(s)
                        act.wait_ge(loaded[s.slot], landed(s, loaded))
                        wait_before(act, sq_summed, s, 3)
                        act.activation(at(xsq, s)[0:r, :], xs[s.slot][0:r, :], ACT.Square).then_inc(squared, 1)

                    def exponent(n):
                        act.wait_ge(f_bias[n], 1)
                        for hd in range(HEADS):
                            m = act.activation(feat[n][:, hd, :], features(hd), ACT.Exp, bias=bias[n][:, hd:hd + 1])
                        m.then_inc(f_exp[n], 1)
                    steps(act, TILES, RING, square, between={35: lambda: exponent("q"), 52: lambda: exponent("k")})
                @block.tensor
                def _(pe):
                    def total_squares(s):
                        r = rows(s)
                        pe.wait_ge(squared, s.n + 1)
                        first = isinstance(s.n, int) and s.n == 0
                        last = isinstance(s.n, int) and s.n == TILES - 1
                        pe.matmul(square_total[:, :], ones[0:r, :], at(xsq, s)[0:r, :], start=first, stop=last).then_inc(sq_summed, 1)

                    def turn_h():
                        pe.wait_ge(f_h, 16)
                        for k in range(KC):
                            m = pe.transpose(bank[0][:, k * R:(k + 1) * R], h[:, k * P:(k + 1) * P], identity[0:R, 0:R])
                        m.then_inc(f_turned, 1)

                    def project(b, n):
                        pe.wait_ge(f_hT, 1)
                        pe.wait_ge(f_w[n], 16)
                        for k in range(KC):
                            m = pe.matmul(bank[1 + b][0:R, :], hT[:, k, :], fw[n][:, k, :], start=k == 0, stop=k == KC - 1)
                        m.then_inc(f_proj, 1)

                    def project_columns(b, n):
                        for c in range(KC):
                            for k in range(KC):
                                m = pe.matmul(bank[4 + b][:, c * R:(c + 1) * R], fw[n][:, k, c * P:(c + 1) * P], hT[:, k, :], start=k == 0, stop=k == KC - 1)
                        m.then_inc(f_colp, 1)

                    def randomize(n, free, value):
                        pe.wait_ge(free, value)
                        pe.wait_ge(f_cols, 2)
                        pe.wait_ge(f_pT, 32)
                        for hd in range(HEADS):
                            o = (hd % 2) * DH
                            m = pe.matmul(features(hd), colform[n][o:o + DH, hd // 2, :], pT[o:o + DH, :], start=True, stop=True)
                        m.then_inc(f_u[n], 1)

                    def turn_features():
                        pe.wait_ge(f_feat["q"], 2)
                        pe.wait_ge(f_cols, 2)
                        for i in range(2 * HEADS):
                            m = pe.transpose(bank[4][:, i * R:(i + 1) * R], feat["q"][:, i // 2, i % 2 * P:(i % 2 + 1) * P], identity[0:R, 0:R])
                        m.then_inc(f_featT, 1)

                    def multiply_features():
                        pe.wait_ge(f_feat["k"], 2)
                        pe.wait_ge(f_one, 1)
                        pe.wait_ge(f_rows, 3)
                        for i in range(2 * HEADS):
                            m = pe.matmul(bank[i // 4][:, (i % 4) * (DH + 1):(i % 4 + 1) * (DH + 1)],
                                          feat["k"][:, i // 2, i % 2 * P:(i % 2 + 1) * P], v_one[:, i // 2, :], start=True, stop=True)
                        m.then_inc(f_kv, 1)

                    def attend_features():
                        pe.wait_ge(f_kvs, 5)
                        for hd in range(HEADS):
                            for half in range(2):
                                i = 2 * hd + half
                                m = pe.matmul(bank[5 + hd // 4][0:R, (hd % 4) * (DH + 1):(hd % 4 + 1) * (DH + 1)],
                                              featT[:, i, :], kv[:, i, :], start=half == 0, stop=half == 1)
                        m.then_inc(f_attn, 1)

                    def turn_attention():
                        pe.wait_ge(f_av, 1)
                        for k in range(KC):
                            m = pe.transpose(bank[4][:, k * R:(k + 1) * R], av[:, k * P:(k + 1) * P], identity[0:R, 0:R])
                        m.then_inc(f_avT, 1)

                    def project_out():
                        pe.wait_ge(f_avD, KC)
                        pe.wait_ge(f_w["o"], 16)
                        for k in range(KC):
                            m = pe.matmul(bank[0][0:R, :], avD[:, k, :], fw["o"][:, k, :], start=k == 0, stop=k == KC - 1)
                        m.then_inc(f_out, 1)

                    steps(pe, TILES, RING, total_squares, between={
                        5: turn_h, 9: lambda: project(0, "q"), 12: lambda: project(1, "k"), 15: lambda: project(2, "v"),
                        19: lambda: project_columns(0, "q"), 23: lambda: project_columns(1, "k"),
                        29: lambda: randomize("q", f_rows, 3), 38: lambda: randomize("k", f_exp["q"], 1),
                        44: turn_features, 58: multiply_features, 65: attend_features, 71: turn_attention, 77: project_out})
                    pe.wait_ge(summed, TILES)
                    pe.matmul(x_total[:, :], ones[:, :], x_sum[:, :], start=True, stop=True)

        def turn_tile(pe, psum, tile, r):
            for k in range(KC):
                m = pe.transpose(psum[:, k * P:k * P + r], tile[0:r, k * P:(k + 1) * P], identity[0:r, 0:r])
            return m

        def product(pe, psum, hi, lo, name, r):
            wh, wl = split[name]
            passes = [(hi, wh), (hi, wl), (lo, wh)]
            for i, (a, w) in enumerate(passes):
                for k in range(KC):
                    m = pe.matmul(psum[0:r, :], a[:, k * P:k * P + r], w[:, k, :],
                                  start=i == 0 and k == 0, stop=i == 2 and k == KC - 1)
            return m

        def blocks_of(t, r):
            return t[:, :].rearrange("p (k n) -> p k n", k=KC)[:, :, 0:r]

        next_stage()
        with ExitStack() as ctx:
            sb = tensors(ctx, "conv")
            RING, AHEAD = 6, 5
            LAG = 6
            window = [sb(f"window{i}", [P, P]) for i in range(RING)]
            same = [sb(f"same{i}", [P, P]) for i in range(RING)]
            same_first = [sb(f"same_first{i}", [P, P]) for i in range(3)]
            idx_in = [sb(f"idx_in{i}", [P, 4], I32) for i in range(RING)]
            idx_out = [sb(f"idx_out{i}", [P, 4], I32) for i in range(RING)]
            xg = [sb(f"xg{i}", [P, D]) for i in range(RING)]
            xr = [sb(f"xr{i}", [P, D]) for i in range(3)]
            count = [sb(f"count{i}", [P, 1]) for i in range(RING)]
            inv_count = [sb(f"inv_count{i}", [P, 1]) for i in range(RING)]
            total_T = [sb(f"total_T{i}", [P, D]) for i in range(3)]
            hi = [sb(f"hi{i}", [P, D], F32R) for i in range(3)]
            lo = [sb(f"lo{i}", [P, D], F32R) for i in range(3)]
            pre = [sb(f"pre{i}", [P, D]) for i in range(3)]
            y_row = [sb(f"y_row{i}", [P, D]) for i in range(3)]
            no_carry = sb("no_carry", [P, 1])
            mean, var, tmp = sb("mean", [P, D]), sb("var", [P, D]), sb("tmp", [P, D])
            mul_col = sb("mul_col", [P, KC])
            addT = sb("addT", [P, KC, P])
            affine, root = sem("affine"), sem("root")
            norm_turned, norm_cols, shifted, row_scaled, hi_folded, folded = (sem(n) for n in (
                "norm_turned", "norm_cols", "shifted", "row_scaled", "hi_folded", "folded"))
            window_loaded, gathered, scattered = sems("window_loaded", RING), sems("gathered", RING), sems("scattered", RING)
            same_stored = sems("same_stored", RING)
            in_indexed, out_indexed, xr_got = sems("in_indexed", RING), sems("out_indexed", RING), sems("xr_got", 3)
            hi_ready, lo_ready, made, biased, row_ready = (sem(n) for n in ("hi_ready", "lo_ready", "made", "biased", "row_ready"))
            cleared, rows_cleared, xr_cleared, same_ready, first_ready, passed = sem("cleared"), sem("rows_cleared"), sem("xr_cleared"), sem("same_ready"), sem("first_ready"), sem("passed")
            summed, counted, carried, inverted, combined = (sem(n) for n in ("summed", "counted", "carried", "inverted", "combined"))
            sums_T = [bank[0], bank[1]]
            counts = [bank[2][:, 0:1], bank[3][:, 0:1]]
            acc = [bank[6], bank[7]]

            def indices(s):
                return edge_index[:, bass.ds(s.n, 1), :].rearrange("p a b -> p (a b)")

            with nc.Block() as block:
                @block.sync
                def _(sp):
                    def load(s):
                        wait_landed_before(sp, gathered, s)
                        sp.dma_start(idx_in[s.slot][:, :], indices(s)).then_inc(in_indexed[s.slot], 16)
                        wait_before(sp, first_ready, s, RING)
                        sp.dma_start(window[s.slot][:, :], window_on_all(dst_f, s)).then_inc(window_loaded[s.slot], 16)

                    def load_out(s):
                        wait_landed_before(sp, scattered, s)
                        sp.dma_start(idx_out[s.slot][:, :], indices(s)).then_inc(out_indexed[s.slot], 16)

                    def store_same(s):
                        sp.wait_ge(same_ready, s.n + 1)
                        sp.dma_start(same_dram[bass.ds(s.n * P, P), :], same[s.slot][:, :]).then_inc(same_stored[s.slot], 16)
                    steps(sp, CHUNKS + LAG, RING, lambda s: staged(CHUNKS, s, ((load, 0), (load_out, -LAG), (store_same, -LAG))), peel_last=LAG, peel_rings=2)
                    wait_all(sp, same_stored, CHUNKS, RING)

                @block.gpsimd
                def _(pool):
                    limit = pool.to_reg(N - 1)

                    def gather(s):
                        wait_before(pool, summed, s, RING)
                        wait_alone(pool, in_indexed[s.slot], landed(s, in_indexed), passed)
                        pool.indirect_dma_start(out=xg[s.slot][:, :], out_offset=None, in_=x,
                                                in_offset=bass.IndirectOffsetOnAxis(ap=idx_in[s.slot][:, 0:1], axis=0),
                                                bounds_check=limit, oob_is_err=False).then_inc(gathered[s.slot], 16)

                    def gather_residual(s):
                        if s.reaches(3):
                            wait_alone(pool, row_ready, s.n - 2, passed)
                        wait_alone(pool, out_indexed[s.slot], landed(s, out_indexed), passed)
                        pool.indirect_dma_start(out=at(xr, s)[:, :], out_offset=None, in_=x,
                                                in_offset=bass.IndirectOffsetOnAxis(ap=idx_out[s.slot][:, 2:3], axis=0),
                                                bounds_check=limit, oob_is_err=False).then_inc(at(xr_got, s), 16)

                    def scatter(s):
                        if s.reaches(1):
                            wait_landed(pool, scattered, s.before())
                        wait_alone(pool, row_ready, s.n + 1, passed)
                        pool.indirect_dma_start(out=y_dram, out_offset=bass.IndirectOffsetOnAxis(ap=idx_out[s.slot][:, 2:3], axis=0),
                                                in_=at(y_row, s)[:, :], in_offset=None,
                                                bounds_check=limit, oob_is_err=False).then_inc(scattered[s.slot], 16)

                    for n in range(AHEAD):
                        pool.wait_ge(rows_cleared, n + 1)
                        gather(Step(RING, 0, n))
                    for i in range(3):
                        pool.memset(xr[i][:, :], 0.0).then_inc(xr_cleared, 1)
                    pool.wait_ge(xr_cleared, 3)
                    pool.wait_ge(rows_cleared, RING)
                    steps(pool, CHUNKS + LAG, RING, lambda s: staged(CHUNKS, s, (
                        (gather, AHEAD), (gather_residual, -2), (scatter, -4))), peel_last=LAG + AHEAD, peel_rings=2)
                    wait_all(pool, scattered, CHUNKS, RING)

                @block.vector
                def _(dve):
                    def compare(s):
                        u = s.slot
                        wait_landed(dve, window_loaded, s)
                        wait_before(dve, counted, s, RING)
                        wait_landed_before(dve, same_stored, s)
                        dve.tensor_scalar(same[u][:, :], window[u][:, ::-1], dst_col[:, bass.ds(s.n, 1)], None, ALU.is_equal).then_inc(same_ready, 1)
                        dve.tensor_scalar(at(same_first, s)[:, :], window[u][:, ::-1], window[u][:, 0:1], None, ALU.is_equal).then_inc(first_ready, 1)

                    def combine(s):
                        wait_before(dve, combined, s, 1)
                        wait_before(dve, lo_ready, s, 3)
                        dve.wait_ge(first_ready, s.n + 1)
                        dve.wait_ge(summed, s.n + 1)
                        for k in range(KC):
                            block_k = slice(k * P, (k + 1) * P)
                            last_sum = at(total_T, s.before())[:, k * P:k * P + 1] if s.reaches(1) else no_carry[:, :]
                            m = dve.scalar_tensor_tensor(at(total_T, s)[:, block_k], at(same_first, s)[:, :], last_sum, at(sums_T, s)[:, block_k], ALU.mult, ALU.add)
                        m.then_inc(combined, 1)

                    def invert(s):
                        if isinstance(s.n, int) and s.n == CHUNKS - 1:
                            dve.wait_ge(counted, s.n + 1)
                        else:
                            dve.wait_ge(carried, s.n + 1)
                        wait_before(dve, biased, s, RING)
                        dve.reciprocal(inv_count[s.slot][:, :], at(counts, s)).then_inc(inverted, 1)

                    def take_lo(s):
                        wait_before(dve, made, s, 3)
                        dve.wait_ge(hi_ready, s.n + 1)
                        dve.tensor_tensor(at(lo, s)[:, :], at(total_T, s)[:, :], at(hi, s)[:, :].bitcast(F32), ALU.subtract).then_inc(lo_ready, 1)

                    def scale_and_shift(s):
                        wait_before(dve, row_ready, s, 3)
                        dve.wait_ge(inverted, s.n + 1)
                        dve.wait_ge(made, s.n + 1)
                        dve.scalar_tensor_tensor(at(pre, s)[:, :], at(acc, s)[:, :], inv_count[s.slot][:, 0:1], conv_shift[:, :], ALU.mult, ALU.add).then_inc(biased, 1)

                    def rectify(s):
                        if s.reaches(3):
                            wait_landed(dve, scattered, s.ahead(-3))
                        wait_landed(dve, xr_got, s)
                        dve.wait_ge(biased, s.n + 1)
                        dve.scalar_tensor_tensor(at(y_row, s)[:, :], at(pre, s)[:, :], 0.0, at(xr, s)[:, :], ALU.max, ALU.add).then_inc(row_ready, 1)

                    for i in range(RING):
                        dve.memset(xg[i][0:1, :], 0.0).then_inc(rows_cleared, 1)
                    for i in range(RING):
                        dve.memset(count[i][:, :], 1.0).then_inc(cleared, 1)
                    dve.memset(no_carry[:, :], 0.0).then_inc(cleared, 1)
                    dve.wait_ge(cleared, RING + 1)
                    compare(Step(RING, 0, 0))
                    compare(Step(RING, 0, 1))
                    dve.tensor_scalar(mean[:, :], x_total[:, :], 1.0 / N, None, ALU.mult).then_inc(affine, 1)
                    dve.tensor_scalar(var[:, :], square_total[:, :], 1.0 / N, EPS, ALU.mult, ALU.add).then_inc(affine, 1)
                    dve.wait_ge(affine, 2)
                    dve.tensor_tensor(tmp[:, :], mean[:, :], mean[:, :], ALU.mult).then_inc(affine, 1)
                    dve.wait_ge(affine, 3)
                    dve.tensor_tensor(var[:, :], var[:, :], tmp[:, :], ALU.subtract).then_inc(affine, 1)
                    dve.wait_ge(root, 1)
                    dve.reciprocal(tmp[:, :], var[:, :]).then_inc(affine, 1)
                    dve.wait_ge(affine, 5)
                    dve.tensor_tensor(norm1_mul[:, :], tmp[:, :], gain[:, :], ALU.mult).then_inc(affine, 1)
                    dve.wait_ge(affine, 6)
                    dve.tensor_tensor(tmp[:, :], mean[:, :], norm1_mul[:, :], ALU.mult).then_inc(affine, 1)
                    dve.wait_ge(affine, 7)
                    dve.tensor_tensor(norm1_add[:, :], shift[:, :], tmp[:, :], ALU.subtract).then_inc(affine, 1)
                    w_hi, w_lo = split["conv"]
                    dve.wait_ge(norm_turned, 1)
                    dve.tensor_copy(mul_col[:, :], bank[4][:, 0:D:P]).then_inc(norm_cols, 1)
                    dve.wait_ge(norm_turned, 2)
                    dve.tensor_copy(addT[:, :, :], bank[5][:, :].rearrange("p (k n) -> p k n", k=KC)).then_inc(norm_cols, 1)
                    dve.wait_ge(norm_cols, 1)
                    for k in range(KC):
                        dve.tensor_scalar(w_scaled[:, k, :], w_raw[:, k, :], mul_col[:, k:k + 1], None, ALU.mult).then_inc(row_scaled, 1)
                    for k in range(KC):
                        dve.wait_ge(hi_folded, k + 1)
                        dve.tensor_tensor(w_lo[:, k, :], w_scaled[:, k, :], w_hi[:, k, :].bitcast(F32), ALU.subtract).then_inc(folded, 1)
                    dve.wait_ge(shifted, 1)
                    dve.tensor_tensor(conv_shift[:, :], bank[6][:, :], bias_conv[:, :], ALU.add).then_inc(folded, 1)
                    steps(dve, CHUNKS + LAG, RING, lambda s: staged(CHUNKS, s, (
                        (combine, 0), (scale_and_shift, -3), (compare, 2), (rectify, -3), (invert, 0), (take_lo, 0))), peel_last=LAG + 3, peel_rings=2)

                @block.tensor
                def _(pe):
                    for psum, t, ready in ((bank[4], norm1_mul, 6), (bank[5], norm1_add, 8)):
                        pe.wait_ge(affine, ready)
                        for k in range(KC):
                            m = pe.transpose(psum[:, k * P:(k + 1) * P], t[:, k * P:(k + 1) * P], identity[:, :])
                        m.then_inc(norm_turned, 1)
                    pe.wait_ge(norm_cols, 2)
                    for k in range(KC):
                        m = pe.matmul(bank[6][:, :], addT[:, k, :], w_raw[:, k, :], start=k == 0, stop=k == KC - 1)
                    m.then_inc(shifted, 1)
                    pe.wait_ge(cleared, RING + 1)

                    def total(s):
                        u = s.slot
                        pe.wait_ge(same_ready, s.n + 1)
                        wait_landed(pe, gathered, s)
                        wait_before(pe, combined, s, 2)
                        for k in range(KC):
                            m = pe.matmul(at(sums_T, s)[:, k * P:(k + 1) * P], xg[u][:, k * P:(k + 1) * P], same[u][:, :], start=True, stop=True)
                        m.then_inc(summed, 1)

                    def count_edges(s):
                        u = s.slot
                        wait_before(pe, inverted, s, 2)
                        if s.reaches(1):
                            pe.wait_ge(carried, s.n)
                        pe.matmul(at(counts, s), same[u][:, :], count[u][:, :], start=True, stop=True).then_inc(counted, 1)

                    def multiply(s):
                        wait_before(pe, biased, s, 2)
                        if isinstance(s.n, int) and s.n == 0:
                            pe.wait_ge(folded, KC + 1)
                        pe.wait_ge(lo_ready, s.n + 1)
                        product(pe, at(acc, s), at(hi, s), at(lo, s), "conv", P).then_inc(made, 1)

                    steps(pe, CHUNKS + LAG, RING, lambda s: staged(CHUNKS, s, (
                        (total, 0), (count_edges, 0), (multiply, -2))), peel_last=LAG + 3, peel_rings=2)

                @block.scalar
                def _(act):
                    act.wait_ge(affine, 4)
                    act.activation(var[:, :], var[:, :], ACT.Sqrt).then_inc(root, 1)
                    for k in range(KC):
                        act.wait_ge(row_scaled, k + 1)
                        act.activation(split["conv"][0][:, k, :], w_scaled[:, k, :], ACT.Copy).then_inc(hi_folded, 1)
                    act.wait_ge(cleared, RING + 1)

                    def carry_count(s):
                        if isinstance(s.n, int) and s.n == CHUNKS - 1:
                            return
                        act.wait_ge(counted, s.n + 1)
                        act.activation(count[s.ahead(1).slot][0:1, :], at(counts, s)[0:1, :], ACT.Copy).then_inc(carried, 1)

                    def copy_hi(s):
                        wait_before(act, made, s, 3)
                        act.wait_ge(combined, s.n + 1)
                        act.activation(at(hi, s)[:, :], at(total_T, s)[:, :], ACT.Copy).then_inc(hi_ready, 1)

                    steps(act, CHUNKS + LAG, RING, lambda s: staged(CHUNKS, s, ((carry_count, 0), (copy_hi, 0))), peel_last=LAG + 3, peel_rings=2)
        fold.close()

        next_stage()
        with ExitStack() as ctx:
            sb = tensors(ctx, "sums")
            RING = 6
            y = [sb(f"y{i}", [P, D]) for i in range(RING)]
            ysq = [sb(f"ysq{i}", [P, D]) for i in range(RING)]
            y_sum = [sb(f"y_sum{i}", [P, D]) for i in range(2)]
            y_loaded = sems("y_loaded", RING)
            cleared, sq_cleared, favored = sem("cleared"), sem("sq_cleared"), sem("favored")
            summed, squared, sq_pool, sq_pe = sem("summed"), sem("squared"), sem("sq_pool"), sem("sq_pe")

            def turns_of_half(s):
                return s.j * (RING // 2) + s.slot // 2 + 1

            with nc.Block() as block:
                @block.sync
                def _(sp):
                    def load(s):
                        r = rows(s)
                        wait_before(sp, summed, s, RING)
                        wait_before(sp, squared, s, RING)
                        sp.dma_start(at(y, s)[0:r, :], node_rows(y_dram, s)).then_inc(at(y_loaded, s), 16)
                    steps(sp, TILES, RING, load)

                @block.vector
                def _(dve):
                    for half in range(2):
                        dve.memset(y_sum[half][:, :], 0.0).then_inc(cleared, 1)
                    dve.wait_ge(cleared, 2)

                    def add(s):
                        r = rows(s)
                        wait_landed(dve, y_loaded, s)
                        if isinstance(s.n, int) and s.n == 0:
                            dve.tensor_tensor(y[0][0:32, :], y[0][0:32, :], favor_out[:, :], ALU.add).then_inc(favored, 1)
                            dve.wait_ge(favored, 1)
                        wait_before(dve, summed, s, 2)
                        total = at(y_sum, s)
                        dve.tensor_tensor(total[0:r, :], total[0:r, :], at(y, s)[0:r, :], ALU.add).then_inc(summed, 1)
                    steps(dve, TILES, RING, add)

                @block.scalar
                def _(act):
                    def square(s):
                        r = rows(s)
                        if s.reaches(RING):
                            act.wait_ge(sq_pe if s.slot % 2 == 0 else sq_pool, turns_of_half(s) - RING // 2)
                        wait_landed(act, y_loaded, s)
                        if isinstance(s.n, int) and s.n == 0:
                            act.wait_ge(favored, 1)
                        act.activation(at(ysq, s)[0:r, :], at(y, s)[0:r, :], ACT.Square).then_inc(squared, 1)
                    steps(act, TILES, RING, square)

                @block.gpsimd
                def _(pool):
                    pool.memset(y_sq_sum[:, :], 0.0).then_inc(sq_cleared, 1)
                    pool.wait_ge(sq_cleared, 1)

                    def add_odd(s):
                        if s.slot % 2 == 0:
                            return
                        r = rows(s)
                        if s.reaches(2):
                            pool.wait_ge(sq_pool, turns_of_half(s) - 1)
                        pool.wait_ge(squared, s.n + 1)
                        pool.tensor_tensor(y_sq_sum[0:r, :], y_sq_sum[0:r, :], at(ysq, s)[0:r, :], ALU.add).then_inc(sq_pool, 1)
                    steps(pool, TILES, RING, add_odd)

                @block.tensor
                def _(pe):
                    def add_even(s):
                        if s.slot % 2 == 1:
                            return
                        r = rows(s)
                        pe.wait_ge(squared, s.n + 1)
                        first = isinstance(s.n, int) and s.n == 0
                        pe.matmul(bank[3][:, :], ones[0:r, :], at(ysq, s)[0:r, :], start=first, stop=False).then_inc(sq_pe, 1)
                    steps(pe, TILES, RING, add_even)
                    pe.wait_ge(summed, TILES)
                    for half in range(2):
                        pe.matmul(bank[2][:, :], ones[:, :], y_sum[half][:, :], start=half == 0, stop=half == 1)
                    pe.wait_ge(sq_pool, TILES // 2)
                    pe.matmul(bank[3][:, :], ones[:, :], y_sq_sum[:, :], start=False, stop=True)

        next_stage()
        with ExitStack() as ctx:
            sb = tensors(ctx, "qkv")
            RING = 4
            LAG = 3
            yb = [sb(f"yb{i}", [P, D]) for i in range(4)]
            xc = [sb(f"xc{i}", [P, D]) for i in range(4)]
            ym = [sb(f"ym{i}", [P, D]) for i in range(2)]
            z = [sb(f"z{i}", [P, D]) for i in range(2)]
            x1 = [sb(f"x1_{i}", [P, D]) for i in range(4)]
            stat = [sb(f"stat{i}", [P, 6]) for i in range(2)]
            mv = [sb(f"mv{i}", [P, 2]) for i in range(2)]
            rstd = [sb(f"rstd{i}", [P, 1]) for i in range(2)]
            veps = [sb(f"veps{i}", [P, 1]) for i in range(2)]
            nmr = [sb(f"nmr{i}", [P, 1]) for i in range(2)]
            xb = [sb(f"xb{i}", [P, D]) for i in range(4)]
            lone = [sb(f"lone{i}", [P, D]) for i in range(2)]
            lone_stat = [sb(f"lone_stat{i}", [P, 6]) for i in range(2)]
            lone_mv = [sb(f"lone_mv{i}", [P, 2]) for i in range(4)]
            lone_veps = [sb(f"lone_veps{i}", [P, 1]) for i in range(4)]
            lone_rstd = [sb(f"lone_rstd{i}", [P, 1]) for i in range(4)]
            lone_nmr = [sb(f"lone_nmr{i}", [P, 1]) for i in range(4)]
            bias_o = sb("bias_o", [P, D])
            minus_half = sb("minus_half", [P, 1])
            hi = [sb(f"hi{i}", [P, D], F32R) for i in range(2)]
            lo = [sb(f"lo{i}", [P, D], F32R) for i in range(2)]
            qo = [sb(f"qo{i}", [P, D]) for i in range(2)]
            kvo = [sb(f"kvo{i}", [P, 2 * D]) for i in range(2)]
            bias_q, bias_kv = sb("bias_q", [P, D]), sb("bias_kv", [P, 2 * D])
            mean, var, tmp = sb("mean", [P, D]), sb("var", [P, D]), sb("tmp", [P, D])
            gain, shift = sb("gain", [P, D]), sb("shift", [P, D])
            norm2_mul, norm2_add = sb("norm2_mul", [P, D]), sb("norm2_add", [P, D])
            y_loaded, x_loaded, consts = sems("y_loaded", 4), sems("x_loaded", 4), sem("consts")
            biases = sem("biases")
            q_stored, kv_stored, xb_stored, lone_stored = sems("q_stored", 2), sems("kv_stored", 2), sems("xb_stored", 4), sems("lone_stored", 2)
            xb_ready, lone_stat_ready, lone_mv_ready, lone_veps_ready, lone_rstd_ready, lone_nmr_ready, lone_ready = (
                sem(n) for n in ("xb_ready", "lone_stat_ready", "lone_mv_ready", "lone_veps_ready", "lone_rstd_ready", "lone_nmr_ready", "lone_ready"))
            affine, root, x_shifted, y_scaled, z_ready = (sem(n) for n in ("affine", "root", "x_shifted", "y_scaled", "z_ready"))
            stat_ready, mv_ready, veps_ready, rstd_ready, nmr_ready, x1_ready = (sem(n) for n in ("stat_ready", "mv_ready", "veps_ready", "rstd_ready", "nmr_ready", "x1_ready"))
            turned, hi_ready, lo_ready, q_ready, kv_ready, half_ready, passed = (sem(n) for n in ("turned", "hi_ready", "lo_ready", "q_ready", "kv_ready", "half_ready", "passed"))
            favored = sem("favored")
            q_made, k_made, v_made = sem("q_made"), sem("k_made"), sem("v_made")
            tpose = [bank[0], bank[1]]
            pq, pk, pv = [bank[2], bank[3]], [bank[4], bank[5]], [bank[6], bank[7]]
            with nc.Block() as block:
                @block.sync
                def _(sp):
                    for t, v in ((gain, g2), (shift, b2)):
                        sp.dma_start(t[:, :], row_on_all(v)).then_inc(consts, 16)

                    def load(s):
                        r = rows(s)
                        wait_before(sp, y_scaled, s, 4)
                        sp.dma_start(at(yb, s)[0:r, :], node_rows(y_dram, s)).then_inc(at(y_loaded, s), 16)
                        wait_before(sp, z_ready, s, 4)
                        sp.dma_start(at(xc, s)[0:r, :], node_rows(x, s)).then_inc(at(x_loaded, s), 16)

                    def store_biased(s):
                        r = rows(s)
                        sp.wait_ge(xb_ready, s.n + 1)
                        sp.dma_start(node_rows(xb_dram, s), at(xb, s)[0:r, :]).then_inc(at(xb_stored, s), 16)

                    def store_lone(s):
                        r = rows(s)
                        sp.wait_ge(lone_ready, s.n + 1)
                        sp.dma_start(node_rows(out, s), at(lone, s)[0:r, :]).then_inc(at(lone_stored, s), 16)

                    for n in range(2):
                        load(Step(RING, 0, n))
                    for t, v in ((bias_q, bq), (bias_kv, bkv), (bias_o, bo)):
                        sp.dma_start(t[:, :], row_on_all(v)).then_inc(biases, 16)
                    for n in range(2, 4):
                        load(Step(RING, 0, n))
                    steps(sp, TILES + LAG, RING, lambda s: staged(TILES, s, ((load, 4), (store_biased, -1), (store_lone, -LAG))), peel_last=LAG + 5, peel_rings=2)
                    wait_all(sp, xb_stored, TILES, RING)
                    wait_all(sp, lone_stored, TILES, RING)

                @block.gpsimd
                def _(pool):
                    pool.memset(minus_half[:, :], -0.5).then_inc(half_ready, 1)
                    pool.wait_ge(half_ready, 1)
                    pool.wait_ge(affine, 8)
                    pool.wait_ge(biases, 48)

                    def shift_x(s):
                        r = rows(s)
                        wait_landed(pool, x_loaded, s)
                        if isinstance(s.n, int) and s.n == 0:
                            wait_landed(pool, y_loaded, s)
                            pool.tensor_tensor(at(yb, s)[0:32, :], at(yb, s)[0:32, :], favor_out[:, :], ALU.add).then_inc(favored, 1)
                        pool.tensor_tensor(at(xc, s)[0:r, :], at(xc, s)[0:r, :], norm2_add[0:r, :], ALU.add).then_inc(x_shifted, 1)

                    def inverse_root(s):
                        r = rows(s)
                        pool.wait_ge(veps_ready, s.n + 1)
                        pool.tensor_tensor(at(rstd, s)[0:r, :], at(veps, s)[0:r, :], minus_half[0:r, :], ALU.pow).then_inc(rstd_ready, 1)

                    first = [Step(RING, 0, n) for n in range(3)]
                    shift_x(first[0])
                    shift_x(first[1])
                    inverse_root(first[0])
                    inverse_root(first[1])
                    shift_x(first[2])

                    def bias_rows(s):
                        r = rows(s)
                        wait_landed_before(pool, xb_stored, s)
                        wait_before(pool, lone_ready, s, 4)
                        pool.wait_ge(x1_ready, s.n + 1)
                        pool.tensor_tensor(at(xb, s)[0:r, :], at(x1, s)[0:r, :], bias_o[0:r, :], ALU.add).then_inc(xb_ready, 1)

                    def lone_root(s):
                        r = rows(s)
                        pool.wait_ge(lone_veps_ready, s.n + 1)
                        pool.tensor_tensor(at(lone_rstd, s)[0:r, :], at(lone_veps, s)[0:r, :], minus_half[0:r, :], ALU.pow).then_inc(lone_rstd_ready, 1)

                    steps(pool, TILES + LAG, RING, lambda s: staged(TILES, s, ((shift_x, 3), (inverse_root, 2), (bias_rows, 0), (lone_root, -1))), peel_last=LAG + 4, peel_rings=2)

                @block.tensor
                def _(pe):
                    def turn(s):
                        pe.wait_ge(x1_ready, s.n + 1)
                        wait_before(pe, lo_ready, s, 2)
                        turn_tile(pe, at(tpose, s), at(x1, s), rows(s)).then_inc(turned, 1)

                    def multiply(s):
                        r = rows(s)
                        pe.wait_ge(lo_ready, s.n + 1)
                        wait_before(pe, kv_ready, s, 2)
                        product(pe, at(pq, s), at(hi, s), at(lo, s), "q", r).then_inc(q_made, 1)
                        product(pe, at(pk, s), at(hi, s), at(lo, s), "k", r).then_inc(k_made, 1)
                        product(pe, at(pv, s), at(hi, s), at(lo, s), "v", r).then_inc(v_made, 1)

                    pe.wait_ge(affine, 2)
                    turn(Step(RING, 0, 0))

                    def both(s):
                        if s.ahead(1).within(TILES):
                            turn(s.ahead(1))
                        multiply(s)
                    steps(pe, TILES, RING, both, peel_last=2, peel_rings=2)

                @block.scalar
                def _(act):
                    act.wait_ge(affine, 4)
                    act.activation(var[:, :], var[:, :], ACT.Sqrt).then_inc(root, 1)

                    def normalize(s):
                        r = rows(s)
                        wait_before(act, xb_ready, s, 4)
                        wait_before(act, turned, s, 4)
                        act.wait_ge(rstd_ready, s.n + 1)
                        act.wait_ge(nmr_ready, s.n + 1)
                        act.activation(at(x1, s)[0:r, :], at(z, s)[0:r, :], ACT.Identity, bias=at(nmr, s)[0:r, 0:1], scale=at(rstd, s)[0:r, 0:1]).then_inc(x1_ready, 1)

                    def copy_hi(s):
                        r = rows(s)
                        wait_before(act, v_made, s, 2)
                        act.wait_ge(turned, s.n + 1)
                        act.activation(blocks_of(at(hi, s), r), blocks_of(at(tpose, s), r), ACT.Copy).then_inc(hi_ready, 1)

                    def store(s):
                        r = rows(s)
                        act.wait_ge(q_ready, s.n + 1)
                        act.dma_start(node_rows(q_dram, s), at(qo, s)[0:r, :]).then_inc(at(q_stored, s), 16)
                        act.wait_ge(kv_ready, s.n + 1)
                        act.dma_start(node_rows(kv_dram, s), at(kvo, s)[0:r, :]).then_inc(at(kv_stored, s), 16)

                    normalize(Step(RING, 0, 0))
                    normalize(Step(RING, 0, 1))
                    copy_hi(Step(RING, 0, 0))

                    def normalize_lone(s):
                        r = rows(s)
                        wait_landed_before(act, lone_stored, s)
                        act.wait_ge(lone_rstd_ready, s.n + 1)
                        act.wait_ge(lone_nmr_ready, s.n + 1)
                        act.activation(at(lone, s)[0:r, :], at(xb, s)[0:r, :], ACT.Identity,
                                       bias=at(lone_nmr, s)[0:r, 0:1], scale=at(lone_rstd, s)[0:r, 0:1]).then_inc(lone_ready, 1)

                    steps(act, TILES + LAG, RING, lambda s: staged(TILES, s, ((copy_hi, 1), (normalize, 2), (normalize_lone, -2), (store, 0))), peel_last=LAG + 3, peel_rings=2)
                    wait_all(act, q_stored, TILES, RING)
                    wait_all(act, kv_stored, TILES, RING)

                @block.vector
                def _(dve):
                    dve.tensor_scalar(mean[:, :], bank[2][:, :], 1.0 / N, None, ALU.mult).then_inc(affine, 1)
                    dve.tensor_scalar(var[:, :], bank[3][:, :], 1.0 / N, EPS, ALU.mult, ALU.add).then_inc(affine, 1)
                    dve.wait_ge(affine, 2)
                    dve.tensor_tensor(tmp[:, :], mean[:, :], mean[:, :], ALU.mult).then_inc(affine, 1)
                    dve.wait_ge(affine, 3)
                    dve.tensor_tensor(var[:, :], var[:, :], tmp[:, :], ALU.subtract).then_inc(affine, 1)
                    dve.wait_ge(root, 1)
                    dve.reciprocal(tmp[:, :], var[:, :]).then_inc(affine, 1)
                    dve.wait_ge(affine, 5)
                    dve.wait_ge(consts, 32)
                    dve.tensor_tensor(norm2_mul[:, :], tmp[:, :], gain[:, :], ALU.mult).then_inc(affine, 1)
                    dve.wait_ge(affine, 6)
                    dve.tensor_tensor(tmp[:, :], mean[:, :], norm2_mul[:, :], ALU.mult).then_inc(affine, 1)
                    dve.wait_ge(affine, 7)
                    dve.tensor_tensor(norm2_add[:, :], shift[:, :], tmp[:, :], ALU.subtract).then_inc(affine, 1)

                    dve.wait_ge(biases, 48)

                    def residual(s):
                        r = rows(s)
                        zt, mt = at(z, s), at(mv, s)
                        wait_landed(dve, y_loaded, s)
                        if isinstance(s.n, int) and s.n == 0:
                            dve.wait_ge(favored, 1)
                        dve.tensor_tensor(at(ym, s)[0:r, :], at(yb, s)[0:r, :], norm2_mul[0:r, :], ALU.mult).then_inc(y_scaled, 1)
                        wait_before(dve, x1_ready, s, 2)
                        dve.wait_ge(x_shifted, s.n + 1)
                        dve.wait_ge(y_scaled, s.n + 1)
                        dve.tensor_tensor(zt[0:r, :], at(ym, s)[0:r, :], at(xc, s)[0:r, :], ALU.add).then_inc(z_ready, 1)
                        dve.wait_ge(z_ready, s.n + 1)
                        dve.bn_stats(at(stat, s)[0:r, :], zt[0:r, :]).then_inc(stat_ready, 1)
                        wait_alone(dve, stat_ready, s.n + 1, passed)
                        dve.bn_aggr(mt[0:r, :], at(stat, s)[0:r, :]).then_inc(mv_ready, 1)
                        dve.wait_ge(mv_ready, s.n + 1)
                        dve.tensor_scalar(at(veps, s)[0:r, :], mt[0:r, 1:2], EPS, None, ALU.add).then_inc(veps_ready, 1)

                    def scaled_mean(s):
                        r = rows(s)
                        dve.wait_ge(rstd_ready, s.n + 1)
                        dve.scalar_tensor_tensor(at(nmr, s)[0:r, :], at(mv, s)[0:r, 0:1], -1.0, at(rstd, s)[0:r, :], ALU.mult, ALU.mult).then_inc(nmr_ready, 1)

                    def take_lo(s):
                        r = rows(s)
                        dve.wait_ge(hi_ready, s.n + 1)
                        dve.tensor_tensor(blocks_of(at(lo, s), r), blocks_of(at(tpose, s), r), blocks_of(at(hi, s), r).bitcast(F32), ALU.subtract).then_inc(lo_ready, 1)

                    def bias_to_q(s):
                        r = rows(s)
                        wait_landed_before(dve, q_stored, s)
                        dve.wait_ge(q_made, s.n + 1)
                        dve.tensor_tensor(at(qo, s)[0:r, :], at(pq, s)[0:r, :], bias_q[0:r, :], ALU.add).then_inc(q_ready, 1)

                    def bias_to_kv(s):
                        r = rows(s)
                        wait_landed_before(dve, kv_stored, s)
                        dve.wait_ge(k_made, s.n + 1)
                        dve.tensor_tensor(at(kvo, s)[0:r, 0:D], at(pk, s)[0:r, :], bias_kv[0:r, 0:D], ALU.add)
                        dve.wait_ge(v_made, s.n + 1)
                        dve.tensor_tensor(at(kvo, s)[0:r, D:2 * D], at(pv, s)[0:r, :], bias_kv[0:r, D:2 * D], ALU.add).then_inc(kv_ready, 1)

                    for n in range(2):
                        residual(Step(RING, 0, n))
                        scaled_mean(Step(RING, 0, n))
                    take_lo(Step(RING, 0, 0))

                    def lone_stats(s):
                        r = rows(s)
                        dve.wait_ge(xb_ready, s.n + 1)
                        dve.bn_stats(at(lone_stat, s)[0:r, :], at(xb, s)[0:r, :]).then_inc(lone_stat_ready, 1)
                        wait_alone(dve, lone_stat_ready, s.n + 1, passed)
                        dve.bn_aggr(at(lone_mv, s)[0:r, :], at(lone_stat, s)[0:r, :]).then_inc(lone_mv_ready, 1)
                        dve.wait_ge(lone_mv_ready, s.n + 1)
                        dve.tensor_scalar(at(lone_veps, s)[0:r, :], at(lone_mv, s)[0:r, 1:2], EPS, None, ALU.add).then_inc(lone_veps_ready, 1)

                    def lone_mean(s):
                        r = rows(s)
                        wait_before(dve, lone_ready, s, 4)
                        dve.wait_ge(lone_rstd_ready, s.n + 1)
                        dve.scalar_tensor_tensor(at(lone_nmr, s)[0:r, :], at(lone_mv, s)[0:r, 0:1], -1.0, at(lone_rstd, s)[0:r, :], ALU.mult, ALU.mult).then_inc(lone_nmr_ready, 1)

                    steps(dve, TILES + LAG, RING, lambda s: staged(TILES, s, (
                        (take_lo, 1), (residual, 2), (bias_to_q, 0), (scaled_mean, 2), (lone_stats, -1), (lone_mean, -2), (bias_to_kv, 0))), peel_last=LAG + 3, peel_rings=2)

        next_stage()
        with ExitStack() as ctx:
            sb = tensors(ctx, "attend")
            RING, AHEAD = 6, 5
            LAG = 7
            same = [sb(f"same{i}", [P, P]) for i in range(RING)]
            apart = [sb(f"apart{i}", [HEADS, P + 1]) for i in range(RING)]
            idx_in = [sb(f"idx_in{i}", [P, 4], I32) for i in range(RING)]
            idx_res = [sb(f"idx_res{i}", [P, 4], I32) for i in range(RING)]
            idx_out = [sb(f"idx_out{i}", [P, 4], I32) for i in range(RING)]
            qe = [sb(f"qe{i}", [P, D]) for i in range(RING)]
            kve = [sb(f"kve{i}", [P, 2 * D]) for i in range(RING)]
            qk = [sb(f"qk{i}", [P, D]) for i in range(2)]
            score = [sb(f"score{i}", [P, HEADS]) for i in range(RING)]
            scoreT = [sb(f"scoreT{i}", [HEADS, P]) for i in range(RING)]
            upto = [sb(f"upto{i}", [HEADS, P]) for i in range(2)]
            peakT = [sb(f"peakT{i}", [HEADS, P]) for i in range(2)]
            below = [sb(f"below{i}", [HEADS, P]) for i in range(RING)]
            probT = [sb(f"probT{i}", [HEADS, P]) for i in range(RING)]
            weight = [sb(f"weight{i}", [P, HEADS]) for i in range(RING)]
            prob = [sb(f"prob{i}", [P, HEADS]) for i in range(RING)]
            pv_e = [sb(f"pv_e{i}", [P, D]) for i in range(3)]
            inv = [sb(f"inv{i}", [P, HEADS]) for i in range(RING)]
            den = [sb(f"den{i}", [P, HEADS]) for i in range(RING)]
            orow = [sb(f"orow{i}", [P, D]) for i in range(3)]
            hi = [sb(f"hi{i}", [P, D], F32R) for i in range(2)]
            lo = [sb(f"lo{i}", [P, D], F32R) for i in range(2)]
            xr = [sb(f"xr{i}", [P, D]) for i in range(3)]
            z = [sb(f"z{i}", [P, D]) for i in range(RING)]
            squares = sb("squares", [P, D])
            z_sum = [sb(f"z_sum{i}", [P, 1]) for i in range(RING)]
            nmean = [sb(f"nmean{i}", [P, 1]) for i in range(RING)]
            sq_sum = [sb(f"sq_sum{i}", [P, 1]) for i in range(RING)]
            rstd = [sb(f"rstd{i}", [P, 1]) for i in range(RING)]
            veps = [sb(f"veps{i}", [P, 1]) for i in range(RING)]
            nmr = [sb(f"nmr{i}", [P, 1]) for i in range(RING)]
            res = [sb(f"res{i}", [P, D]) for i in range(3)]
            minus_half = sb("minus_half", [P, 1])
            same_loaded, apart_loaded = sems("same_loaded", RING), sems("apart_loaded", RING)
            q_got, kv_got, scattered = sems("q_got", RING), sems("kv_got", RING), sems("scattered", RING)
            in_indexed, res_indexed, out_indexed, xr_got = sems("in_indexed", RING), sems("res_indexed", RING), sems("out_indexed", RING), sems("xr_got", 3)
            turned, hi_ready, lo_ready, made = (sem(n) for n in ("turned", "hi_ready", "lo_ready", "made"))
            z_ready, nmean_ready, squared, veps_ready, rstd_ready, nmr_ready, res_ready = (
                sem(n) for n in ("z_ready", "nmean_ready", "squared", "veps_ready", "rstd_ready", "nmr_ready", "res_ready"))
            (cleared, rows_cleared, passed, pe_passed, qk_ready, score_ready, score_turned, scoreT_ready, upto_ready, peak_ready,
             below_ready, probT_ready, prob_turned, pv_ready, summed, inverted, o_ready, carried, score_carried) = (sem(n) for n in (
                 "cleared", "rows_cleared", "passed", "pe_passed", "qk_ready", "score_ready", "score_turned", "scoreT_ready", "upto_ready", "peak_ready",
                 "below_ready", "probT_ready", "prob_turned", "pv_ready", "summed", "inverted", "o_ready", "carried", "score_carried"))
            sums, acc = [bank[0], bank[1]], [bank[2], bank[3]]
            tpose = bank[4]
            den_ps = bank[5][:, 0:HEADS]
            scoreT_ps = bank[6][0:HEADS, 0:P]
            prob_ps = bank[7][:, 0:HEADS]
            SCALE = float(1.0 / np.sqrt(np.float32(DH)))

            def heads(t):
                return t.rearrange("p (h c) -> p h c", h=HEADS)

            def per_head(t):
                return t.rearrange("p (h c) -> p h c", c=1).to_broadcast([P, HEADS, DH])

            def indices(s):
                return edge_index[:, bass.ds(s.n, 1), :].rearrange("p a b -> p (a b)")

            with nc.Block() as block:
                @block.sync
                def _(sp):
                    def load(s):
                        wait_landed_before(sp, q_got, s)
                        wait_landed_before(sp, kv_got, s)
                        sp.dma_start(idx_in[s.slot][:, :], indices(s)).then_inc(in_indexed[s.slot], 16)
                        wait_before(sp, peak_ready, s, RING)
                        sp.dma_start(apart[s.slot][:, :], apart_dram[bass.ds(s.n, 1), :].to_broadcast([HEADS, P + 1])).then_inc(apart_loaded[s.slot], 16)

                    def load_same(s):
                        wait_before(sp, summed, s, RING)
                        sp.dma_start(same[s.slot][:, :], same_dram[bass.ds(s.n * P, P), :]).then_inc(same_loaded[s.slot], 16)

                    def load_out(s):
                        wait_landed_before(sp, scattered, s)
                        sp.dma_start(idx_out[s.slot][:, :], indices(s)).then_inc(out_indexed[s.slot], 16)

                    def load_residual_index(s):
                        if s.reaches(RING):
                            wait_landed(sp, xr_got, s.ahead(-RING))
                        sp.dma_start(idx_res[s.slot][:, :], indices(s)).then_inc(res_indexed[s.slot], 16)
                    steps(sp, CHUNKS + 9, RING, lambda s: staged(CHUNKS, s, (
                        (load, 0), (load_same, -3), (load_residual_index, -4), (load_out, -9))), peel_last=9, peel_rings=3)

                @block.gpsimd
                def _(pool):
                    limit = pool.to_reg(N - 1)

                    def gather(s):
                        u = s.slot
                        wait_before(pool, summed, s, RING)
                        wait_alone(pool, in_indexed[u], landed(s, in_indexed), passed)
                        pool.indirect_dma_start(out=qe[u][:, :], out_offset=None, in_=q_dram[0:N, :],
                                                in_offset=bass.IndirectOffsetOnAxis(ap=idx_in[u][:, 1:2], axis=0),
                                                bounds_check=limit, oob_is_err=False).then_inc(q_got[u], 16)
                        pool.indirect_dma_start(out=kve[u][:, :], out_offset=None, in_=kv_dram[0:N, :],
                                                in_offset=bass.IndirectOffsetOnAxis(ap=idx_in[u][:, 0:1], axis=0),
                                                bounds_check=limit, oob_is_err=False).then_inc(kv_got[u], 16)

                    def gather_residual(s):
                        if s.reaches(3):
                            wait_alone(pool, z_ready, s.n - 2, passed)
                        wait_alone(pool, res_indexed[s.slot], landed(s, res_indexed), passed)
                        pool.indirect_dma_start(out=at(xr, s)[:, :], out_offset=None, in_=xb_dram[0:N, :],
                                                in_offset=bass.IndirectOffsetOnAxis(ap=idx_res[s.slot][:, 2:3], axis=0),
                                                bounds_check=limit, oob_is_err=False).then_inc(at(xr_got, s), 16)

                    def inverse_root(s):
                        wait_before(pool, res_ready, s, RING)
                        pool.wait_ge(veps_ready, s.n + 1)
                        pool.tensor_tensor(at(rstd, s)[:, :], at(veps, s)[:, :], minus_half[:, :], ALU.pow).then_inc(rstd_ready, 1)

                    def scatter(s):
                        wait_alone(pool, out_indexed[s.slot], landed(s, out_indexed), passed)
                        if s.reaches(1):
                            wait_landed(pool, scattered, s.before())
                        wait_alone(pool, res_ready, s.n + 1, passed)
                        pool.indirect_dma_start(out=out, out_offset=bass.IndirectOffsetOnAxis(ap=idx_out[s.slot][:, 2:3], axis=0),
                                                in_=at(res, s)[:, :], in_offset=None,
                                                bounds_check=limit, oob_is_err=False).then_inc(scattered[s.slot], 16)

                    for i in range(RING):
                        pool.memset(weight[i][:, :], 1.0).then_inc(cleared, 1)
                    for n in range(AHEAD):
                        pool.wait_ge(rows_cleared, 2 * (n + 1))
                        gather(Step(RING, 0, n))
                    for i in range(3):
                        pool.memset(xr[i][:, :], 0.0).then_inc(cleared, 1)
                    pool.memset(minus_half[:, :], -0.5).then_inc(cleared, 1)
                    pool.wait_ge(cleared, RING + 4)
                    pool.wait_ge(rows_cleared, 2 * RING)
                    steps(pool, CHUNKS + LAG, RING, lambda s: staged(CHUNKS, s, (
                        (gather, AHEAD), (inverse_root, -5), (gather_residual, -1), (scatter, -LAG))), peel_last=LAG + AHEAD, peel_rings=2)
                    wait_all(pool, scattered, CHUNKS, RING)

                @block.vector
                def _(dve):
                    for i in range(RING):
                        dve.memset(qe[i][0:1, :], 0.0).then_inc(rows_cleared, 1)
                        dve.memset(kve[i][0:1, :], 0.0).then_inc(rows_cleared, 1)
                    dve.memset(scoreT[0][:, 0:1], -FAR).then_inc(score_carried, 1)

                    def multiply_qk(s):
                        u = s.slot
                        wait_landed(dve, q_got, s)
                        wait_landed(dve, kv_got, s)
                        dve.tensor_tensor(at(qk, s)[:, :], qe[u][:, :], kve[u][:, 0:D], ALU.mult).then_inc(qk_ready, 1)

                    def add_qk(s):
                        u = s.slot
                        wait_before(dve, score_turned, s, RING)
                        dve.wait_ge(qk_ready, s.n + 1)
                        dve.tensor_reduce(score[u][:, :], heads(at(qk, s)[:, :]), AX.X, ALU.add).then_inc(score_ready, 1)

                    def peaks_upto(s):
                        u, ut = s.slot, at(upto, s)
                        dve.wait_ge(scoreT_ready, s.n + 1)
                        dve.wait_ge(score_carried, s.n + 1)
                        wait_landed(dve, apart_loaded, s)
                        dve.tensor_tensor_scan(ut[:, :], apart[u][:, 0:P], scoreT[u][:, :], -FAR, ALU.add, ALU.max).then_inc(upto_ready, 1)

                    def peaks(s):
                        u, ut, pt = s.slot, at(upto, s), at(peakT, s)
                        dve.wait_ge(upto_ready, s.n + 1)
                        dve.tensor_tensor_scan(pt[:, ::-1], apart[u][:, 1:P + 1][:, ::-1], ut[:, ::-1], -FAR, ALU.add, ALU.max).then_inc(peak_ready, 1)

                    def below_peak(s):
                        u, pt, to = s.slot, at(peakT, s), s.ahead(1)
                        wait_before(dve, probT_ready, s, RING)
                        dve.wait_ge(peak_ready, s.n + 1)
                        dve.tensor_tensor(below[u][:, :], scoreT[u][:, :], pt[:, :], ALU.subtract).then_inc(below_ready, 1)
                        dve.tensor_copy(scoreT[to.slot][:, 0:1], pt[:, P - 1:P]).then_inc(score_carried, 1)

                    def values(s):
                        u = s.slot
                        wait_before(dve, summed, s, 3)
                        dve.wait_ge(prob_turned, s.n + 1)
                        if s.reaches(1):
                            dve.wait_ge(carried, s.n)
                        dve.tensor_tensor(prob[u][:, :], prob_ps, weight[u][:, :], ALU.mult)
                        dve.tensor_tensor(heads(at(pv_e, s)[:, :]), heads(kve[u][:, D:2 * D]), per_head(prob_ps), ALU.mult).then_inc(pv_ready, 1)

                    def invert(s):
                        u = s.slot
                        dve.wait_ge(carried, s.n + 1)
                        dve.reciprocal(inv[u][:, :], den[u][:, :]).then_inc(inverted, 1)

                    def normalize(s):
                        u = s.slot
                        wait_before(dve, turned, s, 3)
                        dve.wait_ge(inverted, s.n + 1)
                        dve.tensor_tensor(heads(at(orow, s)[:, :]), heads(at(sums, s)[:, :]), per_head(inv[u][:, :]), ALU.mult).then_inc(o_ready, 1)

                    dve.wait_ge(cleared, RING)
                    def take_lo(s):
                        dve.wait_ge(hi_ready, s.n + 1)
                        dve.tensor_tensor(at(lo, s)[:, :], tpose[:, :], at(hi, s)[:, :].bitcast(F32), ALU.subtract).then_inc(lo_ready, 1)

                    for n in range(3):
                        for part in (multiply_qk, add_qk):
                            part(Step(RING, 0, n))
                    for n in range(2):
                        for part in (peaks_upto, peaks, below_peak):
                            part(Step(RING, 0, n))

                    def residual(s):
                        wait_before(dve, res_ready, s, RING)
                        wait_landed(dve, xr_got, s)
                        dve.wait_ge(made, s.n + 1)
                        dve.scalar_tensor_tensor(at(z, s)[:, :], at(acc, s)[:, :], 1.0, at(xr, s)[:, :], ALU.mult, ALU.add,
                                                 accum_out=at(z_sum, s)[:, :]).then_inc(z_ready, 1)

                    steps(dve, CHUNKS + LAG, RING, lambda s: staged(CHUNKS, s, (
                        (values, 0), (invert, -1), (residual, -3), (normalize, -1), (peaks_upto, 2), (multiply_qk, 3), (peaks, 2),
                        (add_qk, 3), (below_peak, 2), (take_lo, -1))), peel_last=LAG + 3, peel_rings=2)

                @block.tensor
                def _(pe):
                    def turn_scores(s):
                        wait_before(pe, scoreT_ready, s, 1)
                        pe.wait_ge(score_ready, s.n + 1)
                        pe.transpose(scoreT_ps, score[s.slot][:, :], identity[:, :]).then_inc(score_turned, 1)

                    def turn_weights(s):
                        wait_before(pe, pv_ready, s, 1)
                        wait_alone(pe, probT_ready, s.n + 1, pe_passed)
                        pe.transpose(prob_ps, probT[s.slot][:, :], identity[0:HEADS, 0:HEADS]).then_inc(prob_turned, 1)

                    def total(s):
                        u = s.slot
                        wait_before(pe, o_ready, s, 2)
                        wait_landed(pe, same_loaded, s)
                        pe.wait_ge(pv_ready, s.n + 1)
                        pe.matmul(den_ps, same[u][:, :], prob[u][:, :], start=True, stop=True)
                        pe.matmul(at(sums, s)[:, :], same[u][:, :], at(pv_e, s)[:, :], start=True, stop=True).then_inc(summed, 1)

                    def turn_rows(s):
                        wait_before(pe, lo_ready, s, 1)
                        pe.wait_ge(o_ready, s.n + 1)
                        turn_tile(pe, tpose, at(orow, s), P).then_inc(turned, 1)

                    def multiply(s):
                        wait_before(pe, z_ready, s, 2)
                        pe.wait_ge(lo_ready, s.n + 1)
                        product(pe, at(acc, s), at(hi, s), at(lo, s), "o", P).then_inc(made, 1)

                    for n in range(3):
                        turn_scores(Step(RING, 0, n))
                    turn_weights(Step(RING, 0, 0))

                    steps(pe, CHUNKS + LAG, RING, lambda s: staged(CHUNKS, s, (
                        (total, 0), (turn_weights, 1), (turn_rows, -1), (multiply, -2), (turn_scores, 3))), peel_last=LAG + 3, peel_rings=2)

                @block.scalar
                def _(act):
                    act.wait_ge(cleared, RING)

                    def copy_scores(s):
                        wait_before(act, below_ready, s, RING)
                        act.wait_ge(score_turned, s.n + 1)
                        act.activation(scoreT[s.slot][:, 1:P], scoreT_ps[:, 1:P], ACT.Copy).then_inc(scoreT_ready, 1)

                    def exponent(s):
                        wait_before(act, prob_turned, s, RING)
                        act.wait_ge(below_ready, s.n + 1)
                        act.activation(probT[s.slot][:, :], below[s.slot][:, :], ACT.Exp, scale=SCALE).then_inc(probT_ready, 1)

                    def carry(s):
                        to = s.ahead(1)
                        wait_before(act, inverted, s, RING)
                        act.wait_ge(summed, s.n + 1)
                        if isinstance(s.n, int) and s.n == CHUNKS - 1:
                            act.activation(den[s.slot][:, :], den_ps, ACT.Copy).then_inc(carried, 1)
                            return
                        act.activation(den[s.slot][:, :], den_ps, ACT.Copy)
                        act.activation(weight[to.slot][0:1, :], den_ps[0:1, :], ACT.Copy)
                        wait_landed(act, kv_got, to)
                        act.activation(kve[to.slot][0:1, D:2 * D], at(sums, s)[0:1, :], ACT.Copy).then_inc(carried, 1)

                    def copy_hi(s):
                        wait_before(act, made, s, 2)
                        act.wait_ge(turned, s.n + 1)
                        act.activation(at(hi, s)[:, :], tpose[:, :], ACT.Copy).then_inc(hi_ready, 1)

                    def variance(s):
                        act.wait_ge(z_ready, s.n + 1)
                        wait_before(act, nmr_ready, s, RING)
                        act.activation(at(nmean, s)[:, :], at(z_sum, s)[:, :], ACT.Copy, scale=-1.0 / D).then_inc(nmean_ready, 1)
                        act.wait_ge(nmean_ready, s.n + 1)
                        act.activation(squares[:, :], at(z, s)[:, :], ACT.Square, bias=at(nmean, s)[:, 0:1],
                                       accum_out=at(sq_sum, s)[:, :]).then_inc(squared, 1)
                        act.wait_ge(squared, s.n + 1)
                        act.activation(at(veps, s)[:, :], at(sq_sum, s)[:, :], ACT.Copy, scale=1.0 / D, bias=EPS).then_inc(veps_ready, 1)

                    def layer_norm(s):
                        if s.reaches(3):
                            wait_landed(act, scattered, s.ahead(-3))
                        act.wait_ge(rstd_ready, s.n + 1)
                        act.activation(at(nmr, s)[:, :], at(nmean, s)[:, :], ACT.Copy, scale=at(rstd, s)[:, 0:1]).then_inc(nmr_ready, 1)
                        act.wait_ge(nmr_ready, s.n + 1)
                        act.activation(at(res, s)[:, :], at(z, s)[:, :], ACT.Identity, bias=at(nmr, s)[:, 0:1], scale=at(rstd, s)[:, 0:1]).then_inc(res_ready, 1)

                    for n in range(3):
                        copy_scores(Step(RING, 0, n))
                    for n in range(2):
                        exponent(Step(RING, 0, n))

                    steps(act, CHUNKS + LAG, RING, lambda s: staged(CHUNKS, s, (
                        (carry, 0), (copy_hi, -1), (exponent, 2), (layer_norm, -6), (copy_scores, 3), (variance, -3))), peel_last=LAG + 3, peel_rings=2)


def kernel(**inputs):
    import concourse.bacc as bacc
    from concourse.bass_utils import run_bass_kernel_spmd

    a = {k: np.asarray(v) for k, v in inputs.items()}
    wkv, bkv = a["L1_gnn_Wkv"], a["L1_gnn_bkv"]
    wkv = wkv.reshape(HEADS, 2, DH, D).transpose(1, 0, 2, 3).reshape(2 * D, D)
    bkv = bkv.reshape(HEADS, 2, DH).transpose(1, 0, 2).reshape(2 * D)
    arrays = {
        "x": a["x"], "src": a["src"], "dst": a["dst"],
        "g1": a["L0_gnn_norm1_g"], "b1": a["L0_gnn_norm1_b"], "g2": a["L0_gnn_norm2_g"], "b2": a["L0_gnn_norm2_b"],
        "w_conv": a["L0_gnn_W_conv"], "b_conv": a["L0_gnn_b_conv"],
        "fq": a["L0_gnn_Wq"], "fk": a["L0_gnn_Wk"], "fv": a["L0_gnn_Wv"], "fo": a["L0_gnn_Wo"],
        "projT": a["L0_gnn_proj"].T,
        "wqT": a["L1_gnn_Wq"].T, "bq": a["L1_gnn_bq"], "wkvT": wkv.T, "bkv": bkv,
        "woT": a["L1_gnn_Wo"].T, "bo": a["L1_gnn_bo"],
    }
    arrays = {f"in_{k}": np.ascontiguousarray(v) for k, v in arrays.items()}
    nc = bacc.Bacc("TRN2", target_bir_lowering=False, num_devices=1)
    args = [nc.dram_tensor(k, v.shape, mybir.dt.from_np(v.dtype), kind="ExternalInput").ap() for k, v in arrays.items()]
    out = nc.dram_tensor("out_dram", list(a["x"].shape), F32, kind="ExternalOutput").ap()
    gnn_program(nc, *args, out)
    r = run_bass_kernel_spmd(nc, [arrays], core_ids=[0])
    return r.results[0]["out_dram"]
```
